# Optimizing a Trainium2 kernel written in Bass

```python
import numpy as np
import jax
import jax.numpy as jnp

def _softmax(x, axis=-1):
    return jax.nn.softmax(x, axis=axis)

def _gelu(x):
    return jax.nn.gelu(x, approximate=True)

def _silu(x):
    return jax.nn.silu(x)

def _sigmoid(x):
    return jax.nn.sigmoid(x)

def _layernorm(x, axis=-1, eps=1e-05):
    m = jnp.mean(x, axis=axis, keepdims=True)
    v = jnp.var(x, axis=axis, keepdims=True)
    return (x - m) / jnp.sqrt(v + eps)

def _scatter_add(tgt, idx, src, axis=0):
    return tgt.at[idx].add(src)

def _segment_sum(src, seg, n):
    return jax.ops.segment_sum(src, seg, n)
kernel_name = 'mk_perceiver_d1_seqx_r4_047d55'

def setup_inputs(seed: int=0):
    np.random.seed(seed)
    _w = jnp.asarray

    def _rec_inputs():
        import jax
        import jax.numpy as jnp
        _rk = jax.random.key(seed)
        x = -0.0003929 + 0.9999 * jax.random.normal(jax.random.fold_in(_rk, 1), (2, 64, 512), jnp.float32)
        _lenS = 64 - jax.random.randint(jax.random.fold_in(_rk, 7), (2,), 0, max(1, 64 // 4) + 1, jnp.int32)
        _lenS2 = 1024 - jax.random.randint(jax.random.fold_in(_rk, 8), (2,), 0, max(1, 1024 // 4) + 1, jnp.int32)
        _ctx_2048P = jax.random.normal(jax.random.fold_in(_rk, 11), (2, 16, 512), jnp.float32)
        _ctx_2048c = jax.random.dirichlet(jax.random.fold_in(_rk, 511), 0.3 * jnp.ones((16,), jnp.float32), (2, 1024))
        _ctx_2048t = jnp.einsum('bsk,bkd->bsd', _ctx_2048c, _ctx_2048P)
        _ctx_2048t = _ctx_2048t * jax.lax.rsqrt(jnp.mean(jnp.square(_ctx_2048t)) + 1e-12) * 0.953939
        ctx_2048 = -0.000514642 + 1.00011 * (_ctx_2048t + 0.3 * jax.random.normal(jax.random.fold_in(_rk, 611), (2, 1024, 512), jnp.float32))
        _validS = jnp.arange(64)[None, :] < _lenS[:, None]
        _validS2 = jnp.arange(1024)[None, :] < _lenS2[:, None]
        _causal = jnp.tril(jnp.ones((64, 64), dtype=bool))
        mask_BxSxS2_ff0 = jnp.where(jnp.ones((2, 64, 1024), dtype=bool), 0.0, -1000000000.0).astype(jnp.float32)
        return (x, ctx_2048, mask_BxSxS2_ff0)
    x, ctx_2048, mask_BxSxS2_ff0 = _rec_inputs()

    def _L0_xattn_setup():
        import jax, jax.numpy as jnp
        import numpy as np
        NUM_HEADS = 16
        EPS = 1e-08

        def _dyn_quant(x):
            s = jnp.maximum(jnp.max(jnp.abs(x), axis=-1, keepdims=True) / 127.0, EPS)
            q = jnp.clip(jnp.round(x / s), -127.0, 127.0)
            return (q, s)

        def _quant_weight(w):
            s = jnp.maximum(jnp.max(jnp.abs(w), axis=1, keepdims=True) / 127.0, EPS)
            q = jnp.clip(jnp.round(w / s), -127.0, 127.0)
            return (q, s)

        def _w8a8_linear(x, w, b):
            qx, sx = _dyn_quant(x)
            qw, sw = _quant_weight(w)
            y = jnp.einsum('bnc,oc->bno', qx, qw) * (sx * sw[:, 0])
            return y + b
        key = jax.random.key(seed)
        ks = jax.random.split(key, 9)
        B, N, L, C = (2, 1024, 128, 512)
        sc = 0.02
        return {'x': jax.random.normal(ks[0], (B, N, C), jnp.float32), 'cond': jax.random.normal(ks[1], (B, L, C), jnp.float32), 'mask': jnp.zeros((B, N, L), jnp.float32), 'wq': jax.random.normal(ks[2], (C, C), jnp.float32) * sc, 'bq': jnp.zeros((C,), jnp.float32), 'wk': jax.random.normal(ks[3], (C, C), jnp.float32) * sc, 'bk': jnp.zeros((C,), jnp.float32), 'wv': jax.random.normal(ks[4], (C, C), jnp.float32) * sc, 'bv': jnp.zeros((C,), jnp.float32), 'wo': jax.random.normal(ks[5], (C, C), jnp.float32) * sc, 'bo': jnp.zeros((C,), jnp.float32)}
    _L0_xattn_all = _L0_xattn_setup()
    _L0_xattn_in = {k: v for k, v in _L0_xattn_all.items() if k in ('wq', 'bq', 'wk', 'bk', 'wv', 'bv', 'wo', 'bo')}
    del _L0_xattn_all

    def _L0_attn_setup():
        import jax, jax.numpy as jnp
        import numpy as np
        B, S, D = (2, 512, 512)
        H, DH, DR = (16, 128, 64)
        DC_KV, DC_Q = (128, 384)
        ROPE_BASE = 10000.0

        def _rope(t):
            s, dr = (t.shape[1], t.shape[-1])
            inv_freq = 1.0 / ROPE_BASE ** (jnp.arange(0, dr, 2, dtype=jnp.float32) / dr)
            ang = jnp.arange(s, dtype=jnp.float32)[:, None] * inv_freq
            cos = jnp.tile(jnp.cos(ang), (1, 2))[None, :, None, :]
            sin = jnp.tile(jnp.sin(ang), (1, 2))[None, :, None, :]
            t1, t2 = jnp.split(t, 2, axis=-1)
            rot = jnp.concatenate([-t2, t1], axis=-1)
            return t * cos + rot * sin
        key = jax.random.key(seed)
        ks = jax.random.split(key, 18)
        g = lambda k, shp: jax.random.normal(k, shp, dtype=jnp.float32) * 0.02
        return {'x': jax.random.normal(ks[0], (B, S, D), dtype=jnp.float32), 'Wkd': g(ks[1], (DC_KV, D)), 'bkd': jnp.zeros((DC_KV,), jnp.float32), 'Wqd': g(ks[2], (DC_Q, D)), 'bqd': jnp.zeros((DC_Q,), jnp.float32), 'Wku': g(ks[3], (H * DH, DC_KV)), 'bku': jnp.zeros((H * DH,), jnp.float32), 'Wvu': g(ks[4], (H * DH, DC_KV)), 'bvu': jnp.zeros((H * DH,), jnp.float32), 'Wqu': g(ks[5], (H * DH, DC_Q)), 'bqu': jnp.zeros((H * DH,), jnp.float32), 'Wkr': g(ks[6], (H * DR, D)), 'bkr': jnp.zeros((H * DR,), jnp.float32), 'Wqr': g(ks[7], (H * DR, DC_Q)), 'bqr': jnp.zeros((H * DR,), jnp.float32), 'Wo': g(ks[8], (D, H * DH)), 'bo': jnp.zeros((D,), jnp.float32)}
    _L0_attn_all = _L0_attn_setup()
    _L0_attn_in = {k: v for k, v in _L0_attn_all.items() if k in ('Wkd', 'bkd', 'Wqd', 'bqd', 'Wku', 'bku', 'Wvu', 'bvu', 'Wqu', 'bqu', 'Wkr', 'bkr', 'Wqr', 'bqr', 'Wo', 'bo')}
    del _L0_attn_all

    def _L0_ffn_setup():
        import jax, jax.numpy as jnp
        import numpy as np
        TOP_K = 4
        key = jax.random.key(seed)
        ks = jax.random.split(key, 9)
        B, T, D, H, NE = (2, 256, 512, 352, 16)
        s = 0.02
        return {'x': jax.random.normal(ks[0], (B, T, D), jnp.float32), 'gate_w': jax.random.normal(ks[1], (NE, D), jnp.float32) * s, 'gate_b': jax.random.normal(ks[2], (NE,), jnp.float32) * s, 'w1_shared': jax.random.normal(ks[3], (D, H), jnp.float32) * s, 'w2_shared': jax.random.normal(ks[4], (H, D), jnp.float32) * s, 'w3_shared': jax.random.normal(ks[5], (D, H), jnp.float32) * s, 'w1_routed': jax.random.normal(ks[6], (NE, D, H), jnp.float32) * s, 'w2_routed': jax.random.normal(ks[7], (NE, H, D), jnp.float32) * s, 'w3_routed': jax.random.normal(ks[8], (NE, D, H), jnp.float32) * s}
    _L0_ffn_all = _L0_ffn_setup()
    _L0_ffn_in = {k: v for k, v in _L0_ffn_all.items() if k in ('gate_w', 'gate_b', 'w1_shared', 'w2_shared', 'w3_shared', 'w1_routed', 'w2_routed', 'w3_routed')}
    del _L0_ffn_all
    return {'x': x, 'ctx_2048': ctx_2048, 'mask_BxSxS2_ff0': mask_BxSxS2_ff0, 'L0_xattn_wq': _L0_xattn_in['wq'], 'L0_xattn_bq': _L0_xattn_in['bq'], 'L0_xattn_wk': _L0_xattn_in['wk'], 'L0_xattn_bk': _L0_xattn_in['bk'], 'L0_xattn_wv': _L0_xattn_in['wv'], 'L0_xattn_bv': _L0_xattn_in['bv'], 'L0_xattn_wo': _L0_xattn_in['wo'], 'L0_xattn_bo': _L0_xattn_in['bo'], 'L0_attn_Wkd': _L0_attn_in['Wkd'], 'L0_attn_bkd': _L0_attn_in['bkd'], 'L0_attn_Wqd': _L0_attn_in['Wqd'], 'L0_attn_bqd': _L0_attn_in['bqd'], 'L0_attn_Wku': _L0_attn_in['Wku'], 'L0_attn_bku': _L0_attn_in['bku'], 'L0_attn_Wvu': _L0_attn_in['Wvu'], 'L0_attn_bvu': _L0_attn_in['bvu'], 'L0_attn_Wqu': _L0_attn_in['Wqu'], 'L0_attn_bqu': _L0_attn_in['bqu'], 'L0_attn_Wkr': _L0_attn_in['Wkr'], 'L0_attn_bkr': _L0_attn_in['bkr'], 'L0_attn_Wqr': _L0_attn_in['Wqr'], 'L0_attn_bqr': _L0_attn_in['bqr'], 'L0_attn_Wo': _L0_attn_in['Wo'], 'L0_attn_bo': _L0_attn_in['bo'], 'L0_ffn_gate_w': _L0_ffn_in['gate_w'], 'L0_ffn_gate_b': _L0_ffn_in['gate_b'], 'L0_ffn_w1_shared': _L0_ffn_in['w1_shared'], 'L0_ffn_w2_shared': _L0_ffn_in['w2_shared'], 'L0_ffn_w3_shared': _L0_ffn_in['w3_shared'], 'L0_ffn_w1_routed': _L0_ffn_in['w1_routed'], 'L0_ffn_w2_routed': _L0_ffn_in['w2_routed'], 'L0_ffn_w3_routed': _L0_ffn_in['w3_routed']}

def reference(x, ctx_2048, mask_BxSxS2_ff0, L0_xattn_wq, L0_xattn_bq, L0_xattn_wk, L0_xattn_bk, L0_xattn_wv, L0_xattn_bv, L0_xattn_wo, L0_xattn_bo, L0_attn_Wkd, L0_attn_bkd, L0_attn_Wqd, L0_attn_bqd, L0_attn_Wku, L0_attn_bku, L0_attn_Wvu, L0_attn_bvu, L0_attn_Wqu, L0_attn_bqu, L0_attn_Wkr, L0_attn_bkr, L0_attn_Wqr, L0_attn_bqr, L0_attn_Wo, L0_attn_bo, L0_ffn_gate_w, L0_ffn_gate_b, L0_ffn_w1_shared, L0_ffn_w2_shared, L0_ffn_w3_shared, L0_ffn_w1_routed, L0_ffn_w2_routed, L0_ffn_w3_routed):
    import jax
    import jax.numpy as jnp

    def _L0_xattn_ref(x, cond, mask, wq, bq, wk, bk, wv, bv, wo, bo):
        import jax, jax.numpy as jnp
        import numpy as np
        NUM_HEADS = 16
        EPS = 1e-08

        def _dyn_quant(x):
            s = jnp.maximum(jnp.max(jnp.abs(x), axis=-1, keepdims=True) / 127.0, EPS)
            q = jnp.clip(jnp.round(x / s), -127.0, 127.0)
            return (q, s)

        def _quant_weight(w):
            s = jnp.maximum(jnp.max(jnp.abs(w), axis=1, keepdims=True) / 127.0, EPS)
            q = jnp.clip(jnp.round(w / s), -127.0, 127.0)
            return (q, s)

        def _w8a8_linear(x, w, b):
            qx, sx = _dyn_quant(x)
            qw, sw = _quant_weight(w)
            y = jnp.einsum('bnc,oc->bno', qx, qw) * (sx * sw[:, 0])
            return y + b
        B, N, C = x.shape
        L = cond.shape[1]
        H = NUM_HEADS
        D = C // H
        inv_sqrt_d = np.float32(1.0 / np.sqrt(D))
        q = _w8a8_linear(x, wq, bq).reshape(B, N, H, D).transpose(0, 2, 1, 3)
        k = (cond @ wk.T + bk).reshape(B, L, H, D).transpose(0, 2, 1, 3)
        v = (cond @ wv.T + bv).reshape(B, L, H, D).transpose(0, 2, 1, 3)
        scores = jnp.einsum('bhnd,bhld->bhnl', q, k) * inv_sqrt_d + mask[:, None]
        attn = jax.nn.softmax(scores, axis=-1)
        o = jnp.einsum('bhnl,bhld->bhnd', attn, v)
        o = o.transpose(0, 2, 1, 3).reshape(B, N, C)
        return _w8a8_linear(o, wo, bo)

    def _L0_attn_ref(x, Wkd, bkd, Wqd, bqd, Wku, bku, Wvu, bvu, Wqu, bqu, Wkr, bkr, Wqr, bqr, Wo, bo):
        import jax, jax.numpy as jnp
        import numpy as np
        B, S, D = (2, 512, 512)
        H, DH, DR = (16, 128, 64)
        DC_KV, DC_Q = (128, 384)
        ROPE_BASE = 10000.0

        def _rope(t):
            s, dr = (t.shape[1], t.shape[-1])
            inv_freq = 1.0 / ROPE_BASE ** (jnp.arange(0, dr, 2, dtype=jnp.float32) / dr)
            ang = jnp.arange(s, dtype=jnp.float32)[:, None] * inv_freq
            cos = jnp.tile(jnp.cos(ang), (1, 2))[None, :, None, :]
            sin = jnp.tile(jnp.sin(ang), (1, 2))[None, :, None, :]
            t1, t2 = jnp.split(t, 2, axis=-1)
            rot = jnp.concatenate([-t2, t1], axis=-1)
            return t * cos + rot * sin
        b, s, _ = x.shape
        kv_c = x @ Wkd.T + bkd
        q_c = x @ Wqd.T + bqd
        k_cnt = (kv_c @ Wku.T + bku).reshape(b, s, H, DH)
        v = (kv_c @ Wvu.T + bvu).reshape(b, s, H, DH)
        q_cnt = (q_c @ Wqu.T + bqu).reshape(b, s, H, DH)
        k_r = (x @ Wkr.T + bkr).reshape(b, s, H, DR)
        q_r = (q_c @ Wqr.T + bqr).reshape(b, s, H, DR)
        q_full = jnp.concatenate([q_cnt, _rope(q_r)], axis=-1)
        k_full = jnp.concatenate([k_cnt, _rope(k_r)], axis=-1)
        scale = 1.0 / jnp.sqrt(jnp.float32(DH + DR))
        scores = jnp.einsum('bqhd,bkhd->bhqk', q_full, k_full) * scale
        causal = jnp.tril(jnp.ones((s, s), dtype=bool))
        scores = jnp.where(causal[None, None], scores, jnp.float32(-1000000000.0))
        probs = jax.nn.softmax(scores, axis=-1)
        attn = jnp.einsum('bhqk,bkhd->bqhd', probs, v).reshape(b, s, H * DH)
        return attn @ Wo.T + bo

    def _L0_ffn_ref(x, gate_w, gate_b, w1_shared, w2_shared, w3_shared, w1_routed, w2_routed, w3_routed):
        import jax, jax.numpy as jnp
        import numpy as np
        TOP_K = 4
        n_experts = w1_routed.shape[0]
        logits = jnp.einsum('ed,btd->bte', gate_w, x)
        scores = jax.nn.sigmoid(logits) + gate_b
        weights, indices = jax.lax.top_k(scores, TOP_K)
        weights = weights / weights.sum(-1, keepdims=True)
        shared_out = jax.nn.silu(x @ w1_shared) * (x @ w3_shared) @ w2_shared
        one_hot = jax.nn.one_hot(indices, n_experts, dtype=x.dtype)
        router_probs = (weights[..., None] * one_hot).sum(-2)
        h1 = jnp.einsum('btd,edc->btec', x, w1_routed)
        h2 = jnp.einsum('btd,edc->btec', x, w3_routed)
        h3 = jax.nn.silu(h1 * h2)
        experts_out = jnp.einsum('btec,ecd->bted', h3, w2_routed)
        routed_out = jnp.einsum('bted,bte->btd', experts_out, router_probs)
        return shared_out + routed_out
    x = x + _L0_xattn_ref(_layernorm(x, axis=-1), ctx_2048, mask_BxSxS2_ff0, L0_xattn_wq, L0_xattn_bq, L0_xattn_wk, L0_xattn_bk, L0_xattn_wv, L0_xattn_bv, L0_xattn_wo, L0_xattn_bo)
    x = x + _L0_attn_ref(_layernorm(x, axis=-1), L0_attn_Wkd, L0_attn_bkd, L0_attn_Wqd, L0_attn_bqd, L0_attn_Wku, L0_attn_bku, L0_attn_Wvu, L0_attn_bvu, L0_attn_Wqu, L0_attn_bqu, L0_attn_Wkr, L0_attn_bkr, L0_attn_Wqr, L0_attn_bqr, L0_attn_Wo, L0_attn_bo)
    x = x + _L0_ffn_ref(_layernorm(x, axis=-1), L0_ffn_gate_w, L0_ffn_gate_b, L0_ffn_w1_shared, L0_ffn_w2_shared, L0_ffn_w3_shared, L0_ffn_w1_routed, L0_ffn_w2_routed, L0_ffn_w3_routed)
    return x

_drawn_inputs = setup_inputs


def setup_inputs(seed=0):
    import zlib

    import numpy as np

    out = dict(_drawn_inputs(seed))
    spreads = {'L0_xattn_bq': (0.0, 0.8),
     'L0_xattn_bk': (0.0, 0.8),
     'L0_xattn_bv': (0.0, 0.1),
     'L0_xattn_bo': (0.0, 0.1),
     'L0_attn_bkd': (0.0, 0.425),
     'L0_attn_bqd': (0.0, 0.8),
     'L0_attn_bku': (0.0, 0.8),
     'L0_attn_bvu': (0.0, 0.1),
     'L0_attn_bqu': (0.0, 0.8),
     'L0_attn_bkr': (0.0, 0.8),
     'L0_attn_bqr': (0.0, 0.8),
     'L0_attn_bo': (0.0, 0.1)}
    factors = {'L0_xattn_wq': 7.567,
     'L0_xattn_wk': 7.519,
     'L0_attn_Wqd': 8.0,
     'L0_attn_Wku': 8.0,
     'L0_attn_Wqu': 8.0,
     'L0_attn_Wkr': 8.0,
     'L0_attn_Wqr': 8.0,
     'L0_ffn_gate_w': 3.369,
     'L0_ffn_gate_b': 8.0,
     'L0_ffn_w1_routed': 2.928,
     'L0_ffn_w2_routed': 2.882,
     'L0_ffn_w3_routed': 2.939}
    for name, (base, spread) in spreads.items():
        noise = np.random.default_rng([zlib.crc32(name.encode()), seed]).standard_normal(out[name].shape)
        drawn = base * np.exp(spread * noise) if base else spread * noise
        out[name] = jnp.asarray(drawn.astype(out[name].dtype))
    for name, factor in factors.items():
        out[name] = (out[name] * factor).astype(out[name].dtype)
    return out
```

```python
from contextlib import ExitStack

import concourse.bass as bass
from concourse import mybir

F32 = mybir.dt.float32
F32R = mybir.dt.float32r
BF16 = mybir.dt.bfloat16
ALU = mybir.AluOpType
ACT = mybir.ActivationFunctionType
AX = mybir.AxisListType

P = 128
B, S, D = 2, 64, 512
KEYS = 1024
KT = D // P
XH, XD = 16, 32
NPAIR = XH // 2
H, DH, DR = 16, 128, 64
DQ = 384
QT = DQ // P
HG = 4
NE, TOPK, FH = 16, 4, 352
FT = 3
FP = FT * P
CH = 512
ITEM = 2048
RAW = 3
RING = 2
QMAX, QEPS = 127.0, 1e-8
ROUND = 1.5 * 2.0 ** 23
NEG = -1e30
X_SCALE = XD ** -0.5
M_SCALE = (DH + DR) ** -0.5
W13 = 2 * KT * FH
W2 = FT * D


def build(nc, a, out):
    ctx = ExitStack()
    with ctx:
        def sb(name, shape, dt=F32):
            return ctx.enter_context(nc.sbuf_tensor(name, shape, dt))

        def sem(name):
            return ctx.enter_context(nc.semaphore(name))

        raw = sb("raw", [P, RAW, ITEM])
        area = sb("area", [P, 17408])
        hl = sb("hl", [P, 2 * (W13 + W2) * 2], F32R)
        kbuf = area[:, 0:4096].rearrange("p (g k) -> p g k", g=4)
        vbuf = [area[:, 4096 * (1 + b):4096 * (2 + b)].rearrange("p (t n) -> p t n", t=8) for b in range(B)]
        sbuf = area[:, 12288:15360].rearrange("p (r k) -> p r k", r=3)
        ptbuf = area[:, 15360:17408].rearrange("p (r k) -> p r k", r=2)
        wq_raw = area[:, 12288:14336].rearrange("p (t n) -> p t n", t=4)
        wo_raw = area[:, 14336:16384].rearrange("p (t n) -> p t n", t=4)
        wq_int = area[:, 8192:9216].bitcast(BF16).rearrange("p (t n) -> p t n", t=4)
        wo_int = area[:, 9216:10240].bitcast(BF16).rearrange("p (t n) -> p t n", t=4)
        eraw13 = [area[:, (W13 + W2) * g:(W13 + W2) * g + W13] for g in range(2)]
        eraw2 = [area[:, (W13 + W2) * g + W13:(W13 + W2) * (g + 1)] for g in range(2)]
        qT = area[:, 9216:11264].rearrange("p (h t) -> p h t", h=H)
        kT = area[:, 11264:13312].rearrange("p (h t) -> p h t", h=H)
        vm = area[:, 13312:15360].rearrange("p (h d) -> p h d", h=H)
        krn = area[:, 15360:16384]
        qrn = area[:, 16384:17408]

        def pair(base):
            return [hl[:, base:base + ITEM], hl[:, base + ITEM:base + 2 * ITEM]]
        wk_hl, wv_hl = pair(0), pair(2 * ITEM)
        ring_hl = [pair((4 + 2 * r) * ITEM) for r in range(RING)]
        attnT = [t.rearrange("p (h t) -> p h t", h=H) for t in wk_hl]
        e13 = [[hl[:, (2 * g + s) * (W13 + W2):(2 * g + s) * (W13 + W2) + W13] for s in range(2)] for g in range(2)]
        e2 = [[hl[:, (2 * g + s) * (W13 + W2) + W13:(2 * g + s + 1) * (W13 + W2)] for s in range(2)] for g in range(2)]

        x = sb("x", [P, D])
        y = sb("y", [P, D])
        tmp = sb("tmp", [P, D])
        ob = sb("ob", [P, D])
        yT = [sb("yTh", [P, KT, P], F32R), sb("yTl", [P, KT, P], F32R)]
        cT = [sb("cTh", [P, KT, P], F32R), sb("cTl", [P, KT, P], F32R)]
        mask = sb("mask", [P, KEYS])
        qd = sb("qd", [P, 2048])
        qdv = qd[:, :].rearrange("p (b j q) -> p b j q", b=B, j=NPAIR)
        krT = qd[:, 0:1024].rearrange("p (j t) -> p j t", j=8)
        qrT = [qd[:, 1024:2048].rearrange("p (j t) -> p j t", j=8), qrn.rearrange("p (j t) -> p j t", j=8)]
        wint = sb("wint", [P, 2048])
        wqT = wint[:, 0:1024].bitcast(BF16).rearrange("p (k n) -> p k n", k=KT)
        woT = wint[:, 1024:2048].bitcast(BF16).rearrange("p (k n) -> p k n", k=KT)
        brope = wint
        bias_a = sb("bias_a", [P, D])
        bias_b = sb("bias_b", [P, D])
        swrow = sb("swrow", [P, D])
        rope = sb("rope", [P, 2, DR])
        ident = sb("ident", [P, P])
        identb = sb("identb", [P, P], BF16)
        cmask = sb("cmask", [P, P])
        ones = sb("ones", [P, P])
        bkT = sb("bkT", [P, 4])
        hbias = sb("hbias", [P, 3, H])
        gw = sb("gw", [P, KT, NE])
        gb = sb("gb", [P, NE])
        tri = area[:, 9728:9728 + NE * NE].rearrange("p (e f) -> p e f", e=NE)
        rk = area[:, 9216:9216 + 2 * NE * NE].rearrange("p (a e f) -> p a e f", a=2, e=NE)
        lg = sb("lg", [P, 6, NE])
        probs = sb("probs", [P, NE])
        small = sb("small", [P, 64])
        rsum = sb("rsum", [P, 32])
        nmax = sb("nmax", [P, 32])
        st = sb("st", [P, 8])
        mv = sb("mv", [P, 2])
        power = sb("power", [P, 1])

        xq = sb("xq", [P, D], BF16)
        xqT = sb("xqT", [P, D], BF16)
        dg = y[:, :].rearrange("p (t n) -> p t n", t=4)
        pg = [mask[:, 0:512], mask[:, 512:1024]]
        ptg = [tmp[:, :], ob[:, :]]

        h1c = [tmp[:, 0:FH], ob[:, 0:FH]]
        vv = [mask[:, 0:FH], mask[:, 512:512 + FH]]
        h3 = [qd[:, 0:FP], qd[:, 512:512 + FP]]
        hT = [t[:, 0:FT, :] for t in cT]

        proj = [ctx.enter_context(nc.psum_tensor(f"proj{i}", [P, 512], F32)) for i in range(2)]
        sps = ctx.enter_context(nc.psum_tensor("sps", [P, 1024], F32))
        tps = [ctx.enter_context(nc.psum_tensor(f"tps{i}", [P, 512], F32)) for i in range(2)]
        pvp = ctx.enter_context(nc.psum_tensor("pvp", [P, 512], F32))
        misc = ctx.enter_context(nc.psum_tensor("misc", [P, 512], F32))

        up_ps = [misc[:, :], pvp[:, :]]
        h2p = [sps[:, 0:FH], sps[:, 512:512 + FH]]

        raw_in = [sem(f"raw_in{i}") for i in range(RAW)]
        hi_done, lo_done = sem("hi_done"), sem("lo_done")
        x_second, bk_in, qrn_r, ropeq_step, f_lo13h = sem("x_second"), sem("bk_in"), sem("qrn_ready"), sem("rope_q_step"), sem("f_lo13_half")
        x_in, wq_in, wo_in, small_in, mask_in = sem("x_in"), sem("wq_in"), sem("wo_in"), sem("small_in"), sem("mask_in")
        ba_in, bb_in, brope_in = sem("ba_in"), sem("bb_in"), sem("brope_in")
        consts = sem("consts")
        dve = sem("dve_step")
        wq_step, wo_step, ropek_step = sem("wq_step"), sem("wo_step"), sem("rope_k_step")
        stats, vareps, rstd = sem("ln_stats"), sem("ln_var_eps"), sem("ln_rstd")
        swq_ready, wq_q, wo_q = sem("sw_ready"), sem("wq_quantised"), sem("wo_quantised")
        xq_ready, xqT_mm, xqT_ready = sem("xq_ready"), sem("xqT_mm"), sem("xqT_ready")
        wT_mm, wT_ready = sem("wT_mm"), sem("wT_ready")
        sw_mm, sw_row, diag = sem("sw_mm"), sem("sw_row"), sem("diag_ready")
        q_mm, q_ready, qT_mm, qd_ready = sem("q_mm"), sem("q_ready"), sem("qT_mm"), sem("qd_ready")
        proj_mm, k_out, v_out = sem("proj_mm"), sem("k_out"), sem("v_out")
        s_mm, s_red, nm_ready, e_done = sem("scores_mm"), sem("scores_reduced"), sem("neg_max"), sem("exp_done")
        t_mm, pt_a, pt_d, pv_mm, o_done = sem("t_mm"), sem("pt_act"), sem("pt_dve"), sem("pv_mm"), sem("o_done")
        y_ready, yT_mm, yTh_r, yTl_r = sem("y_ready"), sem("yT_mm"), sem("yTh_ready"), sem("yTl_ready")
        down_mm, down_r, cT_mm, cTh_r, cTl_r = sem("down_mm"), sem("down_ready"), sem("cT_mm"), sem("cTh_ready"), sem("cTl_ready")
        kr_mm, krn_r, kr_roped, krT_mm, krT_r = sem("kr_mm"), sem("krn_ready"), sem("kr_roped"), sem("krT_mm"), sem("krT_ready")
        qr_mm, qr_roped, qrT_mm, qrT_r = sem("qr_mm"), sem("qr_roped"), sem("qrT_mm"), sem("qrT_ready")
        up_mm, up_out, vu_mm, vu_out = sem("up_mm"), sem("up_out"), sem("vu_mm"), sem("vu_out")
        ms_mm, ms_sub, me_done, mp_r = sem("mla_scores_mm"), sem("mla_centred"), sem("mla_exp"), sem("mla_probs")
        mt_mm, mt_r, ma_mm, ma_b, ma_hi, ma_lo = sem("mla_pT_mm"), sem("mla_pT"), sem("mla_attn_mm"), sem("mla_attn"), sem("mla_attn_hi"), sem("mla_attn_lo")
        wo_mm = sem("wo_mm")
        yT32, gate_mm, gate_e, padded = sem("yT_f32"), sem("gate_mm"), sem("gate_exp"), sem("h3_padded")
        pad_ready, tri_ready, qr_zero = sem("pad_ready"), sem("tri_ready"), sem("qr_zero")
        e13_in = [sem(f"e13_in{g}") for g in range(2)]
        e2_in = [sem(f"e2_in{g}") for g in range(2)]
        f_hi13, f_lo13, f_hi2, f_lo2 = sem("f_hi13"), sem("f_lo13"), sem("f_hi2"), sem("f_lo2")
        f_h1, f_h2, f_h1c, f_v, f_silu, f_h3 = sem("f_h1_mm"), sem("f_h2_mm"), sem("f_h1_copied"), sem("f_product"), sem("f_silu"), sem("f_h3")
        f_t, f_thi, f_tlo, f_out = sem("f_t_mm"), sem("f_t_hi"), sem("f_t_lo"), sem("f_out_mm")
        res_ready, out_done = sem("result_ready"), sem("out_done")

        stream = [(a["wk"], ITEM), (a["ctx"][0], ITEM), (a["wv"], ITEM)] + [(a["ctx"][c], ITEM) for c in (1, 2, 3)]
        N_X = len(stream)
        stream += [(a["wd"], ITEM)] + [(a["wkr"][j], ITEM) for j in range(2)] + [(a["wku"], ITEM)]
        stream += [(a["wvu"], ITEM)] + [(a["wqr"][j], QT * 512) for j in range(2)]
        stream += [(a["wqu"][j], QT * 512) for j in range(4)] + [(a["wom"][j], ITEM) for j in range(4)]
        where, r = [], 0
        for q in range(len(stream)):
            if q == 0:
                where.append((wk_hl, None))
            elif q == 2:
                where.append((wv_hl, None))
            else:
                where.append((ring_hl[r % RING], r))
                r += 1
        CTX_Q = [1, 3, 4, 5]
        WD_Q, WKR_Q, WKU_Q, WVU_Q, WQR_Q, WQU_Q, WOM_Q = 6, 7, 9, 10, 11, 13, 17

        parts = []
        for c in range(2):
            parts += [("K", c, g) for g in range(4)] + [("V", c, t) for t in range(4)]
        for u in range(NPAIR):
            parts.append(("V", 2 + u // 4, u % 4))
            if u:
                parts.append(("K", 2 + (u - 1) % 2, (u - 1) // 2))
        parts.append(("K", 3, 3))
        k_before = [sum(p[0] == "K" for p in parts[:n + 1]) for n in range(len(parts))]
        v_before = [sum(p[0] == "V" for p in parts[:n + 1]) for n in range(len(parts))]
        freed = [(proj_mm, max(n for n, p in enumerate(parts) if p[1] == c) + 1) for c in range(4)]
        freed += [(down_mm, 1), (kr_mm, 1), (kr_mm, 2), (up_mm, 4), (vu_mm, 4), (qr_mm, 1), (qr_mm, 2)]
        freed += [(up_mm, 5 + j) for j in range(4)] + [(wo_mm, j + 1) for j in range(4)]

        block = ctx.enter_context(nc.Block())


        def rows(v):
            return v.partition_broadcast(P)

        def e_of(w, e):
            return w[e] if isinstance(e, int) else w[bass.ds(e, 1)].rearrange("e d n -> (e d) n")

        @block.sync
        def _(sp):
            def item(q):
                if q >= RAW:
                    sp.wait_ge(lo_done, q - RAW + 1)
                sp.dma_start(raw[:, q % RAW, 0:stream[q][1]], stream[q][0]).then_inc(raw_in[q % RAW], 16)

            def expert13(g, w1, w3):
                sp.dma_start(eraw13[g][:, 0:KT * FH], w1.rearrange("(p k) n -> p (k n)", k=KT)).then_inc(e13_in[g], 16)
                sp.dma_start(eraw13[g][:, KT * FH:W13], w3.rearrange("(p k) n -> p (k n)", k=KT)).then_inc(e13_in[g], 16)

            def expert2(g, w2):
                sp.dma_start(eraw2[g][:, 0:2 * D].rearrange("p (t n) -> p t n", t=2),
                             w2[0:2 * P, :].rearrange("(t p) n -> p t n", p=P)).then_inc(e2_in[g], 16)
                sp.dma_start(eraw2[g][0:FH - 2 * P, 2 * D:3 * D], w2[2 * P:FH, :]).then_inc(e2_in[g], 16)

            def routed(g, n, e):
                sp.wait_ge(f_lo13, n - 1)
                expert13(g, e_of(a["w1r"], e), e_of(a["w3r"], e))
                sp.wait_ge(f_lo2, n - 1)
                expert2(g, e_of(a["w2r"], e))

            item(0)
            item(1)
            sp.dma_start(x[:, :], a["x"]).then_inc(x_in, 16)
            item(2)
            sp.dma_start(wq_raw, a["wq"]).then_inc(wq_in, 16)
            item(3)
            sp.dma_start(bkT[:, :], a["bkT"]).then_inc(bk_in, 16)
            sp.dma_start(bias_a[:, :], rows(a["bq"])).then_inc(ba_in, 16)
            item(4)
            sp.dma_start(mask[0:S, :], a["mask"][0:S, :]).then_inc(mask_in, 16)
            sp.dma_start(mask[S:P, :], a["mask"][0:S, :]).then_inc(mask_in, 16)
            sp.dma_start(wo_raw, a["wo"]).then_inc(wo_in, 16)
            item(5)
            sp.dma_start(bias_b[:, :], rows(a["bv"])).then_inc(bb_in, 16)
            sp.dma_start(hbias[:, :, :], a["hbias"]).then_inc(small_in, 16)
            sp.dma_start(gw[:, :, :], a["gw"]).then_inc(small_in, 16)
            sp.dma_start(gb[:, :], rows(a["gb"])).then_inc(small_in, 16)
            sp.dma_start(rope[:, :, :], a["rope"]).then_inc(small_in, 16)
            item(6)
            sp.wait_ge(q_ready, 1)
            sp.dma_start(bias_a[:, :], rows(a["bo"])).then_inc(ba_in, 16)
            sp.wait_ge(s_red, NPAIR)
            sp.dma_start(mask[0:S, :], a["mask"][S:P, :]).then_inc(mask_in, 16)
            sp.dma_start(mask[S:P, :], a["mask"][S:P, :]).then_inc(mask_in, 16)
            item(7)
            item(8)
            sp.wait_ge(pad_ready, 2)
            expert13(0, a["w1s"], a["w3s"])
            sp.wait_ge(xq_ready, 2)
            sp.dma_start(bias_b[:, :], rows(a["bd"])).then_inc(bb_in, 16)
            sp.wait_ge(q_mm, 2)
            sp.dma_start(brope[:, 0:1024], rows(a["bkr"])).then_inc(brope_in, 16)
            sp.dma_start(brope[:, 1024:2048], rows(a["bqr"])).then_inc(brope_in, 16)
            sp.wait_ge(x_second, 1)
            sp.dma_start(bias_a[:, :], rows(a["bom"])).then_inc(ba_in, 16)
            for q in range(9, len(stream)):
                item(q)
                if q == WQU_Q:
                    expert2(0, a["w2s"])
                if q == WQU_Q + 2:
                    expert13(1, a["w1r"][0], a["w3r"][0])
                if q == WOM_Q:
                    expert2(1, a["w2r"][0])
            with sp.Fori(0, NE // 2 - 1) as i:
                routed(0, 2 * i + 2, 2 * i + 1)
                routed(1, 2 * i + 3, 2 * i + 2)
            routed(0, NE, NE - 1)
            sp.wait_ge(res_ready, 1)
            sp.dma_start(out, x[:, :]).then_inc(out_done, 16)
            sp.wait_ge(out_done, 16)

        def rotate(nceng, eng, t, b, step, base, done):
            tv = t.rearrange("p (h r) -> p h r", h=H)
            bv = b.rearrange("p (h r) -> p h r", h=H)
            half = DR // 2
            nceng.tensor_tensor(bv[:, :, 0:half], tv[:, :, half:DR],
                                rope[:, 1:2, 0:half].to_broadcast([P, H, half]), ALU.mult).then_inc(step, 1)
            nceng.tensor_tensor(bv[:, :, half:DR], tv[:, :, 0:half],
                                rope[:, 1:2, half:DR].to_broadcast([P, H, half]), ALU.mult).then_inc(step, 1)
            eng.wait_ge(step, base + 2)
            nceng.tensor_tensor(tv, tv, rope[:, 0:1, :].to_broadcast([P, H, DR]), ALU.mult).then_inc(step, 1)
            eng.wait_ge(step, base + 3)
            nceng.tensor_tensor(t, t, b, ALU.add).then_inc(done, 1)

        @block.gpsimd
        def _(gp):
            def inverse_deviation(n):
                gp.wait_ge(stats, n + 1)
                nc.gpsimd.tensor_scalar(small[:, 60:61], mv[:, 1:2], 1e-5, None, ALU.add).then_inc(vareps, 1)
                gp.wait_ge(vareps, n + 1)
                nc.gpsimd.tensor_tensor(small[:, 61:62], small[:, 60:61], power[:, :], ALU.pow).then_inc(rstd, 1)

            def quantise(src, dst, n, loaded, step, done):
                gp.wait_ge(loaded, 16)
                gp.wait_ge(swq_ready, n + 1)
                for t in range(4):
                    nc.gpsimd.tensor_scalar(src[:, t, :], src[:, t, :], small[:, 16 * n + 8 + t:16 * n + 9 + t],
                                            QMAX, ALU.mult, ALU.min).then_inc(step, 1)
                gp.wait_ge(step, 4)
                nc.gpsimd.tensor_scalar(src, src, -QMAX, ROUND, ALU.max, ALU.add).then_inc(step, 1)
                gp.wait_ge(step, 5)
                nc.gpsimd.tensor_scalar(dst, src, ROUND, None, ALU.subtract).then_inc(done, 1)

            nc.gpsimd.memset(power[:, :], -0.5).then_inc(consts, 1)
            nc.gpsimd.memset(identb[:, :], 0.0).then_inc(consts, 1)
            nc.gpsimd.memset(ident[:, :], 0.0).then_inc(consts, 1)
            nc.gpsimd.memset(ones[:, :], 1.0).then_inc(consts, 1)
            gp.wait_ge(consts, 4)
            for m in (identb, ident):
                gp.affine_select(out=m[:, :], in_=m[:, :], compare_op=ALU.not_equal, fill=1.0, base=0,
                                 pattern=[[-1, P]], channel_multiplier=1).then_inc(consts, 1)
            inverse_deviation(0)
            quantise(wq_raw, wq_int, 0, wq_in, wq_step, wq_q)
            nc.gpsimd.memset(qd[:, :], 0.0).then_inc(consts, 1)
            nc.gpsimd.memset(cmask[:, :], 0.0).then_inc(consts, 1)
            gp.wait_ge(consts, 8)
            gp.affine_select(out=cmask[:, :], in_=cmask[:, :], compare_op=ALU.is_ge, fill=NEG, base=0,
                             pattern=[[-1, P]], channel_multiplier=1).then_inc(consts, 1)
            gp.wait_ge(consts, 9)
            nc.gpsimd.memset(cmask[S:P, 0:S], NEG).then_inc(consts, 1)
            gp.wait_ge(consts, 10)
            quantise(wo_raw, wo_int, 1, wo_in, wo_step, wo_q)
            gp.wait_ge(pv_mm, 2 * NPAIR)
            for g in range(2):
                nc.gpsimd.memset(eraw2[g][96:P, 2 * D:3 * D], 0.0).then_inc(pad_ready, 1)
            gp.wait_ge(pad_ready, 2)
            inverse_deviation(1)
            gp.wait_ge(krn_r, 2)
            gp.wait_ge(small_in, 64)
            gp.wait_ge(s_mm, 2 * NPAIR)
            rotate(nc.gpsimd, gp, krn, qd[:, 0:1024], ropek_step, 0, kr_roped)
            gp.wait_ge(ms_mm, 4)
            nc.gpsimd.memset(tri, 1.0).then_inc(tri_ready, 1)
            gp.wait_ge(tri_ready, 1)
            gp.affine_select(out=tri, in_=tri, compare_op=ALU.is_gt, fill=0.0, base=0,
                             pattern=[[1, NE], [-1, NE]], channel_multiplier=0).then_inc(tri_ready, 1)
            inverse_deviation(2)

            def lo2(n, g):
                gp.wait_ge(f_hi2, n + 1)
                nc.gpsimd.tensor_tensor(e2[g][1], eraw2[g], e2[g][0], ALU.subtract).then_inc(f_lo2, 1)

            lo2(0, 0)
            for n in (1, 2):
                lo2(n, n % 2)
            with gp.Fori(0, NE // 2 - 2) as i:
                lo2(2 * i + 3, 1)
                lo2(2 * i + 4, 0)
            for n in (NE - 1, NE):
                lo2(n, n % 2)

        @block.scalar
        def _(act):
            def copy(o, i):
                return nc.scalar.activation(o, i, ACT.Copy)

            def hi(q):
                w = stream[q][1]
                dst, r = where[q]
                act.wait_ge(raw_in[q % RAW], 16 * (q // RAW + 1))
                if r is not None and r >= RING:
                    act.wait_ge(*freed[r - RING])
                copy(dst[0][:, 0:w], raw[:, q % RAW, 0:w]).then_inc(hi_done, 1)

            def k_evac(n):
                _, c, g = parts[n]
                act.wait_ge(proj_mm, n + 1)
                nc.scalar.activation(kbuf[:, g, (c % 2) * CH:(c % 2 + 1) * CH], proj[n % 2][:, :], ACT.Identity,
                                     bias=bkT[:, g:g + 1]).then_inc(k_out, 1)

            ks = [n for n, p in enumerate(parts) if p[0] == "K"]
            hi(0)
            hi(1)
            hi(2)
            hi(3)
            act.wait_ge(bk_in, 16)
            for n in ks[0:4]:
                k_evac(n)

            def wT_evac(dst, n):
                for k2 in range(2):
                    act.wait_ge(wT_mm, 2 * n + k2 + 1)
                    copy(dst[:, 2 * k2:2 * k2 + 2, :].rearrange("p k n -> p (k n)"), tps[k2][:, :].bitcast(BF16)).then_inc(wT_ready, 1)

            hi(4)
            wT_evac(wqT, 0)
            for n in ks[4:8]:
                k_evac(n)
            hi(5)
            wT_evac(woT, 1)

            def exp_pair(w):
                act.wait_ge(nm_ready, w + 1)
                s = sbuf[:, w % 3, :]
                nc.scalar.activation(s, s, ACT.Exp, bias=nmax[:, 16 + w:17 + w], accum_out=rsum[:, w:w + 1]).then_inc(e_done, 1)

            def pt_evac(w):
                act.wait_ge(t_mm, 2 * w + 1)
                if w >= 2:
                    act.wait_ge(pv_mm, w - 1)
                copy(ptbuf[:, w % 2, 0:512], tps[0][:, :]).then_inc(pt_a, 1)

            kq = list(ks[8:])
            for u in range(NPAIR):
                exp_pair(u)
                if u >= 2:
                    pt_evac(u - 2)
                if u:
                    k_evac(kq.pop(0))
            k_evac(kq.pop(0))
            pt_evac(NPAIR - 2)
            pt_evac(NPAIR - 1)
            hi(6)
            for u in range(NPAIR):
                w = NPAIR + u
                exp_pair(w)
                if u >= 1:
                    pt_evac(w - 1)
            pt_evac(2 * NPAIR - 1)

            def yT_hi(n):
                act.wait_ge(yT_mm, n)
                copy(yT[0][:, :, :].rearrange("p k t -> p (k t)"), misc[:, :]).then_inc(yTh_r, 1)

            hi(7)
            yT_hi(1)
            act.wait_ge(cT_mm, 1)
            copy(cT[0][:, :, :].rearrange("p k t -> p (k t)"), misc[:, :]).then_inc(cTh_r, 1)
            hi(8)
            hi(9)
            hi(10)
            hi(11)
            for j in range(4):
                act.wait_ge(vu_mm, j + 1)
                copy(vm[:, 4 * j:4 * j + 4, :].rearrange("p h d -> p (h d)"), proj[j % 2][:, :]).then_inc(vu_out, 1)
            for q in range(12, 17):
                hi(q)
            for j in range(2):
                act.wait_ge(krT_mm, j + 1)
                copy(krT[:, 4 * j:4 * j + 4, :].rearrange("p j t -> p (j t)"), tps[j][:, :]).then_inc(krT_r, 1)
            hi(17)
            hi(18)
            act.wait_ge(qrT_mm, 2)
            for j in range(2):
                for e in range(2):
                    rr = slice(DR * e, DR * (e + 1))
                    copy(qrT[e][rr, 4 * j:4 * j + 4, :].rearrange("p j t -> p (j t)"), tps[j][rr, :]).then_inc(qrT_r, 1)
            for g in range(4):
                act.wait_ge(ms_sub, g + 1)
                nc.scalar.activation(pg[g % 2], pg[g % 2], ACT.Exp, scale=M_SCALE).then_inc(me_done, 1)
                act.wait_ge(mt_mm, g + 1)
                if g >= 2:
                    act.wait_ge(ma_mm, g - 1)
                copy(ptg[g % 2], tps[g % 2][:, :]).then_inc(mt_r, 1)
                act.wait_ge(ma_b, g + 1)
                copy(attnT[0][:, 4 * g:4 * g + 4, :].rearrange("p h t -> p (h t)"), y[:, :]).then_inc(ma_hi, 1)
            hi(19)
            hi(20)
            yT_hi(2)
            act.wait_ge(gate_mm, 1)
            nc.scalar.activation(lg[:, 0, :], misc[:, 0:NE], ACT.Exp, scale=-1.0).then_inc(gate_e, 1)

            def hi13(n, g, turn, half):
                if half == 0:
                    act.wait_ge(e13_in[g], 32 * (turn + 1))
                    if not isinstance(n, int) or n >= 2:
                        act.wait_ge(f_h2, n - 1)
                c = slice(half * KT * FH, (half + 1) * KT * FH)
                copy(e13[g][0][:, c], eraw13[g][:, c]).then_inc(f_hi13, 1)

            def hi2(n, g, turn):
                act.wait_ge(e2_in[g], 32 * (turn + 1))
                if not isinstance(n, int) or n >= 2:
                    act.wait_ge(f_out, n - 1)
                copy(e2[g][0], eraw2[g]).then_inc(f_hi2, 1)

            def silu(m, g):
                act.wait_ge(f_v, m)
                nc.scalar.activation(vv[g], vv[g], ACT.Silu).then_inc(f_silu, 1)

            def t_hi(m):
                act.wait_ge(f_t, m + 1)
                copy(hT[0].rearrange("p k t -> p (k t)"), tps[0][:, 0:FP]).then_inc(f_thi, 1)

            def h1_copy(n, g, func=ACT.Copy):
                act.wait_ge(f_h1, n + 1)
                if not isinstance(n, int) or n >= 2:
                    act.wait_ge(f_h3, n - 1)
                nc.scalar.activation(h1c[g], proj[g][:, 0:FH], func).then_inc(f_h1c, 1)

            def step(n, g, turn, turn_next, first=False, last=False):
                if not first:
                    silu(n - 1, 1 - g)
                if not last:
                    hi13(n + 1, 1 - g, turn_next, 0)
                t_hi(n - 1)
                if not last:
                    hi13(n + 1, 1 - g, turn_next, 1)
                h1_copy(n, g)
                hi2(n, g, turn)

            act.wait_ge(wo_mm, 4)
            hi13(0, 0, 0, 0)
            hi13(0, 0, 0, 1)
            hi2(0, 0, 0)
            hi13(1, 1, 0, 0)
            hi13(1, 1, 0, 1)
            h1_copy(0, 0, ACT.Silu)
            step(1, 1, 0, 1, first=True)
            step(2, 0, 1, 1)
            with act.Fori(0, NE // 2 - 2) as i:
                step(2 * i + 3, 1, i + 1, i + 2)
                step(2 * i + 4, 0, i + 2, i + 2)
            step(NE - 1, 1, NE // 2 - 1, NE // 2)
            step(NE, 0, NE // 2, 0, last=True)
            silu(NE, 0)
            t_hi(NE)

        @block.vector
        def _(v):
            count = [0]

            def link(ins):
                count[0] += 1
                ins.then_inc(dve, 1)
                v.wait_ge(dve, count[0])

            def lo(q):
                w = stream[q][1]
                dst, _ = where[q]
                v.wait_ge(hi_done, q + 1)
                nc.vector.tensor_tensor(dst[1][:, 0:w], raw[:, q % RAW, 0:w], dst[0][:, 0:w], ALU.subtract).then_inc(lo_done, 1)

            def v_evac(n):
                _, c, t = parts[n]
                v.wait_ge(proj_mm, n + 1)
                nc.vector.tensor_copy(vbuf[c // 2][:, (c % 2) * 4 + t, :], proj[n % 2][:, :]).then_inc(v_out, 1)

            def layer_norm(n):
                link(nc.vector.bn_stats(st[:, 0:6], x[:, :]))
                nc.vector.bn_aggr(mv[:, :], st[:, 0:6]).then_inc(stats, 1)
                v.wait_ge(rstd, n + 1)
                nc.vector.tensor_scalar(y[:, :], x[:, :], mv[:, 0:1], small[:, 61:62], ALU.subtract, ALU.mult).then_inc(y_ready, 1)
                v.wait_ge(y_ready, n + 1)

            def scales(src, amax, s, rs, ready):
                link(nc.vector.tensor_reduce(amax, src, AX.X, ALU.max, apply_absolute_value=True))
                link(nc.vector.tensor_scalar(s, amax, 1.0 / QMAX, QEPS, ALU.mult, ALU.max))
                ins = nc.vector.reciprocal(rs, s)
                link(ins)
                if ready is not None:
                    v.sem_inc(ready, 1)

            def quantise_rows(src, n):
                scales(src, small[:, 32:33], small[:, 33 + n:34 + n], small[:, 35:36], None)
                link(nc.vector.tensor_scalar(tmp[:, :], src, small[:, 35:36], QMAX, ALU.mult, ALU.min))
                link(nc.vector.tensor_scalar(tmp[:, :], tmp[:, :], -QMAX, ROUND, ALU.max, ALU.add))
                nc.vector.tensor_scalar(xq[:, :], tmp[:, :], ROUND, None, ALU.subtract).then_inc(xq_ready, 1)

            def weight_scales(src, n, loaded):
                v.wait_ge(loaded, 16)
                scales(src, small[:, 16 * n:16 * n + 4], small[:, 16 * n + 4:16 * n + 8], small[:, 16 * n + 8:16 * n + 12], swq_ready)

            def scale_row(n):
                for t in range(4):
                    nc.vector.tensor_scalar(dg[:, t, :], ident[:, :], small[:, 16 * n + 4 + t:16 * n + 5 + t], None,
                                            ALU.mult).then_inc(diag, 1)

            def xqT_copy(n):
                v.wait_ge(xqT_mm, n + 1)
                nc.vector.tensor_copy(xqT[:, :], misc[:, 0:256].bitcast(BF16)).then_inc(xqT_ready, 1)

            def take_row(n):
                v.wait_ge(sw_mm, n + 1)
                nc.vector.tensor_copy(swrow[:, :], misc[:, :]).then_inc(sw_row, 1)

            def dequantise(dst, n, bias, bias_in, level):
                v.wait_ge(sw_row, n + 1)
                v.wait_ge(q_mm, n + 1)
                link(nc.vector.scalar_tensor_tensor(dst, misc[:, :], small[:, 33 + n:34 + n], swrow[:, :], ALU.mult, ALU.mult))
                v.wait_ge(bias_in, level)
                nc.vector.tensor_tensor(dst, dst, bias[:, :], ALU.add).then_inc(q_ready, 1)
                v.wait_ge(q_ready, n + 1)

            lo(0)
            lo(1)
            v.wait_ge(x_in, 16)
            layer_norm(0)
            quantise_rows(y[:, :], 0)
            lo(2)
            weight_scales(wq_raw, 0, wq_in)
            lo(3)
            vs = [n for n, p in enumerate(parts) if p[0] == "V"]
            for n in vs[0:4]:
                v_evac(n)
            lo(4)
            xqT_copy(0)
            weight_scales(wo_raw, 1, wo_in)
            v.wait_ge(consts, 6)
            scale_row(0)
            take_row(0)
            dequantise(tmp[:, :], 0, bias_a, ba_in, 16)
            for n in vs[4:8]:
                v_evac(n)
            lo(5)
            v.wait_ge(qT_mm, 1)
            v.wait_ge(consts, 7)
            mv4 = misc[:, :].rearrange("p (g b q) -> p g b q", g=4, b=B)
            for r in range(4):
                rr = slice(XD * r, XD * (r + 1))
                for b in range(B):
                    dst = qdv[rr, b, :, :].rearrange("p (g two) q -> p g two q", two=2)[:, :, r // 2, (r % 2) * S:(r % 2 + 1) * S]
                    nc.vector.tensor_scalar(dst, mv4[rr, :, b, :], X_SCALE, None, ALU.mult).then_inc(qd_ready, 1)

            def reduce_pair(w):
                v.wait_ge(s_mm, w + 1)
                v.wait_ge(mask_in, 32 * (w // NPAIR + 1))
                if w >= 3:
                    v.wait_ge(t_mm, 2 * (w - 2))
                nc.vector.tensor_tensor_reduce(sbuf[:, w % 3, :], sps[:, :], mask[:, :], 1.0, -3e38, ALU.add, ALU.max,
                                               accum_out=nmax[:, w:w + 1]).then_inc(s_red, 1)
                v.wait_ge(s_red, w + 1)
                nc.vector.tensor_scalar(nmax[:, 16 + w:17 + w], nmax[:, w:w + 1], -1.0, None, ALU.mult).then_inc(nm_ready, 1)

            def pt_evac(w):
                v.wait_ge(t_mm, 2 * w + 2)
                if w >= 2:
                    v.wait_ge(pv_mm, w - 1)
                nc.vector.tensor_copy(ptbuf[:, w % 2, 512:1024], tps[1][:, :]).then_inc(pt_d, 1)

            def attend_out(b):
                v.wait_ge(e_done, (b + 1) * NPAIR)
                link(nc.vector.reciprocal(rsum[:, 16 + b * NPAIR:16 + (b + 1) * NPAIR], rsum[:, b * NPAIR:(b + 1) * NPAIR]))
                v.wait_ge(pv_mm, (b + 1) * NPAIR)
                pv4 = pvp[:, :].rearrange("p (j two d) -> p j two d", j=NPAIR, two=2)
                o4 = ob[:, :].rearrange("p (j two d) -> p j two d", j=NPAIR, two=2)
                for t in range(2):
                    rr = slice(S * t, S * (t + 1))
                    nc.vector.tensor_tensor(o4[S * b:S * (b + 1), :, t, :], pv4[rr, :, t, :],
                                            rsum[rr, 16 + b * NPAIR:16 + (b + 1) * NPAIR].unsqueeze(2).to_broadcast([S, NPAIR, XD]),
                                            ALU.mult).then_inc(o_done, 1)

            vq = list(vs[8:])
            for u in range(NPAIR):
                reduce_pair(u)
                v_evac(vq.pop(0))
                if u >= 2:
                    pt_evac(u - 2)
            pt_evac(NPAIR - 2)
            pt_evac(NPAIR - 1)
            attend_out(0)
            scale_row(1)
            lo(6)
            for u in range(NPAIR):
                reduce_pair(NPAIR + u)
                if u >= 1:
                    pt_evac(NPAIR + u - 1)
            pt_evac(2 * NPAIR - 1)
            take_row(1)
            attend_out(1)
            v.wait_ge(o_done, 4)
            v.wait_ge(bb_in, 16)
            link(nc.vector.tensor_tensor(ob[:, :], ob[:, :], bias_b[:, :], ALU.add))
            quantise_rows(ob[:, :], 1)
            xqT_copy(1)
            dequantise(tmp[:, :], 1, bias_a, ba_in, 32)
            nc.vector.tensor_tensor(x[:, :], x[:, :], tmp[:, :], ALU.add).then_inc(x_second, 1)
            v.wait_ge(x_second, 1)
            layer_norm(1)

            def yT_lo(n):
                v.wait_ge(yTh_r, n)
                nc.vector.tensor_tensor(yT[1][:, :, :].rearrange("p k t -> p (k t)"), misc[:, :],
                                        yT[0][:, :, :].rearrange("p k t -> p (k t)"), ALU.subtract).then_inc(yTl_r, 1)

            yT_lo(1)
            lo(7)
            v.wait_ge(down_mm, 1)
            v.wait_ge(bb_in, 32)
            nc.vector.tensor_tensor(tmp[:, :], proj[0][:, :], bias_b[:, :], ALU.add).then_inc(down_r, 1)
            v.wait_ge(cTh_r, 1)
            nc.vector.tensor_tensor(cT[1][:, :, :].rearrange("p k t -> p (k t)"), misc[:, :],
                                    cT[0][:, :, :].rearrange("p k t -> p (k t)"), ALU.subtract).then_inc(cTl_r, 1)
            lo(8)
            v.wait_ge(brope_in, 32)
            for j in range(2):
                v.wait_ge(kr_mm, j + 1)
                nc.vector.tensor_tensor(krn[:, 512 * j:512 * (j + 1)], sps[:, 512 * j:512 * (j + 1)],
                                        brope[:, 512 * j:512 * (j + 1)], ALU.add).then_inc(krn_r, 1)
                lo(9 + j)

            def up_evac(n, dst, which):
                v.wait_ge(up_mm, n + 1)
                j = n % 4
                nc.vector.tensor_tensor(dst[:, 4 * j:4 * j + 4, :], up_ps[n % 2].rearrange("p (h t) -> p h t", h=4),
                                        hbias[:, which, 4 * j:4 * j + 4].unsqueeze(2).to_broadcast([P, 4, P]),
                                        ALU.add).then_inc(up_out, 1)

            v.wait_ge(small_in, 64)
            for j in range(4):
                up_evac(j, kT, 0)
            lo(11)
            lo(12)
            for j in range(2):
                v.wait_ge(qr_mm, j + 1)
                nc.vector.tensor_tensor(qrn[:, 512 * j:512 * (j + 1)], sps[:, 512 * j:512 * (j + 1)],
                                        brope[:, 1024 + 512 * j:1024 + 512 * (j + 1)], ALU.add).then_inc(qrn_r, 1)
                lo(13 + j)
            v.wait_ge(qrn_r, 2)
            rotate(nc.vector, v, qrn, qd[:, 1024:2048], ropeq_step, 0, qr_roped)
            v.wait_ge(qr_roped, 1)
            nc.vector.memset(qd[DR:P, 1024:2048], 0.0).then_inc(qr_zero, 1)
            up_evac(4, qT, 1)
            lo(15)
            up_evac(5, qT, 1)
            lo(16)
            up_evac(6, qT, 1)
            lo(17)
            up_evac(7, qT, 1)
            lo(18)
            v.wait_ge(qrT_mm, 2)
            nc.vector.memset(qrn[0:DR, :], 0.0).then_inc(qr_zero, 1)
            v.wait_ge(consts, 10)
            for g in range(4):
                pgv = pg[g % 2].rearrange("p (h k) -> p h k", h=HG)
                v.wait_ge(ms_mm, g + 1)
                if g >= 2:
                    v.wait_ge(mt_mm, g - 1)
                link(nc.vector.tensor_tensor(pgv, sps[:, 512 * (g % 2):512 * (g % 2 + 1)].rearrange("p (h k) -> p h k", h=HG),
                                             cmask[:, :].unsqueeze(1).to_broadcast([P, HG, P]), ALU.add))
                link(nc.vector.tensor_reduce(small[:, 40:44], pgv, AX.X, ALU.max))
                nc.vector.tensor_tensor(pgv, pgv, small[:, 40:44].unsqueeze(2).to_broadcast([P, HG, P]),
                                        ALU.subtract).then_inc(ms_sub, 1)
                v.wait_ge(me_done, g + 1)
                link(nc.vector.tensor_reduce(small[:, 44:48], pgv, AX.X, ALU.add))
                link(nc.vector.reciprocal(small[:, 48:52], small[:, 44:48]))
                nc.vector.tensor_tensor(pgv, pgv, small[:, 48:52].unsqueeze(2).to_broadcast([P, HG, P]),
                                        ALU.mult).then_inc(mp_r, 1)
                v.wait_ge(ma_mm, g + 1)
                nc.vector.tensor_tensor(y[:, :].rearrange("p (h t) -> p h t", h=4), proj[g % 2][:, :].rearrange("p (h t) -> p h t", h=4),
                                        hbias[:, 2, 4 * g:4 * g + 4].unsqueeze(2).to_broadcast([P, 4, P]), ALU.add).then_inc(ma_b, 1)
                v.wait_ge(ma_hi, g + 1)
                nc.vector.tensor_tensor(attnT[1][:, 4 * g:4 * g + 4, :].rearrange("p h t -> p (h t)"), y[:, :],
                                        attnT[0][:, 4 * g:4 * g + 4, :].rearrange("p h t -> p (h t)"), ALU.subtract).then_inc(ma_lo, 1)
            v.wait_ge(ma_lo, 4)
            lo(19)
            lo(20)
            v.wait_ge(ba_in, 48)
            v.wait_ge(wo_mm, 4)
            link(nc.vector.tensor_tensor(tmp[:, :], pvp[:, :], bias_a[:, :], ALU.add))
            link(nc.vector.tensor_tensor(x[:, :], x[:, :], tmp[:, :], ALU.add))
            layer_norm(2)
            yT_lo(2)
            nc.vector.tensor_copy(tmp[:, :], misc[:, :]).then_inc(yT32, 1)

            def lo13(n, g, half):
                v.wait_ge(f_hi13, 2 * n + 1 + half)
                c = slice(half * KT * FH, (half + 1) * KT * FH)
                nc.vector.tensor_tensor(e13[g][1][:, c], eraw13[g][:, c], e13[g][0][:, c], ALU.subtract)\
                    .then_inc(f_lo13h if half == 0 else f_lo13, 1)

            lo13(0, 0, 0)
            lo13(0, 0, 1)
            v.wait_ge(gate_e, 1)
            link(nc.vector.tensor_scalar(lg[:, 1, :], lg[:, 0, :], 1.0, None, ALU.add))
            link(nc.vector.reciprocal(lg[:, 2, :], lg[:, 1, :]))
            link(nc.vector.tensor_tensor(lg[:, 3, :], lg[:, 2, :], gb[:, :], ALU.add))
            other = lg[:, 3, :].unsqueeze(1).to_broadcast([P, NE, NE])
            own = lg[:, 3, :].unsqueeze(2).to_broadcast([P, NE, NE])
            link(nc.vector.tensor_tensor(rk[:, 0, :, :], other, own, ALU.is_gt))
            link(nc.vector.tensor_tensor(rk[:, 1, :, :], other, own, ALU.is_equal))
            v.wait_ge(tri_ready, 2)
            link(nc.vector.tensor_tensor(rk[:, 1, :, :], rk[:, 1, :, :], tri, ALU.mult))
            link(nc.vector.tensor_tensor(rk[:, 0, :, :], rk[:, 0, :, :], rk[:, 1, :, :], ALU.add))
            link(nc.vector.tensor_reduce(lg[:, 4, :], rk[:, 0, :, :], AX.X, ALU.add))
            link(nc.vector.tensor_scalar(lg[:, 5, :], lg[:, 4, :], float(TOPK), None, ALU.is_lt))
            link(nc.vector.tensor_tensor(lg[:, 4, :], lg[:, 5, :], lg[:, 3, :], ALU.mult))
            link(nc.vector.tensor_reduce(small[:, 52:53], lg[:, 4, :], AX.X, ALU.add))
            link(nc.vector.reciprocal(small[:, 53:54], small[:, 52:53]))
            link(nc.vector.tensor_scalar(probs[:, :], lg[:, 4, :], small[:, 53:54], None, ALU.mult))
            for g in range(2):
                nc.vector.memset(h3[g][:, FH:FP], 0.0).then_inc(padded, 1)

            def product(m, g, out_t, done):
                v.wait_ge(f_h1c, m + 1)
                v.wait_ge(f_h2, m + 1)
                nc.vector.tensor_tensor(out_t, h1c[g], h2p[g], ALU.mult).then_inc(done, 1)

            def weigh(m, g):
                v.wait_ge(f_silu, m)
                if not isinstance(m, int) or m >= 2:
                    v.wait_ge(f_t, m - 1)
                col = probs[:, m - 1:m] if isinstance(m, int) else probs[:, bass.ds(m - 1, 1)]
                nc.vector.tensor_scalar(h3[g][:, 0:FH], vv[g], col, None, ALU.mult).then_inc(f_h3, 1)

            def t_lo(m):
                v.wait_ge(f_thi, m + 1)
                nc.vector.tensor_tensor(hT[1].rearrange("p k t -> p (k t)"), tps[0][:, 0:FP],
                                        hT[0].rearrange("p k t -> p (k t)"), ALU.subtract).then_inc(f_tlo, 1)

            def step(n, g, first=False, last=False):
                if not first:
                    product(n - 1, 1 - g, vv[1 - g], f_v)
                    weigh(n - 1, 1 - g)
                if not last:
                    lo13(n + 1, 1 - g, 0)
                t_lo(n - 1)
                if not last:
                    lo13(n + 1, 1 - g, 1)

            lo13(1, 1, 0)
            lo13(1, 1, 1)
            v.wait_ge(padded, 2)
            product(0, 0, h3[0][:, 0:FH], f_h3)
            step(1, 1, first=True)
            step(2, 0)
            with v.Fori(0, NE // 2 - 2) as i:
                step(2 * i + 3, 1)
                step(2 * i + 4, 0)
            step(NE - 1, 1)
            step(NE, 0, last=True)
            product(NE, 0, vv[0], f_v)
            weigh(NE, 0)
            t_lo(NE)
            v.wait_ge(f_out, NE + 1)
            nc.vector.tensor_tensor(x[:, :], pvp[:, :], x[:, :], ALU.add).then_inc(res_ready, 1)

        @block.tensor
        def _(pe):
            def mm3(o, w, m, start, stop):
                nc.tensor.matmul(o, w[0], m[0], start=start, stop=False)
                nc.tensor.matmul(o, w[1], m[0], start=False, stop=False)
                return nc.tensor.matmul(o, w[0], m[1], start=False, stop=stop)

            def split(hl2, f):
                return [f(t) for t in hl2]

            def wait_item(q):
                pe.wait_ge(lo_done, q + 1)

            def ktile(t, k, lo_, hi_, n):
                return t[:, k * n + lo_:k * n + hi_]

            def evacuated(n):
                if n >= 2:
                    m = n - 2
                    if parts[m][0] == "K":
                        pe.wait_ge(k_out, k_before[m])
                    else:
                        pe.wait_ge(v_out, v_before[m])

            def part(n):
                kind, c, j = parts[n]
                slot, r = where[CTX_Q[c]]
                evacuated(n)
                wait_item(CTX_Q[c])
                if kind == "V":
                    wait_item(2)
                for k in range(KT):
                    if kind == "K":
                        w = split(wk_hl, lambda t: ktile(t, k, P * j, P * (j + 1), D))
                        m = split(slot, lambda t: ktile(t, k, 0, CH, CH))
                    else:
                        w = split(slot, lambda t: ktile(t, k, P * j, P * (j + 1), CH))
                        m = split(wv_hl, lambda t: ktile(t, k, 0, D, D))
                    last = mm3(proj[n % 2][:, :], w, m, k == 0, k == KT - 1)
                last.then_inc(proj_mm, 1)

            def x_transposes(n):
                pe.wait_ge(xq_ready, n + 1)
                o = misc[:, 0:256].bitcast(BF16)
                for k in range(KT):
                    last = nc.tensor.transpose(o[:, P * k:P * (k + 1)], xq[:, P * k:P * (k + 1)], identb[:, :])
                last.then_inc(xqT_mm, 1)

            def w_transposes(src, n, ready):
                pe.wait_ge(ready, 1)
                if n:
                    pe.wait_ge(wT_ready, 2 * n)
                for k2 in range(2):
                    o = tps[k2][:, :].bitcast(BF16)
                    for k in range(2):
                        for t in range(4):
                            last = nc.tensor.transpose(o[:, D * k + P * t:D * k + P * (t + 1)],
                                                       src[:, t, P * (2 * k2 + k):P * (2 * k2 + k + 1)], identb[:, :])
                    last.then_inc(wT_mm, 1)

            def row_of_scales(n):
                pe.wait_ge(diag, 4 * (n + 1))
                nc.tensor.matmul(misc[:, :], ones[:, :], dg[:, :, :].rearrange("p t n -> p (t n)"), start=True, stop=True).then_inc(sw_mm, 1)

            def integer_product(w, n):
                pe.wait_ge(sw_row, n + 1)
                pe.wait_ge(xqT_ready, n + 1)
                pe.wait_ge(wT_ready, 2 * (n + 1))
                for k in range(KT):
                    last = nc.tensor.matmul(misc[:, :], xqT[:, P * k:P * (k + 1)], w[:, k, :], start=(k == 0), stop=(k == KT - 1))
                last.then_inc(q_mm, 1)

            wait_item(0)
            for n in range(0, 8):
                part(n)
            pe.wait_ge(consts, 6)
            x_transposes(0)
            w_transposes(wq_int, 0, wq_q)
            for n in range(8, 12):
                part(n)
            pe.wait_ge(xqT_ready, 1)
            row_of_scales(0)
            w_transposes(wo_int, 1, wo_q)
            for n in range(12, 16):
                part(n)
                if n == 13:
                    integer_product(wqT, 0)
            pe.wait_ge(q_ready, 1)
            for k in range(4):
                last = nc.tensor.transpose(misc[:, P * k:P * (k + 1)], tmp[:, P * k:P * (k + 1)], ident[:, :])
            last.then_inc(qT_mm, 1)
            pe.wait_ge(k_out, 8)
            pe.wait_ge(qd_ready, 8)

            def scores(w):
                b, u = w // NPAIR, w % NPAIR
                if w:
                    pe.wait_ge(s_red, w)
                for c in range(2):
                    last = nc.tensor.matmul(sps[:, CH * c:CH * (c + 1)], qdv[:, b, u, :], kbuf[:, u // 2, CH * c:CH * (c + 1)],
                                            start=True, stop=True)
                last.then_inc(s_mm, 1)

            def p_transposes(w):
                pe.wait_ge(e_done, w + 1)
                for c in range(2):
                    if w:
                        pe.wait_ge((pt_a, pt_d)[c], w)
                    for t in range(4):
                        last = nc.tensor.transpose(tps[c][:, P * t:P * (t + 1)],
                                                   sbuf[:, w % 3, CH * c + P * t:CH * c + P * (t + 1)], ident[:, :])
                    last.then_inc(t_mm, 1)

            def values(w):
                b, u = w // NPAIR, w % NPAIR
                if w == NPAIR:
                    pe.wait_ge(o_done, 2)
                pe.wait_ge(pt_a, w + 1)
                pe.wait_ge(pt_d, w + 1)
                for t in range(8):
                    last = nc.tensor.matmul(pvp[:, 64 * u:64 * (u + 1)], ptbuf[:, w % 2, P * t:P * (t + 1)],
                                            vbuf[b][:, t, 64 * u:64 * (u + 1)], start=(t == 0), stop=(t == 7))
                last.then_inc(pv_mm, 1)

            pe.wait_ge(v_out, 8)
            pe.wait_ge(wT_ready, 4)
            nxt = 16
            for u in range(NPAIR):
                scores(u)
                part(nxt)
                nxt += 1
                if u >= 2:
                    p_transposes(u - 2)
                if u:
                    part(nxt)
                    nxt += 1
                if u >= 2:
                    values(u - 2)
            part(nxt)
            p_transposes(NPAIR - 2)
            values(NPAIR - 2)
            p_transposes(NPAIR - 1)
            pe.wait_ge(k_out, 16)
            pe.wait_ge(v_out, 16)
            for u in range(NPAIR):
                w = NPAIR + u
                scores(w)
                if u:
                    p_transposes(w - 1)
                if u != 1:
                    values(w - 2 if u else w - 1)
            p_transposes(2 * NPAIR - 1)
            row_of_scales(1)
            values(2 * NPAIR - 2)
            values(2 * NPAIR - 1)
            pe.wait_ge(sw_row, 2)
            x_transposes(1)
            integer_product(woT, 1)

            def y_transposes(n):
                pe.wait_ge(y_ready, n + 1)
                yv = y[:, :].rearrange("t (p k) -> t k p", k=KT)
                for k in range(KT):
                    last = nc.tensor.transpose(misc[:, P * k:P * (k + 1)], yv[:, k, :], ident[:, :])
                last.then_inc(yT_mm, 1)

            y_transposes(1)
            pe.wait_ge(yTl_r, 1)
            wait_item(WD_Q)
            for k in range(KT):
                last = mm3(proj[0][:, :], split(yT, lambda t: t[:, k, :]), split(where[WD_Q][0], lambda t: ktile(t, k, 0, D, D)),
                           k == 0, k == KT - 1)
            last.then_inc(down_mm, 1)
            for j in range(2):
                q = WKR_Q + j
                wait_item(q)
                for k in range(KT):
                    last = mm3(sps[:, 512 * j:512 * (j + 1)], split(yT, lambda t: t[:, k, :]),
                               split(where[q][0], lambda t: ktile(t, k, 0, D, D)), k == 0, k == KT - 1)
                last.then_inc(kr_mm, 1)
                if j == 0:
                    pe.wait_ge(down_r, 1)
                    for k in range(4):
                        last = nc.tensor.transpose(misc[:, P * k:P * (k + 1)], tmp[:, P * k:P * (k + 1)], ident[:, :])
                    last.then_inc(cT_mm, 1)
            pe.wait_ge(cTl_r, 1)
            wait_item(WKU_Q)
            for j in range(4):
                if j >= 2:
                    pe.wait_ge(up_out, j - 1)
                for h in range(4):
                    last = mm3(up_ps[j % 2][:, P * h:P * (h + 1)],
                               split(where[WKU_Q][0], lambda t: t[:, P * (4 * j + h):P * (4 * j + h + 1)]),
                               split(cT, lambda t: t[:, 0, :]), True, True)
                last.then_inc(up_mm, 1)
            wait_item(WVU_Q)
            for j in range(4):
                if j >= 2:
                    pe.wait_ge(vu_out, j - 1)
                last = mm3(proj[j % 2][:, :], split(cT, lambda t: t[:, 0, :]),
                           split(where[WVU_Q][0], lambda t: t[:, 512 * j:512 * (j + 1)]), True, True)
                last.then_inc(vu_mm, 1)
            pe.wait_ge(krn_r, 2)
            for j in range(2):
                q = WQR_Q + j
                wait_item(q)
                for k in range(QT):
                    last = mm3(sps[:, 512 * j:512 * (j + 1)], split(cT, lambda t: t[:, 1 + k, :]),
                               split(where[q][0], lambda t: ktile(t, k, 0, 512, 512)), k == 0, k == QT - 1)
                last.then_inc(qr_mm, 1)
            for j in range(4):
                q = WQU_Q + j
                wait_item(q)
                pe.wait_ge(up_out, j + 3)
                for h in range(4):
                    for k in range(QT):
                        last = mm3(up_ps[j % 2][:, P * h:P * (h + 1)], split(where[q][0], lambda t: ktile(t, k, P * h, P * (h + 1), 512)),
                                   split(cT, lambda t: t[:, 1 + k, :]), k == 0, k == QT - 1)
                last.then_inc(up_mm, 1)
                if j == 1:
                    pe.wait_ge(kr_roped, 1)
                    for i in range(2):
                        for t in range(4):
                            last = nc.tensor.transpose(tps[i][:, P * t:P * (t + 1)], krn[:, 512 * i + P * t:512 * i + P * (t + 1)], ident[:, :])
                        last.then_inc(krT_mm, 1)
            pe.wait_ge(qr_roped, 1)
            for i in range(2):
                pe.wait_ge(krT_r, i + 1)
                for t in range(4):
                    last = nc.tensor.transpose(tps[i][:, P * t:P * (t + 1)], qrn[:, 512 * i + P * t:512 * i + P * (t + 1)], ident[:, :])
                last.then_inc(qrT_mm, 1)
            pe.wait_ge(up_out, 8)
            pe.wait_ge(vu_out, 4)
            pe.wait_ge(qrT_r, 4)
            pe.wait_ge(qr_zero, 2)

            def latent_scores(g):
                if g >= 2:
                    pe.wait_ge(ms_sub, g - 1)
                for i in range(HG):
                    h = HG * g + i
                    o = sps[:, 512 * (g % 2) + P * i:512 * (g % 2) + P * (i + 1)]
                    nc.tensor.matmul(o, qT[:, h, :], kT[:, h, :], start=True, stop=False)
                    last = nc.tensor.matmul(o, qrT[h % 2][:, h // 2, :], krT[:, h // 2, :], start=False, stop=True)
                last.then_inc(ms_mm, 1)

            latent_scores(0)
            latent_scores(1)
            for g in range(4):
                pe.wait_ge(mp_r, g + 1)
                if g >= 2:
                    pe.wait_ge(mt_r, g - 1)
                for i in range(HG):
                    last = nc.tensor.transpose(tps[g % 2][:, P * i:P * (i + 1)], pg[g % 2][:, P * i:P * (i + 1)], ident[:, :])
                last.then_inc(mt_mm, 1)
                if g + 2 < 4:
                    latent_scores(g + 2)
                pe.wait_ge(mt_r, g + 1)
                if g >= 2:
                    pe.wait_ge(ma_b, g - 1)
                for i in range(HG):
                    last = nc.tensor.matmul(proj[g % 2][:, P * i:P * (i + 1)], vm[:, HG * g + i, :], ptg[g % 2][:, P * i:P * (i + 1)],
                                            start=True, stop=True)
                last.then_inc(ma_mm, 1)
            for g in range(4):
                q = WOM_Q + g
                wait_item(q)
                pe.wait_ge(ma_lo, g + 1)
                for i in range(HG):
                    h = HG * g + i
                    last = mm3(pvp[:, :], split(attnT, lambda t: t[:, h, :]), split(where[q][0], lambda t: ktile(t, i, 0, D, D)),
                               h == 0, h == H - 1)
                last.then_inc(wo_mm, 1)

            y_transposes(2)
            pe.wait_ge(yTl_r, 2)
            pe.wait_ge(yT32, 1)
            for k in range(KT):
                last = nc.tensor.matmul(misc[:, 0:NE], tmp[:, P * k:P * (k + 1)], gw[:, k, :], start=(k == 0), stop=(k == KT - 1))
            last.then_inc(gate_mm, 1)

            def up(n, g, half):
                if half == 0:
                    pe.wait_ge(f_lo13h, n + 1)
                else:
                    pe.wait_ge(f_lo13, n + 1)
                if not isinstance(n, int) or n >= 2:
                    pe.wait_ge(f_h1c if half == 0 else f_h3, n - 1)
                o = proj[g][:, 0:FH] if half == 0 else h2p[g]
                base = half * KT * FH
                for k in range(KT):
                    last = mm3(o, split(yT, lambda t: t[:, k, :]),
                               split(e13[g], lambda t: t[:, base + k * FH:base + (k + 1) * FH]), k == 0, k == KT - 1)
                last.then_inc(f_h1 if half == 0 else f_h2, 1)

            def h_transposes(m, g):
                pe.wait_ge(f_h3, m + 1)
                if not isinstance(m, int) or m >= 1:
                    pe.wait_ge(f_tlo, m)
                for t in range(FT):
                    last = nc.tensor.transpose(tps[0][:, P * t:P * (t + 1)], h3[g][:, P * t:P * (t + 1)], ident[:, :])
                last.then_inc(f_t, 1)

            def down(m, g, start=False, stop=False):
                pe.wait_ge(f_tlo, m + 1)
                pe.wait_ge(f_lo2, m + 1)
                for t in range(FT):
                    last = mm3(pvp[:, :], split(hT, lambda s: s[:, t, :]), split(e2[g], lambda s: s[:, D * t:D * (t + 1)]),
                               start and t == 0, stop and t == FT - 1)
                last.then_inc(f_out, 1)

            def step(n, g, start=False):
                up(n, g, 0)
                h_transposes(n - 1, 1 - g)
                up(n, g, 1)
                down(n - 1, 1 - g, start=start)

            up(0, 0, 0)
            up(0, 0, 1)
            step(1, 1, start=True)
            step(2, 0)
            with pe.Fori(0, NE // 2 - 2) as i:
                step(2 * i + 3, 1)
                step(2 * i + 4, 0)
            step(NE - 1, 1)
            step(NE, 0)
            h_transposes(NE, 0)
            down(NE, 0, stop=True)


def perceiver_block(nc, inputs, out):
    build(nc, inputs, out)


def kernel(**inputs):
    import numpy as _np
    import concourse.bacc as _bacc
    from concourse import mybir as _mybir
    from concourse.bass_utils import run_bass_kernel_spmd as _run

    g = {k: _np.asarray(v) for k, v in inputs.items()}
    f = _np.ascontiguousarray

    def tiles(w, k, j):
        n = w.shape[1] // j
        return f(w.reshape(k, 128, j, n).transpose(2, 1, 0, 3)).reshape(j, 128, k * n)

    def halves(w):
        return f(w.reshape(128, 4, 2, 512).transpose(2, 0, 1, 3)).reshape(2, 128, 2048)

    freq = (1.0 / 10000.0 ** (_np.arange(0, 64, 2, dtype=_np.float32) / _np.float32(64))).astype(_np.float32)
    ang = (_np.arange(128) % 64).astype(_np.float32)[:, None] * freq
    cos, sin = _np.cos(ang), _np.sin(ang)
    tables = f(_np.stack([_np.concatenate([cos, cos], 1), _np.concatenate([-sin, sin], 1)], 1).astype(_np.float32))

    arrays = {
        "x": f(g["x"].reshape(128, 512)),
        "mask": f(g["mask_BxSxS2_ff0"].reshape(128, 1024)),
        "ctx": f(g["ctx_2048"].reshape(4, 512, 512).transpose(0, 2, 1)).reshape(4, 128, 2048),
        "wk": f(g["L0_xattn_wk"].T).reshape(128, 2048),
        "wv": f(g["L0_xattn_wv"].T).reshape(128, 2048),
        "wq": f(g["L0_xattn_wq"].reshape(4, 128, 512).transpose(1, 0, 2)),
        "wo": f(g["L0_xattn_wo"].reshape(4, 128, 512).transpose(1, 0, 2)),
        "bq": g["L0_xattn_bq"], "bv": g["L0_xattn_bv"], "bo": g["L0_xattn_bo"],
        "bkT": f(g["L0_xattn_bk"].reshape(4, 128).T),
        "wd": f(_np.concatenate([g["L0_attn_Wkd"], g["L0_attn_Wqd"]], 0).T).reshape(128, 2048),
        "bd": f(_np.concatenate([g["L0_attn_bkd"], g["L0_attn_bqd"]], 0)),
        "wkr": halves(g["L0_attn_Wkr"].T),
        "wku": f(g["L0_attn_Wku"].T), "wvu": f(g["L0_attn_Wvu"].T),
        "wqr": tiles(g["L0_attn_Wqr"].T, 3, 2),
        "wqu": tiles(g["L0_attn_Wqu"].T, 3, 4),
        "wom": f(g["L0_attn_Wo"].T.reshape(4, 4, 128, 512).transpose(0, 2, 1, 3)).reshape(4, 128, 2048),
        "bkr": g["L0_attn_bkr"], "bqr": g["L0_attn_bqr"], "bom": g["L0_attn_bo"],
        "hbias": f(_np.stack([g["L0_attn_" + n].reshape(16, 128).T for n in ("bku", "bqu", "bvu")], 1)),
        "rope": tables,
        "gw": f(g["L0_ffn_gate_w"].T).reshape(128, 4, 16),
        "gb": g["L0_ffn_gate_b"],
        "w1s": g["L0_ffn_w1_shared"], "w2s": g["L0_ffn_w2_shared"], "w3s": g["L0_ffn_w3_shared"],
        "w1r": g["L0_ffn_w1_routed"], "w2r": g["L0_ffn_w2_routed"], "w3r": g["L0_ffn_w3_routed"],
    }
    nc = _bacc.Bacc("TRN2", target_bir_lowering=False, num_devices=1)
    feeds, aps = {}, {}
    for name, v in arrays.items():
        v = f(v)
        feeds[f"in_{name}"] = v
        aps[name] = nc.dram_tensor(f"in_{name}", v.shape, _mybir.dt.from_np(v.dtype), kind="ExternalInput").ap()
    out = nc.dram_tensor("out", (128, 512), _mybir.dt.float32, kind="ExternalOutput").ap()
    perceiver_block(nc, aps, out)
    r = _run(nc, [feeds], core_ids=[0])
    return r.results[0]["out"].reshape(2, 64, 512)
```

```python
from contextlib import ExitStack

import concourse.bass as bass
from concourse import mybir

F32 = mybir.dt.float32
F32R = mybir.dt.float32r
BF16 = mybir.dt.bfloat16
ALU = mybir.AluOpType
ACT = mybir.ActivationFunctionType
AX = mybir.AxisListType

P = 128
B, S, D = 2, 64, 512
KEYS = 1024
KT = D // P
XH, XD = 16, 32
NPAIR = XH // 2
H, DH, DR = 16, 128, 64
DQ = 384
QT = DQ // P
HG = 4
NE, TOPK, FH = 16, 4, 352
FT = 3
FP = FT * P
CH = 512
ITEM = 2048
RAW = 3
ERAW = 4
QMAX, QEPS = 127.0, 1e-8
ROUND = 1.5 * 2.0 ** 23
NEG = -1e30
X_SCALE = XD ** -0.5
M_SCALE = (DH + DR) ** -0.5
W13 = 2 * KT * FH
W2 = FT * D


def build(nc, a, out):
    ctx = ExitStack()
    with ctx:
        def sb(name, shape, dt=F32):
            return ctx.enter_context(nc.sbuf_tensor(name, shape, dt))

        def sem(name):
            return ctx.enter_context(nc.semaphore(name))

        raw = sb("raw", [P, RAW, ITEM])
        area = sb("area", [P, 17408])
        hl = sb("hl", [P, 2 * (W13 + W2) * 2], F32R)
        kbuf = area[:, 0:4096].rearrange("p (g k) -> p g k", g=4)
        vbuf = [area[:, 4096 * (1 + b):4096 * (2 + b)].rearrange("p (t n) -> p t n", t=8) for b in range(B)]
        sbuf = area[:, 12288:15360].rearrange("p (r k) -> p r k", r=3)
        ptbuf = area[:, 15360:17408].rearrange("p (r k) -> p r k", r=2)
        wq_raw = area[:, 12288:14336].rearrange("p (t n) -> p t n", t=4)
        wo_raw = area[:, 14336:16384].rearrange("p (t n) -> p t n", t=4)
        wq_int = area[:, 8192:9216].bitcast(BF16).rearrange("p (t n) -> p t n", t=4)
        wo_int = area[:, 9216:10240].bitcast(BF16).rearrange("p (t n) -> p t n", t=4)
        EW = W13 + W2
        raws = raw[:, :, :].rearrange("p r n -> p (r n)")
        slots = [area[:, EW * i:EW * (i + 1)] for i in range(3)] + [raws[:, 0:EW]]
        eraw13 = [t[:, 0:W13] for t in slots]
        eraw2 = [t[:, W13:EW] for t in slots]
        qT = area[:, 9216:11264].rearrange("p (h t) -> p h t", h=H)
        kT = area[:, 11264:13312].rearrange("p (h t) -> p h t", h=H)
        vm = area[:, 13312:15360].rearrange("p (h d) -> p h d", h=H)
        krn = area[:, 15360:16384]
        qrn = area[:, 16384:17408]

        def pair(base):
            return [hl[:, base:base + ITEM], hl[:, base + ITEM:base + 2 * ITEM]]
        wk_hl, wv_hl = pair(0), pair(2 * ITEM)
        ring_hl = [pair((4 + 2 * r) * ITEM) for r in range(2)]
        attnT = [t.rearrange("p (h t) -> p h t", h=H) for t in wk_hl]
        e13 = [[hl[:, (2 * g + s) * (W13 + W2):(2 * g + s) * (W13 + W2) + W13] for s in range(2)] for g in range(2)]
        e2 = [[hl[:, (2 * g + s) * (W13 + W2) + W13:(2 * g + s + 1) * (W13 + W2)] for s in range(2)] for g in range(2)]

        x = sb("x", [P, D])
        y = sb("y", [P, D])
        tmp = sb("tmp", [P, D])
        ob = sb("ob", [P, D])
        yT = [sb("yTh", [P, KT, P], F32R), sb("yTl", [P, KT, P], F32R)]
        cT = [sb("cTh", [P, KT, P], F32R), sb("cTl", [P, KT, P], F32R)]
        mask = sb("mask", [P, KEYS])
        qd = sb("qd", [P, 2048])
        qdv = qd[:, :].rearrange("p (b j q) -> p b j q", b=B, j=NPAIR)
        krT = qd[:, 0:1024].rearrange("p (j t) -> p j t", j=8)
        qrT = [qd[:, 1024:2048].rearrange("p (j t) -> p j t", j=8), qrn.rearrange("p (j t) -> p j t", j=8)]
        wint = sb("wint", [P, 2048])
        wqT = wint[:, 0:1024].bitcast(BF16).rearrange("p (k n) -> p k n", k=KT)
        woT = wint[:, 1024:2048].bitcast(BF16).rearrange("p (k n) -> p k n", k=KT)
        brope = wint
        bias_a = sb("bias_a", [P, D])
        bias_b = sb("bias_b", [P, D])
        swrow = sb("swrow", [P, D])
        rope = sb("rope", [P, 2, DR])
        ident = sb("ident", [P, P])
        identb = sb("identb", [P, P], BF16)
        cmask = sb("cmask", [P, P])
        ones = sb("ones", [P, P])
        bkT = sb("bkT", [P, 4])
        hbias = sb("hbias", [P, 3, H])
        gw = sb("gw", [P, KT, NE])
        gb = sb("gb", [P, NE])
        tri = area[:, 13824:13824 + NE * NE].rearrange("p (e f) -> p e f", e=NE)
        rk = area[:, 13312:13312 + 2 * NE * NE].rearrange("p (a e f) -> p a e f", a=2, e=NE)
        lg = sb("lg", [P, 6, NE])
        probs = sb("probs", [P, NE])
        small = sb("small", [P, 64])
        rsum = sb("rsum", [P, 32])
        nmax = sb("nmax", [P, 32])
        st = sb("st", [P, 8])
        mv = sb("mv", [P, 2])
        power = sb("power", [P, 1])

        mst = swrow[:, 0:48]
        xq = sb("xq", [P, D], BF16)
        xqT = sb("xqT", [P, D], BF16)
        dg = y[:, :].rearrange("p (t n) -> p t n", t=4)
        pg = [mask[:, 0:512], mask[:, 512:1024], tmp[:, :], ob[:, :]]
        ptg = [y[:, :], wint[:, 0:512]]
        stage = [y[:, :], ob[:, :]]

        h1c = [tmp[:, 0:FH], ob[:, 0:FH]]
        vv = [mask[:, 0:FH], mask[:, 512:512 + FH]]
        h3 = [qd[:, 0:FP], qd[:, 512:512 + FP]]
        hT = [t[:, 0:FT, :] for t in cT]

        proj = [ctx.enter_context(nc.psum_tensor(f"proj{i}", [P, 512], F32)) for i in range(2)]
        sps = ctx.enter_context(nc.psum_tensor("sps", [P, 1024], F32))
        tps = [ctx.enter_context(nc.psum_tensor(f"tps{i}", [P, 512], F32)) for i in range(2)]
        pvp = ctx.enter_context(nc.psum_tensor("pvp", [P, 512], F32))
        misc = ctx.enter_context(nc.psum_tensor("misc", [P, 512], F32))

        up_ps = [misc[:, :], pvp[:, :]]
        sgp = [sps[:, 0:512], sps[:, 512:1024], tps[0][:, :], tps[1][:, :]]
        ptp = [misc[:, :], pvp[:, :]]
        qrtp = [misc, pvp]
        wop = tps[0]
        h2p = [sps[:, 0:FH], sps[:, 512:512 + FH]]

        raw_in = [sem(f"raw_in{i}") for i in range(RAW)]
        hi_done, lo_done = sem("hi_done"), sem("lo_done")
        x_second, bk_in, qrn_r, ropeq_step, f_lo13h = sem("x_second"), sem("bk_in"), sem("qrn_ready"), sem("rope_q_step"), sem("f_lo13_half")
        x_in, wq_in, wo_in, small_in, mask_in = sem("x_in"), sem("wq_in"), sem("wo_in"), sem("small_in"), sem("mask_in")
        bq_in, bv_in, brope_in = sem("bq_in"), sem("bv_in"), sem("brope_in")
        bo_in, bd_in, bom_in, mask1_in = sem("bo_in"), sem("bd_in"), sem("bom_in"), sem("mask1_in")
        consts = sem("consts")
        dve = sem("dve_step")
        ropek_step, up_nat, up_t = sem("rope_k_step"), sem("up_staged"), sem("up_t_mm")
        first_in = [sem(f"first_in{i}") for i in range(2)]
        hi_first, lo_first = sem("hi_first"), sem("lo_first")
        stats, vareps, rstd = sem("ln_stats"), sem("ln_var_eps"), sem("ln_rstd")
        swq_ready, wq_q, wo_q = sem("sw_ready"), sem("wq_quantised"), sem("wo_quantised")
        xq_ready, xqT_mm, xqT_ready = sem("xq_ready"), sem("xqT_mm"), sem("xqT_ready")
        wT_mm, wT_ready = sem("wT_mm"), sem("wT_ready")
        sw_mm, sw_row, diag = sem("sw_mm"), sem("sw_row"), sem("diag_ready")
        q_mm, q_ready, qT_mm, qd_ready = sem("q_mm"), sem("q_ready"), sem("qT_mm"), sem("qd_ready")
        proj_mm, k_out, v_out = sem("proj_mm"), sem("k_out"), sem("v_out")
        s_mm, s_red, nm_ready, e_done = sem("scores_mm"), sem("scores_reduced"), sem("neg_max"), sem("exp_done")
        t_mm, pt_a, pt_d, pv_mm, o_done = sem("t_mm"), sem("pt_act"), sem("pt_dve"), sem("pv_mm"), sem("o_done")
        y_ready, yT_mm, yTh_r, yTl_r = sem("y_ready"), sem("yT_mm"), sem("yTh_ready"), sem("yTl_ready")
        down_mm, down_r, cT_mm, cTh_r, cTl_r = sem("down_mm"), sem("down_ready"), sem("cT_mm"), sem("cTh_ready"), sem("cTl_ready")
        kr_mm, krn_r, kr_roped, krT_mm, krT_r = sem("kr_mm"), sem("krn_ready"), sem("kr_roped"), sem("krT_mm"), sem("krT_ready")
        qr_mm, qr_roped, qrT_mm, qrT_r = sem("qr_mm"), sem("qr_roped"), sem("qrT_mm"), sem("qrT_ready")
        up_mm, up_out, vu_mm, vu_out = sem("up_mm"), sem("up_out"), sem("vu_mm"), sem("vu_out")
        ms_mm, mmax, mneg, me_done, mp_r = sem("mla_scores_mm"), sem("mla_max"), sem("mla_neg_max"), sem("mla_exp"), sem("mla_probs")
        qr_zero2 = sem("qr_zero_odd")
        mt_mm, mt_r, ma_mm, ma_hi, ma_lo = sem("mla_pT_mm"), sem("mla_pT"), sem("mla_attn_mm"), sem("mla_attn_hi"), sem("mla_attn_lo")
        wo_mm = sem("wo_mm")
        yT32, gate_mm, gate_e, padded = sem("yT_f32"), sem("gate_mm"), sem("gate_exp"), sem("h3_padded")
        pad_ready, tri_ready, qr_zero = sem("pad_ready"), sem("tri_ready"), sem("qr_zero")
        e13_in = [sem(f"e13_in{g}") for g in range(ERAW)]
        e2_in = [sem(f"e2_in{g}") for g in range(ERAW)]
        f_hi13, f_lo13, f_hi2, f_lo2 = sem("f_hi13"), sem("f_lo13"), sem("f_hi2"), sem("f_lo2")
        f_h1, f_h2, f_h1c, f_v, f_silu, f_h3 = sem("f_h1_mm"), sem("f_h2_mm"), sem("f_h1_copied"), sem("f_product"), sem("f_silu"), sem("f_h3")
        f_t, f_thi, f_tlo, f_out = sem("f_t_mm"), sem("f_t_hi"), sem("f_t_lo"), sem("f_out_mm")
        res_ready, out_done = sem("result_ready"), sem("out_done")

        stream = [(a["wk"], ITEM), (a["ctx"][0], ITEM), (a["wv"], ITEM)] + [(a["ctx"][c], ITEM) for c in (1, 2, 3)]
        N_X = len(stream)
        stream += [(a["wd"], ITEM)] + [(a["wkr"][j], ITEM) for j in range(2)] + [(a["wku"], ITEM)]
        stream = stream[:-1] + [(a["wqr"][j], QT * 512) for j in range(2)] + [(a["wku"], ITEM), (a["wvu"], ITEM)]
        stream += [(a["wqu"][j], QT * 512) for j in range(4)] + [(a["wom"][j], ITEM) for j in range(4)]
        place = [wk_hl, wv_hl] + ring_hl
        order = [0, 2, 1, 3, 2, 3] + [1, 2, 0, 3, 1, 2, 0, 3, 1, 2, 3, 1, 2, 3, 1]
        where = [place[i] for i in order]
        CTX_Q = [1, 3, 4, 5]
        WD_Q, WKR_Q, WQR_Q, WKU_Q, WVU_Q, WQU_Q, WOM_Q = 6, 7, 9, 11, 12, 13, 17

        parts = []
        for c in range(2):
            parts += [("K", c, g) for g in range(4)] + [("V", c, t) for t in range(4)]
        for u in range(NPAIR):
            parts.append(("V", 2 + u // 4, u % 4))
            if u:
                parts.append(("K", 2 + (u - 1) % 2, (u - 1) // 2))
        parts.append(("K", 3, 3))
        k_before = [sum(p[0] == "K" for p in parts[:n + 1]) for n in range(len(parts))]
        v_before = [sum(p[0] == "V" for p in parts[:n + 1]) for n in range(len(parts))]
        last_k = max(n for n, p in enumerate(parts) if p[0] == "K") + 1
        last_v = max(n for n, p in enumerate(parts) if p[0] == "V") + 1
        last_c = [max(n for n, p in enumerate(parts) if p[1] == c) + 1 for c in range(4)]
        freed = [(proj_mm, n) for n in (last_k, last_c[0], last_v, last_c[1], last_c[2], last_c[3])]
        freed += [(down_mm, 1), (kr_mm, 1), (kr_mm, 2), (qr_mm, 1), (qr_mm, 2), (up_mm, 4), (vu_mm, 4)]
        freed += [(up_mm, 5 + j) for j in range(4)] + [(wo_mm, j + 1) for j in range(4)]

        block = ctx.enter_context(nc.Block())


        def rows(v):
            return v.partition_broadcast(P)

        def e_of(w, e):
            return w[e] if isinstance(e, int) else w[bass.ds(e, 1)].rearrange("e d n -> (e d) n")

        @block.sync
        def _(sp):
            def item(q):
                if q >= RAW:
                    sp.wait_ge(lo_done, q - RAW + 1)
                sp.dma_start(raw[:, q % RAW, 0:stream[q][1]], stream[q][0]).then_inc(raw_in[q % RAW], 16)

            def expert(s, w1, w3, w2):
                sp.dma_start(eraw13[s][:, 0:KT * FH], w1.rearrange("(p k) n -> p (k n)", k=KT)).then_inc(e13_in[s], 16)
                sp.dma_start(eraw13[s][:, KT * FH:W13], w3.rearrange("(p k) n -> p (k n)", k=KT)).then_inc(e13_in[s], 16)
                sp.dma_start(eraw2[s][:, 0:2 * D].rearrange("p (t n) -> p t n", t=2),
                             w2[0:2 * P, :].rearrange("(t p) n -> p t n", p=P)).then_inc(e2_in[s], 16)
                sp.dma_start(eraw2[s][0:FH - 2 * P, 2 * D:3 * D], w2[2 * P:FH, :]).then_inc(e2_in[s], 16)

            def routed(s, n):
                sp.wait_ge(f_lo13, n - ERAW + 1)
                sp.wait_ge(f_lo2, n - ERAW + 1)
                expert(s, *(e_of(a[w], n - 1) for w in ("w1r", "w3r", "w2r")))

            for h in range(2):
                for q in range(2):
                    c = slice(h * ITEM // 2, (h + 1) * ITEM // 2)
                    sp.dma_start(raw[:, q, c], stream[q][0][:, c]).then_inc((first_in, raw_in)[h][q], 16)
                if h == 0:
                    sp.dma_start(x[:, :], a["x"]).then_inc(x_in, 16)
            item(2)
            sp.dma_start(bkT[:, :], a["bkT"]).then_inc(bk_in, 16)
            sp.dma_start(wq_raw, a["wq"]).then_inc(wq_in, 16)
            item(3)
            sp.dma_start(bias_a[:, :], rows(a["bq"])).then_inc(bq_in, 16)
            sp.dma_start(wo_raw, a["wo"]).then_inc(wo_in, 16)
            item(4)
            sp.dma_start(mask[0:S, :], a["mask"][0:S, :]).then_inc(mask_in, 16)
            sp.dma_start(mask[S:P, :], a["mask"][0:S, :]).then_inc(mask_in, 16)
            item(5)
            sp.dma_start(bias_b[:, :], rows(a["bv"])).then_inc(bv_in, 16)
            sp.dma_start(hbias[:, :, :], a["hbias"]).then_inc(small_in, 16)
            sp.dma_start(gw[:, :, :], a["gw"]).then_inc(small_in, 16)
            sp.dma_start(gb[:, :], rows(a["gb"])).then_inc(small_in, 16)
            sp.dma_start(rope[:, :, :], a["rope"]).then_inc(small_in, 16)
            for q in range(6, 13):
                item(q)
            sp.wait_ge(pad_ready, 2)
            expert(0, a["w1s"], a["w3s"], a["w2s"])
            item(13)
            item(14)
            item(15)
            expert(1, a["w1r"][0], a["w3r"][0], a["w2r"][0])
            for q in range(16, len(stream)):
                item(q)
            sp.wait_ge(pad_ready, 3)
            expert(2, a["w1r"][1], a["w3r"][1], a["w2r"][1])
            sp.wait_ge(pad_ready, 4)
            expert(3, a["w1r"][2], a["w3r"][2], a["w2r"][2])
            with sp.Fori(0, (NE - ERAW) // 4) as i:
                for j in range(4):
                    routed(j, 4 * i + 4 + j)
            routed(0, NE)
            sp.wait_ge(res_ready, 1)
            sp.dma_start(out, x[:, :]).then_inc(out_done, 16)
            sp.wait_ge(out_done, 16)

        def rotate(nceng, eng, t, b, step, base, done):
            tv = t.rearrange("p (h r) -> p h r", h=H)
            bv = b.rearrange("p (h r) -> p h r", h=H)
            half = DR // 2
            nceng.tensor_tensor(bv[:, :, 0:half], tv[:, :, half:DR],
                                rope[:, 1:2, 0:half].to_broadcast([P, H, half]), ALU.mult).then_inc(step, 1)
            nceng.tensor_tensor(bv[:, :, half:DR], tv[:, :, 0:half],
                                rope[:, 1:2, half:DR].to_broadcast([P, H, half]), ALU.mult).then_inc(step, 1)
            eng.wait_ge(step, base + 2)
            nceng.tensor_tensor(tv, tv, rope[:, 0:1, :].to_broadcast([P, H, DR]), ALU.mult).then_inc(step, 1)
            eng.wait_ge(step, base + 3)
            nceng.tensor_tensor(t, t, b, ALU.add).then_inc(done, 1)

        @block.gpsimd
        def _(gp):
            def inverse_deviation(n):
                gp.wait_ge(stats, n + 1)
                nc.gpsimd.tensor_scalar(small[:, 60:61], mv[:, 1:2], 1e-5, None, ALU.add).then_inc(vareps, 1)
                gp.wait_ge(vareps, n + 1)
                nc.gpsimd.tensor_tensor(small[:, 61:62], small[:, 60:61], power[:, :], ALU.pow).then_inc(rstd, 1)

            nc.gpsimd.memset(power[:, :], -0.5).then_inc(consts, 1)
            nc.gpsimd.memset(identb[:, :], 0.0).then_inc(consts, 1)
            nc.gpsimd.memset(ident[:, :], 0.0).then_inc(consts, 1)
            nc.gpsimd.memset(ones[:, :], 1.0).then_inc(consts, 1)
            gp.wait_ge(consts, 4)
            for m in (identb, ident):
                gp.affine_select(out=m[:, :], in_=m[:, :], compare_op=ALU.not_equal, fill=1.0, base=0,
                                 pattern=[[-1, P]], channel_multiplier=1).then_inc(consts, 1)
            inverse_deviation(0)
            nc.gpsimd.memset(qd[:, :], 0.0).then_inc(consts, 1)
            nc.gpsimd.memset(cmask[:, :], 0.0).then_inc(consts, 1)
            gp.wait_ge(consts, 8)
            gp.affine_select(out=cmask[:, :], in_=cmask[:, :], compare_op=ALU.is_ge, fill=NEG, base=0,
                             pattern=[[-1, P]], channel_multiplier=1).then_inc(consts, 1)
            gp.wait_ge(consts, 9)
            nc.gpsimd.memset(cmask[S:P, 0:S], NEG).then_inc(consts, 1)
            gp.wait_ge(consts, 10)
            gp.wait_ge(q_ready, 1)
            gp.dma_start(bias_a[:, :], rows(a["bo"])).then_inc(bo_in, 16)
            gp.wait_ge(s_red, NPAIR)
            gp.dma_start(mask[0:S, :], a["mask"][S:P, :]).then_inc(mask1_in, 16)
            gp.dma_start(mask[S:P, :], a["mask"][S:P, :]).then_inc(mask1_in, 16)
            gp.wait_ge(pv_mm, 2 * NPAIR)
            for i in range(2):
                nc.gpsimd.memset(eraw2[i][96:P, 2 * D:3 * D], 0.0).then_inc(pad_ready, 1)
            gp.wait_ge(pad_ready, 2)
            gp.wait_ge(xq_ready, 2)
            gp.dma_start(bias_b[:, :], rows(a["bd"])).then_inc(bd_in, 16)
            gp.wait_ge(q_mm, 2)
            gp.dma_start(brope[:, 0:1024], rows(a["bkr"])).then_inc(brope_in, 16)
            gp.dma_start(brope[:, 1024:2048], rows(a["bqr"])).then_inc(brope_in, 16)
            inverse_deviation(1)
            gp.wait_ge(x_second, 1)
            gp.dma_start(bias_a[:, :], rows(a["bom"])).then_inc(bom_in, 16)
            gp.wait_ge(krn_r, 2)
            gp.wait_ge(small_in, 64)
            gp.wait_ge(s_mm, 2 * NPAIR)
            rotate(nc.gpsimd, gp, krn, qd[:, 0:1024], ropek_step, 0, kr_roped)
            gp.wait_ge(qrn_r, 2)
            rotate(nc.gpsimd, gp, qrn, qd[:, 1024:2048], ropeq_step, 0, qr_roped)
            gp.wait_ge(qr_roped, 1)
            nc.gpsimd.memset(qd[DR:P, 1024:2048], 0.0).then_inc(qr_zero, 1)
            gp.wait_ge(qr_zero, 1)
            gp.wait_ge(ms_mm, 4)
            nc.gpsimd.memset(eraw2[2][96:P, 2 * D:3 * D], 0.0).then_inc(pad_ready, 1)
            gp.wait_ge(ma_mm, 4)
            gp.wait_ge(pad_ready, 3)
            nc.gpsimd.memset(tri, 1.0).then_inc(tri_ready, 1)
            gp.wait_ge(tri_ready, 1)
            gp.affine_select(out=tri, in_=tri, compare_op=ALU.is_gt, fill=0.0, base=0,
                             pattern=[[1, NE], [-1, NE]], channel_multiplier=0).then_inc(tri_ready, 1)
            gp.wait_ge(lo_done, len(stream))
            gp.wait_ge(tri_ready, 2)
            nc.gpsimd.memset(eraw2[3][96:P, 2 * D:3 * D], 0.0).then_inc(pad_ready, 1)
            gp.wait_ge(pad_ready, 4)
            inverse_deviation(2)

            def lo2(n, g, s):
                gp.wait_ge(f_hi2, n + 1)
                nc.gpsimd.tensor_tensor(e2[g][1], eraw2[s], e2[g][0], ALU.subtract).then_inc(f_lo2, 1)

            for n in range(3):
                lo2(n, n % 2, n % ERAW)
            with gp.Fori(0, (NE - 4) // 4) as i:
                for j in range(4):
                    lo2(4 * i + 3 + j, (3 + j) % 2, (3 + j) % ERAW)
            for n in (NE - 1, NE):
                lo2(n, n % 2, n % ERAW)

        @block.scalar
        def _(act):
            def copy(o, i):
                return nc.scalar.activation(o, i, ACT.Copy)

            def slot_free(q):
                before = [p for p in range(q) if order[p] == order[q]]
                if before:
                    act.wait_ge(*freed[before[-1]])

            def hi(q):
                w = stream[q][1]
                act.wait_ge(raw_in[q % RAW], 16 * (q // RAW + 1))
                slot_free(q)
                copy(where[q][0][:, 0:w], raw[:, q % RAW, 0:w]).then_inc(hi_done, 1)

            def k_evac(n):
                _, c, g = parts[n]
                act.wait_ge(proj_mm, n + 1)
                nc.scalar.activation(kbuf[:, g, (c % 2) * CH:(c % 2 + 1) * CH], proj[n % 2][:, :], ACT.Identity,
                                     bias=bkT[:, g:g + 1]).then_inc(k_out, 1)

            ks = [n for n, p in enumerate(parts) if p[0] == "K"]
            for h in range(2):
                for q in range(2):
                    c = slice(h * ITEM // 2, (h + 1) * ITEM // 2)
                    act.wait_ge((first_in, raw_in)[h][q], 16)
                    copy(where[q][0][:, c], raw[:, q, c]).then_inc((hi_first, hi_done)[h], 1)
            hi(2)
            hi(3)
            act.wait_ge(bk_in, 16)
            for n in ks[0:4]:
                k_evac(n)

            def wT_evac(dst, n):
                for k2 in range(2):
                    act.wait_ge(wT_mm, 2 * n + k2 + 1)
                    copy(dst[:, 2 * k2:2 * k2 + 2, :].rearrange("p k n -> p (k n)"), tps[k2][:, :].bitcast(BF16)).then_inc(wT_ready, 1)

            hi(4)
            for n in ks[4:8]:
                k_evac(n)
            wT_evac(wqT, 0)
            hi(5)
            wT_evac(woT, 1)

            def exp_pair(w):
                act.wait_ge(nm_ready, w + 1)
                s = sbuf[:, w % 3, :]
                nc.scalar.activation(s, s, ACT.Exp, bias=nmax[:, 16 + w:17 + w], accum_out=rsum[:, w:w + 1]).then_inc(e_done, 1)

            def pt_evac(w):
                act.wait_ge(t_mm, 2 * w + 1)
                if w >= 2:
                    act.wait_ge(pv_mm, w - 1)
                copy(ptbuf[:, w % 2, 0:512], tps[0][:, :]).then_inc(pt_a, 1)

            kq = list(ks[8:])
            for u in range(NPAIR):
                exp_pair(u)
                if u >= 2:
                    pt_evac(u - 2)
                if u:
                    k_evac(kq.pop(0))
            k_evac(kq.pop(0))
            pt_evac(NPAIR - 2)
            pt_evac(NPAIR - 1)
            for u in range(NPAIR):
                w = NPAIR + u
                exp_pair(w)
                if u >= 1:
                    pt_evac(w - 1)
                if u in (1, 3, 5, 6):
                    hi(6 + (1, 3, 5, 6).index(u))
            pt_evac(2 * NPAIR - 1)

            def yT_hi(n):
                act.wait_ge(yT_mm, n)
                copy(yT[0][:, :, :].rearrange("p k t -> p (k t)"), misc[:, :]).then_inc(yTh_r, 1)

            yT_hi(1)
            act.wait_ge(cT_mm, 1)
            copy(cT[0][:, :, :].rearrange("p k t -> p (k t)"), misc[:, :]).then_inc(cTh_r, 1)
            hi(10)
            hi(11)
            hi(12)

            def up_stage(n):
                act.wait_ge(up_mm, n + 1)
                if n >= 2:
                    act.wait_ge(up_t, n - 1)
                copy(stage[n % 2], up_ps[n % 2]).then_inc(up_nat, 1)

            for j in range(4):
                up_stage(j)
            hi(13)
            for j in range(4):
                act.wait_ge(vu_mm, j + 1)
                copy(vm[:, 4 * j:4 * j + 4, :].rearrange("p h d -> p (h d)"), proj[j % 2][:, :]).then_inc(vu_out, 1)
                if j == 1:
                    hi(14)
            hi(15)
            hi(16)
            up_stage(4)
            hi(17)
            up_stage(5)
            hi(18)
            up_stage(6)
            hi(19)
            up_stage(7)
            for j in range(2):
                act.wait_ge(krT_mm, j + 1)
                copy(krT[:, 4 * j:4 * j + 4, :].rearrange("p j t -> p (j t)"), proj[j][:, :]).then_inc(krT_r, 1)
            act.wait_ge(qrT_mm, 2)
            act.wait_ge(qr_zero, 1)
            for j in range(2):
                for e in range(2):
                    rr = slice(DR * e, DR * (e + 1))
                    copy(qrT[e][rr, 4 * j:4 * j + 4, :].rearrange("p j t -> p (j t)"), qrtp[j][rr, :]).then_inc(qrT_r, 1)

            def latent_exp(g):
                act.wait_ge(mneg, g + 1)
                for i in range(HG):
                    t = pg[g][:, P * i:P * (i + 1)]
                    nc.scalar.activation(t, t, ACT.Exp, bias=mst[:, 16 + HG * g + i:17 + HG * g + i], scale=M_SCALE,
                                         accum_out=mst[:, 32 + HG * g + i:33 + HG * g + i]).then_inc(me_done, 1)

            def latent_pT(g):
                act.wait_ge(mt_mm, g + 1)
                if g >= 2:
                    act.wait_ge(ma_mm, g - 1)
                copy(ptg[g % 2], ptp[g % 2]).then_inc(mt_r, 1)

            def attn_hi(g):
                act.wait_ge(ma_mm, g + 1)
                for i in range(HG):
                    h = HG * g + i
                    nc.scalar.activation(attnT[0][:, h, :], proj[g % 2][:, P * i:P * (i + 1)], ACT.Identity,
                                         bias=hbias[:, 2, h:h + 1]).then_inc(ma_hi, 1)

            latent_exp(0)
            latent_exp(1)
            latent_pT(0)
            latent_exp(2)
            attn_hi(0)
            latent_pT(1)
            latent_exp(3)
            attn_hi(1)
            latent_pT(2)
            attn_hi(2)
            latent_pT(3)
            attn_hi(3)
            hi(20)

            def hi13(n, g, s, turn, half):
                if half == 0:
                    act.wait_ge(e13_in[s], 32 * (turn + 1))
                    if not isinstance(n, int) or n >= 2:
                        act.wait_ge(f_h2, n - 1)
                c = slice(half * KT * FH, (half + 1) * KT * FH)
                copy(e13[g][0][:, c], eraw13[s][:, c]).then_inc(f_hi13, 1)

            def hi2(n, g, s, turn):
                act.wait_ge(e2_in[s], 32 * (turn + 1))
                if not isinstance(n, int) or n >= 2:
                    act.wait_ge(f_out, n - 1)
                copy(e2[g][0], eraw2[s]).then_inc(f_hi2, 1)

            def silu(m, g):
                act.wait_ge(f_v, m)
                nc.scalar.activation(vv[g], vv[g], ACT.Silu).then_inc(f_silu, 1)

            def t_hi(m):
                act.wait_ge(f_t, m + 1)
                copy(hT[0].rearrange("p k t -> p (k t)"), tps[0][:, 0:FP]).then_inc(f_thi, 1)

            def h1_copy(n, g, func=ACT.Copy):
                act.wait_ge(f_h1, n + 1)
                if not isinstance(n, int) or n >= 2:
                    act.wait_ge(f_h3, n - 1)
                nc.scalar.activation(h1c[g], proj[g][:, 0:FH], func).then_inc(f_h1c, 1)

            def step(n, g, s, turn, turn_next, first=False, last=False):
                if not first:
                    silu(n - 1, 1 - g)
                if not last:
                    hi13(n + 1, 1 - g, (s + 1) % ERAW, turn_next, 0)
                t_hi(n - 1)
                if not last:
                    hi13(n + 1, 1 - g, (s + 1) % ERAW, turn_next, 1)
                h1_copy(n, g)
                hi2(n, g, s, turn)

            act.wait_ge(wo_mm, 4)
            act.wait_ge(pad_ready, 4)
            hi13(0, 0, 0, 0, 0)
            hi13(0, 0, 0, 0, 1)
            yT_hi(2)
            act.wait_ge(gate_mm, 1)
            nc.scalar.activation(lg[:, 0, :], misc[:, 0:NE], ACT.Exp, scale=-1.0).then_inc(gate_e, 1)
            hi13(1, 1, 1, 0, 0)
            h1_copy(0, 0, ACT.Silu)
            hi2(0, 0, 0, 0)
            hi13(1, 1, 1, 0, 1)
            step(1, 1, 1, 0, 0, first=True)
            step(2, 0, 2, 0, 0)
            with act.Fori(0, (NE - 4) // 4) as i:
                for j in range(4):
                    step(4 * i + 3 + j, (3 + j) % 2, (3 + j) % ERAW, i if j == 0 else i + 1, i + 1)
            step(NE - 1, 1, 3, 3, 4)
            step(NE, 0, 0, 4, 0, last=True)
            silu(NE, 0)
            t_hi(NE)

        @block.vector
        def _(v):
            count = [0]

            def link(ins):
                count[0] += 1
                ins.then_inc(dve, 1)
                v.wait_ge(dve, count[0])

            def lo(q):
                w = stream[q][1]
                dst = where[q]
                v.wait_ge(hi_done, q + 1)
                nc.vector.tensor_tensor(dst[1][:, 0:w], raw[:, q % RAW, 0:w], dst[0][:, 0:w], ALU.subtract).then_inc(lo_done, 1)

            def v_evac(n):
                _, c, t = parts[n]
                v.wait_ge(proj_mm, n + 1)
                nc.vector.tensor_copy(vbuf[c // 2][:, (c % 2) * 4 + t, :], proj[n % 2][:, :]).then_inc(v_out, 1)

            def layer_norm(n):
                link(nc.vector.bn_stats(st[:, 0:6], x[:, :]))
                nc.vector.bn_aggr(mv[:, :], st[:, 0:6]).then_inc(stats, 1)
                normalise(n)

            def normalise(n):
                v.wait_ge(rstd, n + 1)
                nc.vector.tensor_scalar(y[:, :], x[:, :], mv[:, 0:1], small[:, 61:62], ALU.subtract, ALU.mult).then_inc(y_ready, 1)
                v.wait_ge(y_ready, n + 1)

            def scales(src, amax, s, rs):
                link(nc.vector.tensor_reduce(amax, src, AX.X, ALU.max, apply_absolute_value=True))
                link(nc.vector.tensor_scalar(s, amax, 1.0 / QMAX, QEPS, ALU.mult, ALU.max))
                link(nc.vector.reciprocal(rs, s))

            def quantise_rows(src, n):
                scales(src, small[:, 32:33], small[:, 33 + n:34 + n], small[:, 35:36])
                link(nc.vector.tensor_scalar(tmp[:, :], src, small[:, 35:36], QMAX, ALU.mult, ALU.min))
                link(nc.vector.tensor_scalar(tmp[:, :], tmp[:, :], -QMAX, ROUND, ALU.max, ALU.add))
                nc.vector.tensor_scalar(xq[:, :], tmp[:, :], ROUND, None, ALU.subtract).then_inc(xq_ready, 1)

            def quantise_weights(src, dst, n, loaded, done):
                v.wait_ge(loaded, 16)
                scales(src, small[:, 16 * n:16 * n + 4], small[:, 16 * n + 4:16 * n + 8], small[:, 16 * n + 8:16 * n + 12])
                for t in range(4):
                    link(nc.vector.tensor_scalar(src[:, t, :], src[:, t, :], small[:, 16 * n + 8 + t:16 * n + 9 + t],
                                                 QMAX, ALU.mult, ALU.min))
                link(nc.vector.tensor_scalar(src, src, -QMAX, ROUND, ALU.max, ALU.add))
                nc.vector.tensor_scalar(dst, src, ROUND, None, ALU.subtract).then_inc(done, 1)

            def scale_row(n):
                for t in range(4):
                    nc.vector.tensor_scalar(dg[:, t, :], ident[:, :], small[:, 16 * n + 4 + t:16 * n + 5 + t], None,
                                            ALU.mult).then_inc(diag, 1)

            def xqT_copy(n):
                v.wait_ge(xqT_mm, n + 1)
                nc.vector.tensor_copy(xqT[:, :], misc[:, 0:256].bitcast(BF16)).then_inc(xqT_ready, 1)

            def take_row(n):
                v.wait_ge(sw_mm, n + 1)
                nc.vector.tensor_copy(swrow[:, :], misc[:, :]).then_inc(sw_row, 1)

            def dequantise(dst, n, bias, bias_in):
                v.wait_ge(sw_row, n + 1)
                v.wait_ge(q_mm, n + 1)
                link(nc.vector.scalar_tensor_tensor(dst, misc[:, :], small[:, 33 + n:34 + n], swrow[:, :], ALU.mult, ALU.mult))
                v.wait_ge(bias_in, 16)
                nc.vector.tensor_tensor(dst, dst, bias[:, :], ALU.add).then_inc(q_ready, 1)
                v.wait_ge(q_ready, n + 1)

            for h in range(2):
                for q in range(2):
                    c = slice(h * ITEM // 2, (h + 1) * ITEM // 2)
                    v.wait_ge((hi_first, hi_done)[h], q + 1)
                    nc.vector.tensor_tensor(where[q][1][:, c], raw[:, q, c], where[q][0][:, c],
                                            ALU.subtract).then_inc((lo_first, lo_done)[h], 1)
            v.wait_ge(x_in, 16)
            layer_norm(0)
            quantise_rows(y[:, :], 0)
            lo(2)
            lo(3)
            quantise_weights(wq_raw, wq_int, 0, wq_in, wq_q)
            vs = [n for n, p in enumerate(parts) if p[0] == "V"]
            for n in vs[0:4]:
                v_evac(n)
            lo(4)
            xqT_copy(0)
            v.wait_ge(consts, 6)
            scale_row(0)
            quantise_weights(wo_raw, wo_int, 1, wo_in, wo_q)
            take_row(0)
            v_evac(vs[4])
            v_evac(vs[5])
            dequantise(tmp[:, :], 0, bias_a, bq_in)
            v_evac(vs[6])
            v_evac(vs[7])
            v.wait_ge(qT_mm, 1)
            v.wait_ge(consts, 7)
            mv4 = misc[:, :].rearrange("p (g b q) -> p g b q", g=4, b=B)
            for r in range(4):
                rr = slice(XD * r, XD * (r + 1))
                for b in range(B):
                    dst = qdv[rr, b, :, :].rearrange("p (g two) q -> p g two q", two=2)[:, :, r // 2, (r % 2) * S:(r % 2 + 1) * S]
                    nc.vector.tensor_scalar(dst, mv4[rr, :, b, :], X_SCALE, None, ALU.mult).then_inc(qd_ready, 1)

            def reduce_pair(w):
                v.wait_ge(s_mm, w + 1)
                v.wait_ge((mask_in, mask1_in)[w // NPAIR], 32)
                if w >= 3:
                    v.wait_ge(t_mm, 2 * (w - 2))
                nc.vector.tensor_tensor_reduce(sbuf[:, w % 3, :], sps[:, :], mask[:, :], 1.0, -3e38, ALU.add, ALU.max,
                                               accum_out=nmax[:, w:w + 1]).then_inc(s_red, 1)
                v.wait_ge(s_red, w + 1)
                nc.vector.tensor_scalar(nmax[:, 16 + w:17 + w], nmax[:, w:w + 1], -1.0, None, ALU.mult).then_inc(nm_ready, 1)

            def pt_evac(w):
                v.wait_ge(t_mm, 2 * w + 2)
                if w >= 2:
                    v.wait_ge(pv_mm, w - 1)
                nc.vector.tensor_copy(ptbuf[:, w % 2, 512:1024], tps[1][:, :]).then_inc(pt_d, 1)

            def attend_out(b):
                v.wait_ge(e_done, (b + 1) * NPAIR)
                link(nc.vector.reciprocal(rsum[:, 16 + b * NPAIR:16 + (b + 1) * NPAIR], rsum[:, b * NPAIR:(b + 1) * NPAIR]))
                v.wait_ge(pv_mm, (b + 1) * NPAIR)
                pv4 = pvp[:, :].rearrange("p (j two d) -> p j two d", j=NPAIR, two=2)
                o4 = ob[:, :].rearrange("p (j two d) -> p j two d", j=NPAIR, two=2)
                for t in range(2):
                    rr = slice(S * t, S * (t + 1))
                    nc.vector.tensor_tensor(o4[S * b:S * (b + 1), :, t, :], pv4[rr, :, t, :],
                                            rsum[rr, 16 + b * NPAIR:16 + (b + 1) * NPAIR].unsqueeze(2).to_broadcast([S, NPAIR, XD]),
                                            ALU.mult).then_inc(o_done, 1)

            lo(5)
            vq = list(vs[8:])
            for u in range(NPAIR):
                reduce_pair(u)
                v_evac(vq.pop(0))
                if u >= 2:
                    pt_evac(u - 2)
            pt_evac(NPAIR - 2)
            pt_evac(NPAIR - 1)
            reduce_pair(NPAIR)
            attend_out(0)
            for u in range(1, NPAIR):
                reduce_pair(NPAIR + u)
                pt_evac(NPAIR + u - 1)
                if u == 1:
                    scale_row(1)
                if u in (2, 4, 6, 7):
                    lo(6 + (2, 4, 6, 7).index(u))
            pt_evac(2 * NPAIR - 1)
            take_row(1)
            attend_out(1)
            v.wait_ge(o_done, 4)
            v.wait_ge(bv_in, 16)
            link(nc.vector.tensor_tensor(ob[:, :], ob[:, :], bias_b[:, :], ALU.add))
            quantise_rows(ob[:, :], 1)
            xqT_copy(1)
            dequantise(tmp[:, :], 1, bias_a, bo_in)
            nc.vector.tensor_tensor(x[:, :], x[:, :], tmp[:, :], ALU.add).then_inc(x_second, 1)
            v.wait_ge(x_second, 1)
            layer_norm(1)

            def yT_lo(n):
                v.wait_ge(yTh_r, n)
                nc.vector.tensor_tensor(yT[1][:, :, :].rearrange("p k t -> p (k t)"), misc[:, :],
                                        yT[0][:, :, :].rearrange("p k t -> p (k t)"), ALU.subtract).then_inc(yTl_r, 1)

            yT_lo(1)
            v.wait_ge(down_mm, 1)
            v.wait_ge(bd_in, 16)
            nc.vector.tensor_tensor(tmp[:, :], proj[0][:, :], bias_b[:, :], ALU.add).then_inc(down_r, 1)
            v.wait_ge(cTh_r, 1)
            nc.vector.tensor_tensor(cT[1][:, :, :].rearrange("p k t -> p (k t)"), misc[:, :],
                                    cT[0][:, :, :].rearrange("p k t -> p (k t)"), ALU.subtract).then_inc(cTl_r, 1)
            v.wait_ge(brope_in, 32)
            for j in range(2):
                v.wait_ge(kr_mm, j + 1)
                nc.vector.tensor_tensor(krn[:, 512 * j:512 * (j + 1)], sps[:, 512 * j:512 * (j + 1)],
                                        brope[:, 512 * j:512 * (j + 1)], ALU.add).then_inc(krn_r, 1)
            lo(10)
            for j in range(2):
                v.wait_ge(qr_mm, j + 1)
                nc.vector.tensor_tensor(qrn[:, 512 * j:512 * (j + 1)], sps[:, 512 * j:512 * (j + 1)],
                                        brope[:, 1024 + 512 * j:1024 + 512 * (j + 1)], ALU.add).then_inc(qrn_r, 1)
                lo(11 + j)

            def up_evac(n, dst, which):
                v.wait_ge(up_t, n + 1)
                j = n % 4
                nc.vector.tensor_tensor(dst[:, 4 * j:4 * j + 4, :], tps[n % 2][:, :].rearrange("p (h t) -> p h t", h=4),
                                        hbias[:, which, 4 * j:4 * j + 4].unsqueeze(2).to_broadcast([P, 4, P]),
                                        ALU.add).then_inc(up_out, 1)

            v.wait_ge(small_in, 64)
            up_evac(0, kT, 0)
            up_evac(1, kT, 0)
            up_evac(2, kT, 0)
            lo(13)
            up_evac(3, kT, 0)
            for q in (14, 15, 16):
                lo(q)
            up_evac(4, qT, 1)
            lo(17)
            up_evac(5, qT, 1)
            lo(18)
            up_evac(6, qT, 1)
            lo(19)
            up_evac(7, qT, 1)
            v.wait_ge(qrT_mm, 2)
            nc.vector.memset(qrn[0:DR, :], 0.0).then_inc(qr_zero2, 1)
            v.wait_ge(consts, 10)

            def latent_mask(g):
                v.wait_ge(ms_mm, g + 1)
                for i in range(HG):
                    c = slice(P * i, P * (i + 1))
                    nc.vector.tensor_tensor_reduce(pg[g][:, c], sgp[g][:, c], cmask[:, :], 1.0, -3e38, ALU.add, ALU.max,
                                                   accum_out=mst[:, HG * g + i:HG * g + i + 1]).then_inc(mmax, 1)
                v.wait_ge(mmax, HG * (g + 1))
                nc.vector.tensor_scalar(mst[:, 16 + HG * g:16 + HG * (g + 1)], mst[:, HG * g:HG * (g + 1)], -M_SCALE, None,
                                        ALU.mult).then_inc(mneg, 1)

            def latent_norm(g):
                v.wait_ge(me_done, HG * (g + 1))
                r = mst[:, 32 + HG * g:32 + HG * (g + 1)]
                link(nc.vector.reciprocal(r, r))
                pgv = pg[g].rearrange("p (h k) -> p h k", h=HG)
                nc.vector.tensor_tensor(pgv, pgv, r.unsqueeze(2).to_broadcast([P, HG, P]), ALU.mult).then_inc(mp_r, 1)

            def attn_lo(g):
                v.wait_ge(ma_hi, HG * (g + 1))
                for i in range(HG):
                    h = HG * g + i
                    nc.vector.scalar_tensor_tensor(attnT[1][:, h, :], proj[g % 2][:, P * i:P * (i + 1)], hbias[:, 2, h:h + 1],
                                                   attnT[0][:, h, :], ALU.add, ALU.subtract).then_inc(ma_lo, 1)

            latent_mask(0)
            latent_mask(1)
            latent_norm(0)
            latent_mask(2)
            latent_norm(1)
            latent_mask(3)
            latent_norm(2)
            attn_lo(0)
            latent_norm(3)
            attn_lo(1)
            attn_lo(2)
            attn_lo(3)
            lo(20)
            v.wait_ge(bom_in, 16)
            v.wait_ge(wo_mm, 4)
            link(nc.vector.tensor_tensor(tmp[:, :], wop[:, :], bias_a[:, :], ALU.add))
            link(nc.vector.tensor_tensor(x[:, :], x[:, :], tmp[:, :], ALU.add))
            link(nc.vector.bn_stats(st[:, 0:6], x[:, :]))
            nc.vector.bn_aggr(mv[:, :], st[:, 0:6]).then_inc(stats, 1)

            def lo13(n, g, s, half):
                v.wait_ge(f_hi13, 2 * n + 1 + half)
                c = slice(half * KT * FH, (half + 1) * KT * FH)
                nc.vector.tensor_tensor(e13[g][1][:, c], eraw13[s][:, c], e13[g][0][:, c], ALU.subtract)\
                    .then_inc(f_lo13h if half == 0 else f_lo13, 1)

            lo13(0, 0, 0, 0)
            normalise(2)
            lo13(0, 0, 0, 1)
            yT_lo(2)
            nc.vector.tensor_copy(tmp[:, :], misc[:, :]).then_inc(yT32, 1)
            lo13(1, 1, 1, 0)
            def routing():
                v.wait_ge(gate_e, 1)
                link(nc.vector.tensor_scalar(lg[:, 1, :], lg[:, 0, :], 1.0, None, ALU.add))
                link(nc.vector.reciprocal(lg[:, 2, :], lg[:, 1, :]))
                link(nc.vector.tensor_tensor(lg[:, 3, :], lg[:, 2, :], gb[:, :], ALU.add))
                other = lg[:, 3, :].unsqueeze(1).to_broadcast([P, NE, NE])
                own = lg[:, 3, :].unsqueeze(2).to_broadcast([P, NE, NE])
                link(nc.vector.tensor_tensor(rk[:, 0, :, :], other, own, ALU.is_gt))
                link(nc.vector.tensor_tensor(rk[:, 1, :, :], other, own, ALU.is_equal))
                v.wait_ge(tri_ready, 2)
                link(nc.vector.tensor_tensor(rk[:, 1, :, :], rk[:, 1, :, :], tri, ALU.mult))
                link(nc.vector.tensor_tensor(rk[:, 0, :, :], rk[:, 0, :, :], rk[:, 1, :, :], ALU.add))
                link(nc.vector.tensor_reduce(lg[:, 4, :], rk[:, 0, :, :], AX.X, ALU.add))
                link(nc.vector.tensor_scalar(lg[:, 5, :], lg[:, 4, :], float(TOPK), None, ALU.is_lt))
                link(nc.vector.tensor_tensor(lg[:, 4, :], lg[:, 5, :], lg[:, 3, :], ALU.mult))
                link(nc.vector.tensor_reduce(small[:, 52:53], lg[:, 4, :], AX.X, ALU.add))
                link(nc.vector.reciprocal(small[:, 53:54], small[:, 52:53]))
                link(nc.vector.tensor_scalar(probs[:, :], lg[:, 4, :], small[:, 53:54], None, ALU.mult))

            for g in range(2):
                nc.vector.memset(h3[g][:, FH:FP], 0.0).then_inc(padded, 1)

            def product(m, g, out_t, done):
                v.wait_ge(f_h1c, m + 1)
                v.wait_ge(f_h2, m + 1)
                nc.vector.tensor_tensor(out_t, h1c[g], h2p[g], ALU.mult).then_inc(done, 1)

            def weigh(m, g):
                v.wait_ge(f_silu, m)
                if not isinstance(m, int) or m >= 2:
                    v.wait_ge(f_t, m - 1)
                col = probs[:, m - 1:m] if isinstance(m, int) else probs[:, bass.ds(m - 1, 1)]
                nc.vector.tensor_scalar(h3[g][:, 0:FH], vv[g], col, None, ALU.mult).then_inc(f_h3, 1)

            def t_lo(m):
                v.wait_ge(f_thi, m + 1)
                nc.vector.tensor_tensor(hT[1].rearrange("p k t -> p (k t)"), tps[0][:, 0:FP],
                                        hT[0].rearrange("p k t -> p (k t)"), ALU.subtract).then_inc(f_tlo, 1)

            def step(n, g, s, first=False, last=False):
                if not first:
                    product(n - 1, 1 - g, vv[1 - g], f_v)
                    weigh(n - 1, 1 - g)
                if not last:
                    lo13(n + 1, 1 - g, (s + 1) % ERAW, 0)
                t_lo(n - 1)
                if not last:
                    lo13(n + 1, 1 - g, (s + 1) % ERAW, 1)

            v.wait_ge(padded, 2)
            product(0, 0, h3[0][:, 0:FH], f_h3)
            lo13(1, 1, 1, 1)
            routing()
            step(1, 1, 1, first=True)
            step(2, 0, 2)
            with v.Fori(0, (NE - 4) // 4) as i:
                for j in range(4):
                    step(4 * i + 3 + j, (3 + j) % 2, (3 + j) % ERAW)
            step(NE - 1, 1, 3)
            step(NE, 0, 0, last=True)
            product(NE, 0, vv[0], f_v)
            weigh(NE, 0)
            t_lo(NE)
            v.wait_ge(f_out, NE + 1)
            nc.vector.tensor_tensor(x[:, :], pvp[:, :], x[:, :], ALU.add).then_inc(res_ready, 1)

        @block.tensor
        def _(pe):
            def mm3(o, w, m, start, stop):
                nc.tensor.matmul(o, w[0], m[0], start=start, stop=False)
                nc.tensor.matmul(o, w[1], m[0], start=False, stop=False)
                return nc.tensor.matmul(o, w[0], m[1], start=False, stop=stop)

            def split(hl2, f):
                return [f(t) for t in hl2]

            def wait_item(q):
                pe.wait_ge(lo_done, q + 1)

            def ktile(t, k, lo_, hi_, n):
                return t[:, k * n + lo_:k * n + hi_]

            def evacuated(n):
                if n >= 2:
                    m = n - 2
                    if parts[m][0] == "K":
                        pe.wait_ge(k_out, k_before[m])
                    else:
                        pe.wait_ge(v_out, v_before[m])

            def part(n):
                kind, c, j = parts[n]
                slot = where[CTX_Q[c]]
                evacuated(n)
                if n == 0:
                    pe.wait_ge(lo_first, 2)
                else:
                    wait_item(CTX_Q[c])
                if kind == "V":
                    wait_item(2)
                for k in range(KT):
                    if n == 0 and k == KT // 2:
                        wait_item(1)
                    if kind == "K":
                        w = split(wk_hl, lambda t: ktile(t, k, P * j, P * (j + 1), D))
                        m = split(slot, lambda t: ktile(t, k, 0, CH, CH))
                    else:
                        w = split(slot, lambda t: ktile(t, k, P * j, P * (j + 1), CH))
                        m = split(wv_hl, lambda t: ktile(t, k, 0, D, D))
                    last = mm3(proj[n % 2][:, :], w, m, k == 0, k == KT - 1)
                last.then_inc(proj_mm, 1)

            def x_transposes(n):
                pe.wait_ge(xq_ready, n + 1)
                o = misc[:, 0:256].bitcast(BF16)
                for k in range(KT):
                    last = nc.tensor.transpose(o[:, P * k:P * (k + 1)], xq[:, P * k:P * (k + 1)], identb[:, :])
                last.then_inc(xqT_mm, 1)

            def w_transposes(src, n, ready):
                pe.wait_ge(ready, 1)
                if n:
                    pe.wait_ge(wT_ready, 2 * n)
                for k2 in range(2):
                    o = tps[k2][:, :].bitcast(BF16)
                    for k in range(2):
                        for t in range(4):
                            last = nc.tensor.transpose(o[:, D * k + P * t:D * k + P * (t + 1)],
                                                       src[:, t, P * (2 * k2 + k):P * (2 * k2 + k + 1)], identb[:, :])
                    last.then_inc(wT_mm, 1)

            def row_of_scales(n):
                pe.wait_ge(diag, 4 * (n + 1))
                nc.tensor.matmul(misc[:, :], ones[:, :], dg[:, :, :].rearrange("p t n -> p (t n)"), start=True, stop=True).then_inc(sw_mm, 1)

            def integer_product(w, n):
                pe.wait_ge(sw_row, n + 1)
                pe.wait_ge(xqT_ready, n + 1)
                pe.wait_ge(wT_ready, 2 * (n + 1))
                for k in range(KT):
                    last = nc.tensor.matmul(misc[:, :], xqT[:, P * k:P * (k + 1)], w[:, k, :], start=(k == 0), stop=(k == KT - 1))
                last.then_inc(q_mm, 1)

            for n in range(0, 8):
                part(n)
            pe.wait_ge(consts, 6)
            x_transposes(0)
            for n in range(8, 12):
                part(n)
            pe.wait_ge(xqT_ready, 1)
            row_of_scales(0)
            w_transposes(wq_int, 0, wq_q)
            for n in range(12, 14):
                part(n)
            integer_product(wqT, 0)
            for n in range(14, 16):
                part(n)
            pe.wait_ge(q_ready, 1)
            for k in range(4):
                last = nc.tensor.transpose(misc[:, P * k:P * (k + 1)], tmp[:, P * k:P * (k + 1)], ident[:, :])
            last.then_inc(qT_mm, 1)
            w_transposes(wo_int, 1, wo_q)
            pe.wait_ge(k_out, 8)
            pe.wait_ge(qd_ready, 8)

            def scores(w):
                b, u = w // NPAIR, w % NPAIR
                if w:
                    pe.wait_ge(s_red, w)
                for c in range(2):
                    last = nc.tensor.matmul(sps[:, CH * c:CH * (c + 1)], qdv[:, b, u, :], kbuf[:, u // 2, CH * c:CH * (c + 1)],
                                            start=True, stop=True)
                last.then_inc(s_mm, 1)

            def p_transposes(w):
                pe.wait_ge(e_done, w + 1)
                for c in range(2):
                    if w:
                        pe.wait_ge((pt_a, pt_d)[c], w)
                    for t in range(4):
                        last = nc.tensor.transpose(tps[c][:, P * t:P * (t + 1)],
                                                   sbuf[:, w % 3, CH * c + P * t:CH * c + P * (t + 1)], ident[:, :])
                    last.then_inc(t_mm, 1)

            def values(w):
                b, u = w // NPAIR, w % NPAIR
                if w == NPAIR:
                    pe.wait_ge(o_done, 2)
                pe.wait_ge(pt_a, w + 1)
                pe.wait_ge(pt_d, w + 1)
                for t in range(8):
                    last = nc.tensor.matmul(pvp[:, 64 * u:64 * (u + 1)], ptbuf[:, w % 2, P * t:P * (t + 1)],
                                            vbuf[b][:, t, 64 * u:64 * (u + 1)], start=(t == 0), stop=(t == 7))
                last.then_inc(pv_mm, 1)

            pe.wait_ge(v_out, 8)
            pe.wait_ge(wT_ready, 4)
            nxt = 16
            for u in range(NPAIR):
                scores(u)
                part(nxt)
                nxt += 1
                if u >= 2:
                    p_transposes(u - 2)
                if u:
                    part(nxt)
                    nxt += 1
                if u >= 2:
                    values(u - 2)
            part(nxt)
            p_transposes(NPAIR - 2)
            values(NPAIR - 2)
            p_transposes(NPAIR - 1)
            pe.wait_ge(k_out, 16)
            pe.wait_ge(v_out, 16)
            for u in range(NPAIR):
                w = NPAIR + u
                scores(w)
                if u:
                    p_transposes(w - 1)
                if u != 1:
                    values(w - 2 if u else w - 1)
            p_transposes(2 * NPAIR - 1)
            row_of_scales(1)
            values(2 * NPAIR - 2)
            values(2 * NPAIR - 1)
            pe.wait_ge(sw_row, 2)
            x_transposes(1)
            integer_product(woT, 1)

            def y_transposes(n):
                pe.wait_ge(y_ready, n + 1)
                yv = y[:, :].rearrange("t (p k) -> t k p", k=KT)
                for k in range(KT):
                    last = nc.tensor.transpose(misc[:, P * k:P * (k + 1)], yv[:, k, :], ident[:, :])
                last.then_inc(yT_mm, 1)

            y_transposes(1)
            pe.wait_ge(yTl_r, 1)
            wait_item(WD_Q)
            for k in range(KT):
                last = mm3(proj[0][:, :], split(yT, lambda t: t[:, k, :]), split(where[WD_Q], lambda t: ktile(t, k, 0, D, D)),
                           k == 0, k == KT - 1)
            last.then_inc(down_mm, 1)
            for j in range(2):
                q = WKR_Q + j
                wait_item(q)
                for k in range(KT):
                    last = mm3(sps[:, 512 * j:512 * (j + 1)], split(yT, lambda t: t[:, k, :]),
                               split(where[q], lambda t: ktile(t, k, 0, D, D)), k == 0, k == KT - 1)
                last.then_inc(kr_mm, 1)
                if j == 0:
                    pe.wait_ge(down_r, 1)
                    for k in range(4):
                        last = nc.tensor.transpose(misc[:, P * k:P * (k + 1)], tmp[:, P * k:P * (k + 1)], ident[:, :])
                    last.then_inc(cT_mm, 1)
            pe.wait_ge(cTl_r, 1)
            for j in range(2):
                q = WQR_Q + j
                wait_item(q)
                pe.wait_ge(krn_r, j + 1)
                for k in range(QT):
                    last = mm3(sps[:, 512 * j:512 * (j + 1)], split(cT, lambda t: t[:, 1 + k, :]),
                               split(where[q], lambda t: ktile(t, k, 0, 512, 512)), k == 0, k == QT - 1)
                last.then_inc(qr_mm, 1)

            def up_transposes(n):
                pe.wait_ge(up_nat, n + 1)
                if n >= 2:
                    pe.wait_ge(up_out, n - 1)
                for t in range(4):
                    last = nc.tensor.transpose(tps[n % 2][:, P * t:P * (t + 1)], stage[n % 2][:, P * t:P * (t + 1)], ident[:, :])
                last.then_inc(up_t, 1)

            wait_item(WKU_Q)
            for j in range(4):
                if j >= 2:
                    pe.wait_ge(up_nat, j - 1)
                last = mm3(up_ps[j % 2], split(cT, lambda t: t[:, 0, :]),
                           split(where[WKU_Q], lambda t: t[:, 512 * j:512 * (j + 1)]), True, True)
                last.then_inc(up_mm, 1)
                if j:
                    up_transposes(j - 1)
            wait_item(WVU_Q)
            for j in range(4):
                if j >= 2:
                    pe.wait_ge(vu_out, j - 1)
                last = mm3(proj[j % 2][:, :], split(cT, lambda t: t[:, 0, :]),
                           split(where[WVU_Q], lambda t: t[:, 512 * j:512 * (j + 1)]), True, True)
                last.then_inc(vu_mm, 1)
                if j == 0:
                    up_transposes(3)
            for j in range(4):
                q = WQU_Q + j
                wait_item(q)
                pe.wait_ge(up_nat, j + 3)
                for k in range(QT):
                    last = mm3(up_ps[j % 2], split(cT, lambda t: t[:, 1 + k, :]),
                               split(where[q], lambda t: ktile(t, k, 0, 512, 512)), k == 0, k == QT - 1)
                last.then_inc(up_mm, 1)
                if j:
                    up_transposes(4 + j - 1)
            pe.wait_ge(kr_roped, 1)
            pe.wait_ge(vu_out, 4)
            for i in range(2):
                for t in range(4):
                    last = nc.tensor.transpose(proj[i][:, P * t:P * (t + 1)], krn[:, 512 * i + P * t:512 * i + P * (t + 1)], ident[:, :])
                last.then_inc(krT_mm, 1)
            up_transposes(7)
            pe.wait_ge(qr_roped, 1)
            pe.wait_ge(up_nat, 8)
            for i in range(2):
                for t in range(4):
                    last = nc.tensor.transpose(qrtp[i][:, P * t:P * (t + 1)], qrn[:, 512 * i + P * t:512 * i + P * (t + 1)], ident[:, :])
                last.then_inc(qrT_mm, 1)
            pe.wait_ge(up_out, 8)
            pe.wait_ge(krT_r, 2)
            pe.wait_ge(qrT_r, 4)
            pe.wait_ge(qr_zero2, 1)
            pe.wait_ge(qrn_r, 2)

            def latent_scores(g):
                for i in range(HG):
                    h = HG * g + i
                    o = sgp[g][:, P * i:P * (i + 1)]
                    nc.tensor.matmul(o, qT[:, h, :], kT[:, h, :], start=True, stop=False)
                    last = nc.tensor.matmul(o, qrT[h % 2][:, h // 2, :], krT[:, h // 2, :], start=False, stop=True)
                last.then_inc(ms_mm, 1)

            def latent_transposes(g):
                pe.wait_ge(mp_r, g + 1)
                if g >= 2:
                    pe.wait_ge(mt_r, g - 1)
                for i in range(HG):
                    last = nc.tensor.transpose(ptp[g % 2][:, P * i:P * (i + 1)], pg[g][:, P * i:P * (i + 1)], ident[:, :])
                last.then_inc(mt_mm, 1)

            def latent_values(g):
                pe.wait_ge(mt_r, g + 1)
                if g >= 2:
                    pe.wait_ge(ma_lo, HG * (g - 1))
                for i in range(HG):
                    last = nc.tensor.matmul(proj[g % 2][:, P * i:P * (i + 1)], vm[:, HG * g + i, :], ptg[g % 2][:, P * i:P * (i + 1)],
                                            start=True, stop=True)
                last.then_inc(ma_mm, 1)

            def latent_out(g):
                q = WOM_Q + g
                wait_item(q)
                pe.wait_ge(ma_lo, HG * (g + 1))
                for i in range(HG):
                    h = HG * g + i
                    last = mm3(wop[:, :], split(attnT, lambda t: t[:, h, :]), split(where[q], lambda t: ktile(t, i, 0, D, D)),
                               h == 0, h == H - 1)
                last.then_inc(wo_mm, 1)

            for g in range(4):
                latent_scores(g)
            latent_transposes(0)
            latent_transposes(1)
            latent_values(0)
            latent_values(1)
            latent_transposes(2)
            pe.wait_ge(mmax, HG * 3)
            latent_out(0)
            latent_values(2)
            latent_transposes(3)
            latent_out(1)
            latent_values(3)
            latent_out(2)
            latent_out(3)

            y_transposes(2)
            pe.wait_ge(yTl_r, 2)
            pe.wait_ge(yT32, 1)
            for k in range(KT):
                last = nc.tensor.matmul(misc[:, 0:NE], tmp[:, P * k:P * (k + 1)], gw[:, k, :], start=(k == 0), stop=(k == KT - 1))
            last.then_inc(gate_mm, 1)

            def up(n, g, half):
                if half == 0:
                    pe.wait_ge(f_lo13h, n + 1)
                else:
                    pe.wait_ge(f_lo13, n + 1)
                if not isinstance(n, int) or n >= 2:
                    pe.wait_ge(f_h1c if half == 0 else f_h3, n - 1)
                o = proj[g][:, 0:FH] if half == 0 else h2p[g]
                base = half * KT * FH
                for k in range(KT):
                    last = mm3(o, split(yT, lambda t: t[:, k, :]),
                               split(e13[g], lambda t: t[:, base + k * FH:base + (k + 1) * FH]), k == 0, k == KT - 1)
                last.then_inc(f_h1 if half == 0 else f_h2, 1)

            def h_transposes(m, g):
                pe.wait_ge(f_h3, m + 1)
                if not isinstance(m, int) or m >= 1:
                    pe.wait_ge(f_tlo, m)
                for t in range(FT):
                    last = nc.tensor.transpose(tps[0][:, P * t:P * (t + 1)], h3[g][:, P * t:P * (t + 1)], ident[:, :])
                last.then_inc(f_t, 1)

            def down(m, g, start=False, stop=False):
                pe.wait_ge(f_tlo, m + 1)
                pe.wait_ge(f_lo2, m + 1)
                for t in range(FT):
                    last = mm3(pvp[:, :], split(hT, lambda s: s[:, t, :]), split(e2[g], lambda s: s[:, D * t:D * (t + 1)]),
                               start and t == 0, stop and t == FT - 1)
                last.then_inc(f_out, 1)

            def step(n, g, start=False):
                up(n, g, 0)
                h_transposes(n - 1, 1 - g)
                up(n, g, 1)
                down(n - 1, 1 - g, start=start)

            up(0, 0, 0)
            up(0, 0, 1)
            step(1, 1, start=True)
            step(2, 0)
            with pe.Fori(0, (NE - 4) // 4) as i:
                for j in range(4):
                    step(4 * i + 3 + j, (3 + j) % 2)
            step(NE - 1, 1)
            step(NE, 0)
            h_transposes(NE, 0)
            down(NE, 0, stop=True)


def perceiver_block(nc, inputs, out):
    build(nc, inputs, out)


def kernel(**inputs):
    import numpy as _np
    import concourse.bacc as _bacc
    from concourse import mybir as _mybir
    from concourse.bass_utils import run_bass_kernel_spmd as _run

    g = {k: _np.asarray(v) for k, v in inputs.items()}
    f = _np.ascontiguousarray

    def tiles(w, k, j):
        n = w.shape[1] // j
        return f(w.reshape(k, 128, j, n).transpose(2, 1, 0, 3)).reshape(j, 128, k * n)

    def halves(w):
        return f(w.reshape(128, 4, 2, 512).transpose(2, 0, 1, 3)).reshape(2, 128, 2048)

    freq = (1.0 / 10000.0 ** (_np.arange(0, 64, 2, dtype=_np.float32) / _np.float32(64))).astype(_np.float32)
    ang = (_np.arange(128) % 64).astype(_np.float32)[:, None] * freq
    cos, sin = _np.cos(ang), _np.sin(ang)
    tables = f(_np.stack([_np.concatenate([cos, cos], 1), _np.concatenate([-sin, sin], 1)], 1).astype(_np.float32))

    arrays = {
        "x": f(g["x"].reshape(128, 512)),
        "mask": f(g["mask_BxSxS2_ff0"].reshape(128, 1024)),
        "ctx": f(g["ctx_2048"].reshape(4, 512, 512).transpose(0, 2, 1)).reshape(4, 128, 2048),
        "wk": f(g["L0_xattn_wk"].T).reshape(128, 2048),
        "wv": f(g["L0_xattn_wv"].T).reshape(128, 2048),
        "wq": f(g["L0_xattn_wq"].reshape(4, 128, 512).transpose(1, 0, 2)),
        "wo": f(g["L0_xattn_wo"].reshape(4, 128, 512).transpose(1, 0, 2)),
        "bq": g["L0_xattn_bq"], "bv": g["L0_xattn_bv"], "bo": g["L0_xattn_bo"],
        "bkT": f(g["L0_xattn_bk"].reshape(4, 128).T),
        "wd": f(_np.concatenate([g["L0_attn_Wkd"], g["L0_attn_Wqd"]], 0).T).reshape(128, 2048),
        "bd": f(_np.concatenate([g["L0_attn_bkd"], g["L0_attn_bqd"]], 0)),
        "wkr": halves(g["L0_attn_Wkr"].T),
        "wku": f(g["L0_attn_Wku"].T), "wvu": f(g["L0_attn_Wvu"].T),
        "wqr": tiles(g["L0_attn_Wqr"].T, 3, 2),
        "wqu": tiles(g["L0_attn_Wqu"].T, 3, 4),
        "wom": f(g["L0_attn_Wo"].T.reshape(4, 4, 128, 512).transpose(0, 2, 1, 3)).reshape(4, 128, 2048),
        "bkr": g["L0_attn_bkr"], "bqr": g["L0_attn_bqr"], "bom": g["L0_attn_bo"],
        "hbias": f(_np.stack([g["L0_attn_" + n].reshape(16, 128).T for n in ("bku", "bqu", "bvu")], 1)),
        "rope": tables,
        "gw": f(g["L0_ffn_gate_w"].T).reshape(128, 4, 16),
        "gb": g["L0_ffn_gate_b"],
        "w1s": g["L0_ffn_w1_shared"], "w2s": g["L0_ffn_w2_shared"], "w3s": g["L0_ffn_w3_shared"],
        "w1r": g["L0_ffn_w1_routed"], "w2r": g["L0_ffn_w2_routed"], "w3r": g["L0_ffn_w3_routed"],
    }
    nc = _bacc.Bacc("TRN2", target_bir_lowering=False, num_devices=1)
    feeds, aps = {}, {}
    for name, v in arrays.items():
        v = f(v)
        feeds[f"in_{name}"] = v
        aps[name] = nc.dram_tensor(f"in_{name}", v.shape, _mybir.dt.from_np(v.dtype), kind="ExternalInput").ap()
    out = nc.dram_tensor("out", (128, 512), _mybir.dt.float32, kind="ExternalOutput").ap()
    perceiver_block(nc, aps, out)
    r = _run(nc, [feeds], core_ids=[0])
    return r.results[0]["out"].reshape(2, 64, 512)
```

```python
from contextlib import ExitStack

import concourse.bass as bass
from concourse import mybir

F32 = mybir.dt.float32
F32R = mybir.dt.float32r
BF16 = mybir.dt.bfloat16
ALU = mybir.AluOpType
ACT = mybir.ActivationFunctionType
AX = mybir.AxisListType

P = 128
B, S, D = 2, 64, 512
KEYS = 1024
KT = D // P
XH, XD = 16, 32
NPAIR = XH // 2
H, DH, DR = 16, 128, 64
DQ = 384
QT = DQ // P
HG = 4
NE, TOPK, FH = 16, 4, 352
FT = 3
FP = FT * P
CH = 512
ITEM = 2048
RAW = 3
ERAW = 4
QMAX, QEPS = 127.0, 1e-8
ROUND = 1.5 * 2.0 ** 23
NEG = -1e30
X_SCALE = XD ** -0.5
M_SCALE = (DH + DR) ** -0.5
W13 = 2 * KT * FH
W2 = FT * D


def build(nc, a, out):
    ctx = ExitStack()
    with ctx:
        def sb(name, shape, dt=F32):
            return ctx.enter_context(nc.sbuf_tensor(name, shape, dt))

        def sem(name):
            return ctx.enter_context(nc.semaphore(name))

        raw = sb("raw", [P, RAW, ITEM])
        area = sb("area", [P, 17408])
        hl = sb("hl", [P, 2 * (W13 + W2) * 2], F32R)
        kbuf = area[:, 0:4096].rearrange("p (g k) -> p g k", g=4)
        vbuf = [area[:, 4096 * (1 + b):4096 * (2 + b)].rearrange("p (t n) -> p t n", t=8) for b in range(B)]
        sbuf = area[:, 12288:15360].rearrange("p (r k) -> p r k", r=3)
        ptbuf = area[:, 15360:17408].rearrange("p (r k) -> p r k", r=2)
        wq_raw = area[:, 12288:14336].rearrange("p (t n) -> p t n", t=4)
        wo_raw = area[:, 14336:16384].rearrange("p (t n) -> p t n", t=4)
        wq_int = area[:, 8192:9216].bitcast(BF16).rearrange("p (t n) -> p t n", t=4)
        wo_int = area[:, 9216:10240].bitcast(BF16).rearrange("p (t n) -> p t n", t=4)
        EW = W13 + W2
        raws = raw[:, :, :].rearrange("p r n -> p (r n)")
        slots = [area[:, EW * i:EW * (i + 1)] for i in range(3)] + [raws[:, 0:EW]]
        eraw13 = [t[:, 0:W13] for t in slots]
        eraw2 = [t[:, W13:EW] for t in slots]
        qT = area[:, 9216:11264].rearrange("p (h t) -> p h t", h=H)
        kT = area[:, 11264:13312].rearrange("p (h t) -> p h t", h=H)
        vm = area[:, 13312:15360].rearrange("p (h d) -> p h d", h=H)
        krn = area[:, 15360:16384]
        qrn = area[:, 16384:17408]

        def pair(base):
            return [hl[:, base:base + ITEM], hl[:, base + ITEM:base + 2 * ITEM]]
        wk_hl, wv_hl = pair(0), pair(2 * ITEM)
        ring_hl = [pair((4 + 2 * r) * ITEM) for r in range(2)]
        attnT = [t.rearrange("p (h t) -> p h t", h=H) for t in wk_hl]
        def halves_of(g, lo_, hi_):
            return [hl[:, (2 * (1 - g) + i) * EW + lo_:(2 * (1 - g) + i) * EW + hi_] for i in range(2)]
        e13 = [halves_of(g, 0, W13) for g in range(2)]
        e2 = [halves_of(g, W13, EW) for g in range(2)]

        x = sb("x", [P, D])
        y = sb("y", [P, D])
        tmp = sb("tmp", [P, D])
        ob = sb("ob", [P, D])
        yT = [sb("yTh", [P, KT, P], F32R), sb("yTl", [P, KT, P], F32R)]
        cT = [sb("cTh", [P, KT, P], F32R), sb("cTl", [P, KT, P], F32R)]
        mask = sb("mask", [P, KEYS])
        qd = sb("qd", [P, 2048])
        qdv = qd[:, :].rearrange("p (b j q) -> p b j q", b=B, j=NPAIR)
        krT = qd[:, 0:1024].rearrange("p (j t) -> p j t", j=8)
        qrT = [qd[:, 1024:2048].rearrange("p (j t) -> p j t", j=8), qrn.rearrange("p (j t) -> p j t", j=8)]
        wint = sb("wint", [P, 2048])
        wqT = wint[:, 0:1024].bitcast(BF16).rearrange("p (k n) -> p k n", k=KT)
        woT = wint[:, 1024:2048].bitcast(BF16).rearrange("p (k n) -> p k n", k=KT)
        brope = wint
        bias_a = sb("bias_a", [P, D])
        bias_b = sb("bias_b", [P, D])
        swrow = sb("swrow", [P, D])
        rope = sb("rope", [P, 2, DR])
        ident = sb("ident", [P, P])
        identb = sb("identb", [P, P], BF16)
        cmask = sb("cmask", [P, P])
        ones = sb("ones", [P, P])
        bkT = sb("bkT", [P, 4])
        hbias = sb("hbias", [P, 3, H])
        gw = sb("gw", [P, KT, NE])
        gb = sb("gb", [P, NE])
        tri = area[:, 13824:13824 + NE * NE].rearrange("p (e f) -> p e f", e=NE)
        rk = area[:, 13312:13312 + 2 * NE * NE].rearrange("p (a e f) -> p a e f", a=2, e=NE)
        lg = sb("lg", [P, 6, NE])
        probs = sb("probs", [P, NE])
        small = sb("small", [P, 64])
        rsum = sb("rsum", [P, 32])
        nmax = sb("nmax", [P, 32])
        st = sb("st", [P, 8])
        mv = sb("mv", [P, 2])
        power = sb("power", [P, 1])

        mst = swrow[:, 0:48]
        xq = sb("xq", [P, D], BF16)
        xqT = sb("xqT", [P, D], BF16)
        dg = y[:, :].rearrange("p (t n) -> p t n", t=4)
        pg = [mask[:, 0:512], mask[:, 512:1024], tmp[:, :], ob[:, :]]
        ptg = [y[:, :], wint[:, 0:512]]
        stage = [y[:, :], ob[:, :]]

        h1c = [tmp[:, 0:FH], ob[:, 0:FH]]
        vv = [mask[:, 0:FH], mask[:, 512:512 + FH]]
        h3 = [qd[:, 0:FP], qd[:, 512:512 + FP]]
        hT = [t[:, 0:FT, :] for t in cT]

        proj = [ctx.enter_context(nc.psum_tensor(f"proj{i}", [P, 512], F32)) for i in range(2)]
        sps = ctx.enter_context(nc.psum_tensor("sps", [P, 1024], F32))
        tps = [ctx.enter_context(nc.psum_tensor(f"tps{i}", [P, 512], F32)) for i in range(2)]
        pvp = ctx.enter_context(nc.psum_tensor("pvp", [P, 512], F32))
        misc = ctx.enter_context(nc.psum_tensor("misc", [P, 512], F32))

        up_ps = [misc[:, :], pvp[:, :]]
        sgp = [sps[:, 0:512], sps[:, 512:1024], tps[0][:, :], tps[1][:, :]]
        ptp = [misc[:, :], pvp[:, :]]
        wop = tps[0]
        h2p = [sps[:, 0:FH], sps[:, 512:512 + FH]]

        raw_in = [sem(f"raw_in{i}") for i in range(RAW)]
        hi_done, lo_done, hi_dve, lo_pool = sem("hi_done"), sem("lo_done"), sem("hi_by_dve"), sem("lo_by_pool")
        x_second, x_bias, bk_in, qrn_r, ropeq_step, f_lo13h = sem("x_second"), sem("x_bias"), sem("bk_in"), sem("qrn_ready"), sem("rope_q_step"), sem("f_lo13_half")
        x_in, wq_in, wo_in, small_in, mask_in = sem("x_in"), sem("wq_in"), sem("wo_in"), sem("small_in"), sem("mask_in")
        bq_in, bv_in, brope_in = sem("bq_in"), sem("bv_in"), sem("brope_in")
        bo_in, bd_in, bom_in, mask1_in = sem("bo_in"), sem("bd_in"), sem("bom_in"), sem("mask1_in")
        consts = sem("consts")
        dve = sem("dve_step")
        ropek_step, up_nat, up_t = sem("rope_k_step"), sem("up_staged"), sem("up_t_mm")
        first_in = [sem(f"first_in{i}") for i in range(2 * KT)]
        hi_first, lo_first = sem("hi_first"), sem("lo_first")
        stats, vareps, rstd = sem("ln_stats"), sem("ln_var_eps"), sem("ln_rstd")
        wq_q, wo_q = sem("wq_quantised"), sem("wo_quantised")
        xq_ready, xqT_mm, xqT_ready = sem("xq_ready"), sem("xqT_mm"), sem("xqT_ready")
        wT_mm, wT_ready = sem("wT_mm"), sem("wT_ready")
        sw_mm, sw_row, diag = sem("sw_mm"), sem("sw_row"), sem("diag_ready")
        q_mm, q_ready, qT_mm, qd_ready = sem("q_mm"), sem("q_ready"), sem("qT_mm"), sem("qd_ready")
        proj_mm, k_out, v_out = sem("proj_mm"), sem("k_out"), sem("v_out")
        s_mm, s_red, nm_ready, e_done = sem("scores_mm"), sem("scores_reduced"), sem("neg_max"), sem("exp_done")
        t_mm, pt_a, pt_d, pv_mm, o_done = sem("t_mm"), sem("pt_act"), sem("pt_dve"), sem("pv_mm"), sem("o_done")
        y_ready, yT_mm, yTh_r, yTl_r = sem("y_ready"), sem("yT_mm"), sem("yTh_ready"), sem("yTl_ready")
        down_mm, down_r, cT_mm, cTh_r, cTl_r = sem("down_mm"), sem("down_ready"), sem("cT_mm"), sem("cTh_ready"), sem("cTl_ready")
        kr_mm, krn_r, kr_roped, krT_mm, krT_r = sem("kr_mm"), sem("krn_ready"), sem("kr_roped"), sem("krT_mm"), sem("krT_ready")
        qr_mm, qr_roped, qrT_mm, qrT_r = sem("qr_mm"), sem("qr_roped"), sem("qrT_mm"), sem("qrT_ready")
        up_mm, up_out, vu_mm, vu_out = sem("up_mm"), sem("up_out"), sem("vu_mm"), sem("vu_out")
        ms_mm, mmax, mneg, me_done, mp_r = sem("mla_scores_mm"), sem("mla_max"), sem("mla_neg_max"), sem("mla_exp"), sem("mla_probs")
        qr_zero2 = sem("qr_zero_odd")
        mt_mm, mt_r, ma_mm, ma_hi, ma_lo = sem("mla_pT_mm"), sem("mla_pT"), sem("mla_attn_mm"), sem("mla_attn_hi"), sem("mla_attn_lo")
        ma_hi_dve = sem("mla_attn_hi_by_dve")
        wo_mm = sem("wo_mm")
        yT32, gate_mm, gate_e, padded = sem("yT_f32"), sem("gate_mm"), sem("gate_exp"), sem("h3_padded")
        pad_ready, tri_ready, qr_zero = sem("pad_ready"), sem("tri_ready"), sem("qr_zero")
        e13_in = [sem(f"e13_in{g}") for g in range(ERAW)]
        e2_in = [sem(f"e2_in{g}") for g in range(ERAW)]
        f_hi13, f_lo13, f_hi2, f_lo2 = sem("f_hi13"), sem("f_lo13"), sem("f_hi2"), sem("f_lo2")
        f_h1, f_h2, f_h1c, f_v, f_silu, f_h3 = sem("f_h1_mm"), sem("f_h2_mm"), sem("f_h1_copied"), sem("f_product"), sem("f_silu"), sem("f_h3")
        f_t, f_thi, f_tlo, f_out = sem("f_t_mm"), sem("f_t_hi"), sem("f_t_lo"), sem("f_out_mm")
        res_ready, out_done = sem("result_ready"), sem("out_done")

        stream = [(a["ctx"][0], ITEM), (a["wk"], ITEM), (a["wv"], ITEM)] + [(a["ctx"][c], ITEM) for c in (1, 2, 3)]
        stream += [(a["wd"], ITEM)] + [(a["wkr"][j], ITEM) for j in range(2)]
        stream += [(a["wqr"][j], QT * 512) for j in range(2)] + [(a["wku"], ITEM), (a["wvu"], ITEM)]
        stream += [(a["wqu"][j], QT * 512) for j in range(4)] + [(a["wom"][j], ITEM) for j in range(4)]
        place = [wk_hl, wv_hl] + ring_hl
        order = [2, 0, 1, 3, 2, 3] + [1, 2, 0, 3, 1, 2, 0, 3, 1, 2, 3, 1, 2, 3, 1]
        where = [place[i] for i in order]
        CTX_Q, WK_Q, WV_Q = [0, 3, 4, 5], 1, 2
        WD_Q, WKR_Q, WQR_Q, WKU_Q, WVU_Q, WQU_Q, WOM_Q = 6, 7, 9, 11, 12, 13, 17
        pieces = [(WK_Q, 0)] + [(0, k) for k in range(KT)] + [(WK_Q, g) for g in range(1, 4)]

        def piece_at(i, first, done):
            q, c = pieces[i]
            return (done, q + 1) if c == KT - 1 else (first, sum(p[1] < KT - 1 for p in pieces[:i + 1]))

        HI_DVE, LO_POOL = WOM_Q + 2, (WOM_Q + 1, WOM_Q + 2, WOM_Q + 3)

        def hi_count(q):
            return q + 1 - (q > HI_DVE)

        def split_at(q):
            if q in LO_POOL:
                return lo_pool, LO_POOL.index(q) + 1
            return lo_done, q + 1 - sum(p < q for p in LO_POOL)

        parts = []
        for c in range(2):
            parts += [("K", c, g) for g in range(4)] + [("V", c, t) for t in range(4)]
        for u in range(NPAIR):
            parts.append(("V", 2 + u // 4, u % 4))
            if u:
                parts.append(("K", 2 + (u - 1) % 2, (u - 1) // 2))
        parts.append(("K", 3, 3))
        k_before = [sum(p[0] == "K" for p in parts[:n + 1]) for n in range(len(parts))]
        v_before = [sum(p[0] == "V" for p in parts[:n + 1]) for n in range(len(parts))]
        last_k = max(n for n, p in enumerate(parts) if p[0] == "K") + 1
        last_v = max(n for n, p in enumerate(parts) if p[0] == "V") + 1
        last_c = [max(n for n, p in enumerate(parts) if p[1] == c) + 1 for c in range(4)]
        freed = [(proj_mm, n) for n in (last_c[0], last_k, last_v, last_c[1], last_c[2], last_c[3])]
        freed += [(down_mm, 1), (kr_mm, 1), (kr_mm, 2), (qr_mm, 1), (qr_mm, 2), (up_mm, 4), (vu_mm, 4)]
        freed += [(up_mm, 5 + j) for j in range(4)] + [(wo_mm, j + 1) for j in range(4)]

        block = ctx.enter_context(nc.Block())

        def rows(v):
            return v.partition_broadcast(P)

        def e_of(w, e):
            return w[e] if isinstance(e, int) else w[bass.ds(e, 1)].rearrange("e d n -> (e d) n")

        @block.sync
        def _(sp):
            def item(q):
                if q >= RAW:
                    sp.wait_ge(lo_done, q - RAW + 1)
                sp.dma_start(raw[:, q % RAW, 0:stream[q][1]], stream[q][0]).then_inc(raw_in[q % RAW], 16)

            def expert(s, w1, w3, w2):
                sp.dma_start(eraw13[s][:, 0:KT * FH], w1.rearrange("(p k) n -> p (k n)", k=KT)).then_inc(e13_in[s], 16)
                sp.dma_start(eraw13[s][:, KT * FH:W13], w3.rearrange("(p k) n -> p (k n)", k=KT)).then_inc(e13_in[s], 16)
                sp.dma_start(eraw2[s][:, 0:2 * D].rearrange("p (t n) -> p t n", t=2),
                             w2[0:2 * P, :].rearrange("(t p) n -> p t n", p=P)).then_inc(e2_in[s], 16)
                sp.dma_start(eraw2[s][0:FH - 2 * P, 2 * D:3 * D], w2[2 * P:FH, :]).then_inc(e2_in[s], 16)

            def routed(s, n):
                sp.wait_ge(f_lo13, n - ERAW + 1)
                sp.wait_ge(f_lo2, n - ERAW + 1)
                expert(s, *(e_of(a[w], n - 1) for w in ("w1r", "w3r", "w2r")))

            for i, (q, k) in enumerate(pieces):
                c = slice(k * D, (k + 1) * D)
                sp.dma_start(raw[:, q, c], stream[q][0][:, c]).then_inc(raw_in[q] if k == KT - 1 else first_in[i], 16)
            sp.dma_start(bkT[:, :], a["bkT"]).then_inc(bk_in, 16)
            sp.dma_start(x[:, :], a["x"]).then_inc(x_in, 16)
            item(2)
            sp.dma_start(wq_raw, a["wq"]).then_inc(wq_in, 16)
            sp.dma_start(bias_b[:, :], rows(a["bv"])).then_inc(bv_in, 16)
            item(3)
            sp.dma_start(bias_a[:, :], rows(a["bq"])).then_inc(bq_in, 16)
            sp.dma_start(wo_raw, a["wo"]).then_inc(wo_in, 16)
            item(4)
            sp.dma_start(mask[0:S, :], a["mask"][0:S, :]).then_inc(mask_in, 16)
            sp.dma_start(mask[S:P, :], a["mask"][0:S, :]).then_inc(mask_in, 16)
            item(5)
            sp.dma_start(hbias[:, :, :], a["hbias"]).then_inc(small_in, 16)
            sp.dma_start(gw[:, :, :], a["gw"]).then_inc(small_in, 16)
            sp.dma_start(gb[:, :], rows(a["gb"])).then_inc(small_in, 16)
            sp.dma_start(rope[:, :, :], a["rope"]).then_inc(small_in, 16)
            for q in range(6, 13):
                item(q)
            sp.wait_ge(pad_ready, 2)
            expert(0, a["w1s"], a["w3s"], a["w2s"])
            for q in range(WQU_Q, WOM_Q + 4):
                item(q)
            expert(1, a["w1r"][0], a["w3r"][0], a["w2r"][0])
            sp.wait_ge(pad_ready, 3)
            expert(2, a["w1r"][1], a["w3r"][1], a["w2r"][1])
            sp.wait_ge(pad_ready, 4)
            expert(3, a["w1r"][2], a["w3r"][2], a["w2r"][2])
            with sp.Fori(0, (NE - ERAW) // 4) as i:
                for j in range(4):
                    routed(j, 4 * i + 4 + j)
            routed(0, NE)
            sp.wait_ge(res_ready, 1)
            sp.dma_start(out, x[:, :]).then_inc(out_done, 16)
            sp.wait_ge(out_done, 16)

        def rotate(nceng, eng, t, b, step, base, done):
            tv = t.rearrange("p (h r) -> p h r", h=H)
            bv = b.rearrange("p (h r) -> p h r", h=H)
            half = DR // 2
            nceng.tensor_tensor(bv[:, :, 0:half], tv[:, :, half:DR],
                                rope[:, 1:2, 0:half].to_broadcast([P, H, half]), ALU.mult).then_inc(step, 1)
            nceng.tensor_tensor(bv[:, :, half:DR], tv[:, :, 0:half],
                                rope[:, 1:2, half:DR].to_broadcast([P, H, half]), ALU.mult).then_inc(step, 1)
            eng.wait_ge(step, base + 2)
            nceng.tensor_tensor(tv, tv, rope[:, 0:1, :].to_broadcast([P, H, DR]), ALU.mult).then_inc(step, 1)
            eng.wait_ge(step, base + 3)
            nceng.tensor_tensor(t, t, b, ALU.add).then_inc(done, 1)

        @block.gpsimd
        def _(gp):
            def inverse_deviation(n):
                gp.wait_ge(stats, n + 1)
                nc.gpsimd.tensor_scalar(small[:, 60:61], mv[:, 1:2], 1e-5, None, ALU.add).then_inc(vareps, 1)
                gp.wait_ge(vareps, n + 1)
                nc.gpsimd.tensor_tensor(small[:, 61:62], small[:, 60:61], power[:, :], ALU.pow).then_inc(rstd, 1)

            nc.gpsimd.memset(power[:, :], -0.5).then_inc(consts, 1)
            nc.gpsimd.memset(identb[:, :], 0.0).then_inc(consts, 1)
            nc.gpsimd.memset(ident[:, :], 0.0).then_inc(consts, 1)
            nc.gpsimd.memset(ones[:, :], 1.0).then_inc(consts, 1)
            gp.wait_ge(consts, 4)
            for m in (identb, ident):
                gp.affine_select(out=m[:, :], in_=m[:, :], compare_op=ALU.not_equal, fill=1.0, base=0,
                                 pattern=[[-1, P]], channel_multiplier=1).then_inc(consts, 1)
            inverse_deviation(0)
            nc.gpsimd.memset(qd[:, :], 0.0).then_inc(consts, 1)
            nc.gpsimd.memset(cmask[:, :], 0.0).then_inc(consts, 1)
            gp.wait_ge(consts, 8)
            gp.affine_select(out=cmask[:, :], in_=cmask[:, :], compare_op=ALU.is_ge, fill=NEG, base=0,
                             pattern=[[-1, P]], channel_multiplier=1).then_inc(consts, 1)
            gp.wait_ge(consts, 9)
            nc.gpsimd.memset(cmask[S:P, 0:S], NEG).then_inc(consts, 1)
            gp.wait_ge(consts, 10)
            gp.wait_ge(q_ready, 1)
            gp.dma_start(bias_a[:, :], rows(a["bo"])).then_inc(bo_in, 16)
            gp.wait_ge(s_red, NPAIR)
            gp.dma_start(mask[0:S, :], a["mask"][S:P, :]).then_inc(mask1_in, 16)
            gp.dma_start(mask[S:P, :], a["mask"][S:P, :]).then_inc(mask1_in, 16)
            gp.wait_ge(v_out, 16)
            gp.dma_start(bias_b[:, :], rows(a["bd"])).then_inc(bd_in, 16)
            gp.wait_ge(x_bias, 1)
            gp.dma_start(bias_a[:, :], rows(a["bom"])).then_inc(bom_in, 16)
            gp.wait_ge(pv_mm, 2 * NPAIR)
            for i in range(2):
                nc.gpsimd.memset(eraw2[i][96:P, 2 * D:3 * D], 0.0).then_inc(pad_ready, 1)
            gp.wait_ge(pad_ready, 2)
            gp.wait_ge(q_mm, 2)
            gp.dma_start(brope[:, 0:1024], rows(a["bkr"])).then_inc(brope_in, 16)
            gp.dma_start(brope[:, 1024:2048], rows(a["bqr"])).then_inc(brope_in, 16)
            inverse_deviation(1)
            gp.wait_ge(krn_r, 2)
            gp.wait_ge(small_in, 64)
            gp.wait_ge(s_mm, 2 * NPAIR)
            rotate(nc.gpsimd, gp, krn, qd[:, 0:1024], ropek_step, 0, kr_roped)
            gp.wait_ge(qrn_r, 2)
            rotate(nc.gpsimd, gp, qrn, qd[:, 1024:2048], ropeq_step, 0, qr_roped)
            gp.wait_ge(qr_roped, 1)
            nc.gpsimd.memset(qd[DR:P, 1024:2048], 0.0).then_inc(qr_zero, 1)
            gp.wait_ge(qr_zero, 1)
            gp.wait_ge(qrT_mm, 2)
            nc.gpsimd.memset(qrn[0:DR, :], 0.0).then_inc(qr_zero2, 1)
            gp.wait_ge(qr_zero2, 1)

            def lo(q, made, count):
                gp.wait_ge(made, count)
                nc.gpsimd.tensor_tensor(where[q][1][:, :], raw[:, q % RAW, :], where[q][0][:, :], ALU.subtract).then_inc(lo_pool, 1)

            lo(LO_POOL[0], hi_done, hi_count(LO_POOL[0]))
            gp.wait_ge(lo_pool, 1)
            gp.wait_ge(ms_mm, 4)
            nc.gpsimd.memset(eraw2[2][96:P, 2 * D:3 * D], 0.0).then_inc(pad_ready, 1)
            gp.wait_ge(pad_ready, 3)
            lo(LO_POOL[1], hi_dve, 1)
            gp.wait_ge(lo_pool, 2)
            lo(LO_POOL[2], hi_done, hi_count(LO_POOL[2]))
            gp.wait_ge(ma_mm, 4)
            gp.wait_ge(lo_pool, 3)
            nc.gpsimd.memset(tri, 1.0).then_inc(tri_ready, 1)
            gp.wait_ge(tri_ready, 1)
            gp.affine_select(out=tri, in_=tri, compare_op=ALU.is_gt, fill=0.0, base=0,
                             pattern=[[1, NE], [-1, NE]], channel_multiplier=0).then_inc(tri_ready, 1)
            gp.wait_ge(*split_at(len(stream) - 1))
            gp.wait_ge(tri_ready, 2)
            nc.gpsimd.memset(eraw2[3][96:P, 2 * D:3 * D], 0.0).then_inc(pad_ready, 1)
            gp.wait_ge(pad_ready, 4)
            inverse_deviation(2)

            def lo2(n, g, s):
                gp.wait_ge(f_hi2, n + 1)
                nc.gpsimd.tensor_tensor(e2[g][1], eraw2[s], e2[g][0], ALU.subtract).then_inc(f_lo2, 1)

            lo2(0, 0, 0)
            gp.wait_ge(f_hi13, 4)
            gp.wait_ge(f_lo13, 1)
            c = slice(KT * FH, W13)
            nc.gpsimd.tensor_tensor(e13[1][1][:, c], eraw13[1][:, c], e13[1][0][:, c], ALU.subtract).then_inc(f_lo13, 1)
            lo2(1, 1, 1)
            lo2(2, 0, 2)
            with gp.Fori(0, (NE - 4) // 4) as i:
                for j in range(4):
                    lo2(4 * i + 3 + j, (3 + j) % 2, (3 + j) % ERAW)
            for n in (NE - 1, NE):
                lo2(n, n % 2, n % ERAW)

        @block.scalar
        def _(act):
            def copy(o, i):
                return nc.scalar.activation(o, i, ACT.Copy)

            def slot_free(q):
                before = [p for p in range(q) if order[p] == order[q]]
                if before:
                    act.wait_ge(*freed[before[-1]])

            def hi(q):
                w = stream[q][1]
                act.wait_ge(raw_in[q % RAW], 16 * (q // RAW + 1))
                slot_free(q)
                copy(where[q][0][:, 0:w], raw[:, q % RAW, 0:w]).then_inc(hi_done, 1)

            def k_evac(n):
                _, c, g = parts[n]
                act.wait_ge(proj_mm, n + 1)
                nc.scalar.activation(kbuf[:, g, (c % 2) * CH:(c % 2 + 1) * CH], proj[n % 2][:, :], ACT.Identity,
                                     bias=bkT[:, g:g + 1]).then_inc(k_out, 1)

            ks = [n for n, p in enumerate(parts) if p[0] == "K"]
            for i, (q, k) in enumerate(pieces):
                c = slice(k * D, (k + 1) * D)
                act.wait_ge(raw_in[q] if k == KT - 1 else first_in[i], 16)
                copy(where[q][0][:, c], raw[:, q, c]).then_inc(hi_done if k == KT - 1 else hi_first, 1)
            act.wait_ge(bk_in, 16)
            k_evac(ks[0])
            k_evac(ks[1])
            hi(2)
            k_evac(ks[2])
            k_evac(ks[3])
            hi(3)

            def wT_evac(dst, n):
                for k2 in range(2):
                    act.wait_ge(wT_mm, 2 * n + k2 + 1)
                    copy(dst[:, 2 * k2:2 * k2 + 2, :].rearrange("p k n -> p (k n)"), tps[k2][:, :].bitcast(BF16)).then_inc(wT_ready, 1)

            hi(4)
            for n in ks[4:8]:
                k_evac(n)
            wT_evac(wqT, 0)
            hi(5)
            wT_evac(woT, 1)

            def exp_pair(w):
                act.wait_ge(nm_ready, w + 1)
                s = sbuf[:, w % 3, :]
                nc.scalar.activation(s, s, ACT.Exp, bias=nmax[:, 16 + w:17 + w], accum_out=rsum[:, w:w + 1]).then_inc(e_done, 1)

            def pt_evac(w):
                act.wait_ge(t_mm, 2 * w + 1)
                if w >= 2:
                    act.wait_ge(pv_mm, w - 1)
                copy(ptbuf[:, w % 2, 0:512], tps[0][:, :]).then_inc(pt_a, 1)

            kq = list(ks[8:])
            for u in range(NPAIR):
                exp_pair(u)
                if u:
                    k_evac(kq.pop(0))
                if u >= 2:
                    pt_evac(u - 2)
            k_evac(kq.pop(0))
            pt_evac(NPAIR - 2)
            pt_evac(NPAIR - 1)
            exp_pair(NPAIR)
            for u in range(1, NPAIR):
                w = NPAIR + u
                exp_pair(w)
                pt_evac(w - 1)
                if u in (1, 3, 5, 6):
                    hi(6 + (1, 3, 5, 6).index(u))
            pt_evac(2 * NPAIR - 1)

            def yT_hi(n):
                act.wait_ge(yT_mm, n)
                copy(yT[0][:, :, :].rearrange("p k t -> p (k t)"), misc[:, :]).then_inc(yTh_r, 1)

            yT_hi(1)
            hi(10)
            act.wait_ge(cT_mm, 1)
            copy(cT[0][:, :, :].rearrange("p k t -> p (k t)"), misc[:, :]).then_inc(cTh_r, 1)
            hi(11)
            hi(12)
            hi(13)

            def up_stage(n):
                act.wait_ge(up_mm, n + 1)
                if n >= 2:
                    act.wait_ge(up_t, n - 1)
                copy(stage[n % 2], up_ps[n % 2]).then_inc(up_nat, 1)

            def value_evac(j):
                act.wait_ge(vu_mm, j + 1)
                copy(vm[:, 4 * j:4 * j + 4, :].rearrange("p h d -> p (h d)"), proj[j % 2][:, :]).then_inc(vu_out, 1)

            for j in range(4):
                up_stage(j)
            value_evac(0)
            value_evac(1)
            hi(14)
            value_evac(2)
            value_evac(3)
            hi(15)
            up_stage(4)
            for j in range(2):
                act.wait_ge(krT_mm, j + 1)
                copy(krT[:, 4 * j:4 * j + 4, :].rearrange("p j t -> p (j t)"), proj[j][:, :]).then_inc(krT_r, 1)
            hi(16)
            up_stage(5)
            act.wait_ge(qrT_mm, 2)
            act.wait_ge(qr_zero, 1)
            for j in range(2):
                for e in range(2):
                    rr = slice(DR * e, DR * (e + 1))
                    copy(qrT[e][rr, 4 * j:4 * j + 4, :].rearrange("p j t -> p (j t)"), proj[j][rr, :]).then_inc(qrT_r, 1)
            up_stage(6)
            hi(17)

            def latent_exp(g):
                act.wait_ge(mneg, g + 1)
                for i in range(HG):
                    t = pg[g][:, P * i:P * (i + 1)]
                    nc.scalar.activation(t, t, ACT.Exp, bias=mst[:, 16 + HG * g + i:17 + HG * g + i], scale=M_SCALE,
                                         accum_out=mst[:, 32 + HG * g + i:33 + HG * g + i]).then_inc(me_done, 1)

            def latent_pT(g):
                act.wait_ge(mt_mm, g + 1)
                if g >= 2:
                    act.wait_ge(ma_mm, g - 1)
                copy(ptg[g % 2], ptp[g % 2]).then_inc(mt_r, 1)

            def attn_hi(g):
                act.wait_ge(ma_mm, g + 1)
                for i in range(HG):
                    h = HG * g + i
                    nc.scalar.activation(attnT[0][:, h, :], proj[g % 2][:, P * i:P * (i + 1)], ACT.Identity,
                                         bias=hbias[:, 2, h:h + 1]).then_inc(ma_hi, 1)

            latent_exp(0)
            up_stage(7)
            hi(18)
            latent_pT(0)
            latent_exp(1)
            attn_hi(0)
            latent_exp(2)
            latent_pT(1)
            latent_exp(3)
            latent_pT(2)
            latent_pT(3)
            hi(20)
            attn_hi(2)

            def hi13(n, g, s, turn, half):
                if half == 0:
                    act.wait_ge(e13_in[s], 32 * (turn + 1))
                    if not isinstance(n, int) or n >= 2:
                        act.wait_ge(f_h2, n - 1)
                c = slice(half * KT * FH, (half + 1) * KT * FH)
                copy(e13[g][0][:, c], eraw13[s][:, c]).then_inc(f_hi13, 1)

            def hi2(n, g, s, turn):
                act.wait_ge(e2_in[s], 32 * (turn + 1))
                if not isinstance(n, int) or n >= 2:
                    act.wait_ge(f_out, n - 1)
                copy(e2[g][0], eraw2[s]).then_inc(f_hi2, 1)

            def silu(m, g):
                act.wait_ge(f_v, m)
                nc.scalar.activation(vv[g], vv[g], ACT.Silu).then_inc(f_silu, 1)

            def t_hi(m):
                act.wait_ge(f_t, m + 1)
                copy(hT[0].rearrange("p k t -> p (k t)"), tps[0][:, 0:FP]).then_inc(f_thi, 1)

            def h1_copy(n, g, func=ACT.Copy):
                act.wait_ge(f_h1, n + 1)
                if not isinstance(n, int) or n >= 2:
                    act.wait_ge(f_h3, n - 1)
                nc.scalar.activation(h1c[g], proj[g][:, 0:FH], func).then_inc(f_h1c, 1)

            def step(n, g, s, turn, turn_next, last=False):
                if not isinstance(n, int) or n >= 2:
                    silu(n - 1, 1 - g)
                if not last:
                    hi13(n + 1, 1 - g, (s + 1) % ERAW, turn_next, 0)
                if last:
                    hi2(n, g, s, turn)
                t_hi(n - 1)
                if not last:
                    hi13(n + 1, 1 - g, (s + 1) % ERAW, turn_next, 1)
                h1_copy(n, g)
                if not last:
                    hi2(n, g, s, turn)

            act.wait_ge(wo_mm, 3)
            hi13(0, 0, 0, 0, 0)
            hi13(0, 0, 0, 0, 1)
            hi2(0, 0, 0, 0)
            act.wait_ge(wo_mm, 4)
            hi13(1, 1, 1, 0, 0)
            yT_hi(2)
            hi13(1, 1, 1, 0, 1)
            act.wait_ge(gate_mm, 1)
            nc.scalar.activation(lg[:, 0, :], misc[:, 0:NE], ACT.Exp, scale=-1.0).then_inc(gate_e, 1)
            h1_copy(0, 0, ACT.Silu)
            step(1, 1, 1, 0, 0)
            step(2, 0, 2, 0, 0)
            with act.Fori(0, (NE - 4) // 4) as i:
                for j in range(4):
                    step(4 * i + 3 + j, (3 + j) % 2, (3 + j) % ERAW, i if j == 0 else i + 1, i + 1)
            step(NE - 1, 1, 3, 3, 4)
            step(NE, 0, 0, 4, 0, last=True)
            silu(NE, 0)
            t_hi(NE)

        @block.vector
        def _(v):
            count = [0]

            def link(ins):
                count[0] += 1
                ins.then_inc(dve, 1)
                v.wait_ge(dve, count[0])

            def lo(q):
                w = stream[q][1]
                dst = where[q]
                v.wait_ge(hi_done, hi_count(q))
                nc.vector.tensor_tensor(dst[1][:, 0:w], raw[:, q % RAW, 0:w], dst[0][:, 0:w], ALU.subtract).then_inc(lo_done, 1)

            def v_evac(n):
                _, c, t = parts[n]
                v.wait_ge(proj_mm, n + 1)
                nc.vector.tensor_tensor(vbuf[c // 2][:, (c % 2) * 4 + t, :], proj[n % 2][:, :], bias_b[:, :],
                                        ALU.add).then_inc(v_out, 1)

            def layer_norm(n):
                link(nc.vector.bn_stats(st[:, 0:6], x[:, :]))
                nc.vector.bn_aggr(mv[:, :], st[:, 0:6]).then_inc(stats, 1)
                normalise(n)

            def normalise(n):
                v.wait_ge(rstd, n + 1)
                nc.vector.tensor_scalar(y[:, :], x[:, :], mv[:, 0:1], small[:, 61:62], ALU.subtract, ALU.mult).then_inc(y_ready, 1)
                v.wait_ge(y_ready, n + 1)

            def scales(src, amax, s, rs):
                if src is not None:
                    link(nc.vector.tensor_reduce(amax, src, AX.X, ALU.max, apply_absolute_value=True))
                link(nc.vector.tensor_scalar(s, amax, 1.0 / QMAX, QEPS, ALU.mult, ALU.max))
                link(nc.vector.reciprocal(rs, s))

            def quantise_rows(src, n):
                scales(src if n == 0 else None, small[:, 32:33], small[:, 33 + n:34 + n], small[:, 35:36])
                link(nc.vector.tensor_scalar(tmp[:, :], src, small[:, 35:36], QMAX, ALU.mult, ALU.min))
                link(nc.vector.tensor_scalar(tmp[:, :], tmp[:, :], -QMAX, ROUND, ALU.max, ALU.add))
                nc.vector.tensor_scalar(xq[:, :], tmp[:, :], ROUND, None, ALU.subtract).then_inc(xq_ready, 1)

            def weight_scales(src, n, loaded):
                v.wait_ge(loaded, 16)
                scales(src, small[:, 16 * n:16 * n + 4], small[:, 16 * n + 4:16 * n + 8], small[:, 16 * n + 8:16 * n + 12])

            def scale_weights(src, n):
                for t in range(4):
                    link(nc.vector.tensor_scalar(src[:, t, :], src[:, t, :], small[:, 16 * n + 8 + t:16 * n + 9 + t],
                                                 QMAX, ALU.mult, ALU.min))

            def round_weights(src, dst, done):
                link(nc.vector.tensor_scalar(src, src, -QMAX, ROUND, ALU.max, ALU.add))
                nc.vector.tensor_scalar(dst, src, ROUND, None, ALU.subtract).then_inc(done, 1)

            def scale_row(n):
                for t in range(4):
                    nc.vector.tensor_scalar(dg[:, t, :], ident[:, :], small[:, 16 * n + 4 + t:16 * n + 5 + t], None,
                                            ALU.mult).then_inc(diag, 1)

            def xqT_copy(n):
                v.wait_ge(xqT_mm, n + 1)
                nc.vector.tensor_copy(xqT[:, :], misc[:, 0:256].bitcast(BF16)).then_inc(xqT_ready, 1)

            def take_row(n):
                v.wait_ge(sw_mm, n + 1)
                nc.vector.tensor_copy(swrow[:, :], misc[:, :]).then_inc(sw_row, 1)

            def dequantise(n):
                v.wait_ge(sw_row, n + 1)
                v.wait_ge(q_mm, n + 1)
                link(nc.vector.scalar_tensor_tensor(tmp[:, :], misc[:, :], small[:, 33 + n:34 + n], swrow[:, :], ALU.mult, ALU.mult))

            for i, (q, k) in enumerate(pieces):
                c = slice(k * D, (k + 1) * D)
                v.wait_ge(*piece_at(i, hi_first, hi_done))
                nc.vector.tensor_tensor(where[q][1][:, c], raw[:, q, c], where[q][0][:, c],
                                        ALU.subtract).then_inc(lo_done if k == KT - 1 else lo_first, 1)
            v.wait_ge(x_in, 16)
            layer_norm(0)
            quantise_rows(y[:, :], 0)
            lo(2)
            weight_scales(wq_raw, 0, wq_in)
            vs = [n for n, p in enumerate(parts) if p[0] == "V"]
            v.wait_ge(bv_in, 16)
            v_evac(vs[0])
            lo(3)
            v_evac(vs[1])
            scale_weights(wq_raw, 0)
            v_evac(vs[2])
            round_weights(wq_raw, wq_int, wq_q)
            v_evac(vs[3])
            lo(4)
            xqT_copy(0)
            v.wait_ge(consts, 6)
            scale_row(0)
            weight_scales(wo_raw, 1, wo_in)
            scale_weights(wo_raw, 1)
            round_weights(wo_raw, wo_int, wo_q)
            take_row(0)
            v_evac(vs[4])
            v_evac(vs[5])
            dequantise(0)
            v.wait_ge(bq_in, 16)
            nc.vector.tensor_tensor(tmp[:, :], tmp[:, :], bias_a[:, :], ALU.add).then_inc(q_ready, 1)
            v_evac(vs[6])
            v_evac(vs[7])
            v.wait_ge(qT_mm, 1)
            v.wait_ge(consts, 7)
            mv4 = misc[:, :].rearrange("p (g b q) -> p g b q", g=4, b=B)
            for r in range(4):
                rr = slice(XD * r, XD * (r + 1))
                for b in range(B):
                    dst = qdv[rr, b, :, :].rearrange("p (g two) q -> p g two q", two=2)[:, :, r // 2, (r % 2) * S:(r % 2 + 1) * S]
                    nc.vector.tensor_scalar(dst, mv4[rr, :, b, :], X_SCALE, None, ALU.mult).then_inc(qd_ready, 1)

            def reduce_pair(w):
                v.wait_ge(s_mm, w + 1)
                v.wait_ge((mask_in, mask1_in)[w // NPAIR], 32)
                if w >= 3:
                    v.wait_ge(t_mm, 2 * (w - 2))
                nc.vector.tensor_tensor_reduce(sbuf[:, w % 3, :], sps[:, :], mask[:, :], 1.0, -3e38, ALU.add, ALU.max,
                                               accum_out=nmax[:, w:w + 1]).then_inc(s_red, 1)
                v.wait_ge(s_red, w + 1)
                nc.vector.tensor_scalar(nmax[:, 16 + w:17 + w], nmax[:, w:w + 1], -1.0, None, ALU.mult).then_inc(nm_ready, 1)

            def pt_evac(w):
                v.wait_ge(t_mm, 2 * w + 2)
                if w >= 2:
                    v.wait_ge(pv_mm, w - 1)
                nc.vector.tensor_copy(ptbuf[:, w % 2, 512:1024], tps[1][:, :]).then_inc(pt_d, 1)

            def attend_out(b, j0, j1):
                c = slice(b * NPAIR + j0, b * NPAIR + j1)
                r = slice(16 + b * NPAIR + j0, 16 + b * NPAIR + j1)
                v.wait_ge(e_done, b * NPAIR + j1)
                link(nc.vector.reciprocal(rsum[:, r], rsum[:, c]))
                v.wait_ge(pv_mm, b * NPAIR + j1)
                pv4 = pvp[:, :].rearrange("p (j two d) -> p j two d", j=NPAIR, two=2)
                o4 = ob[:, :].rearrange("p (j two d) -> p j two d", j=NPAIR, two=2)
                for t in range(2):
                    rr = slice(S * t, S * (t + 1))
                    nc.vector.tensor_tensor(o4[S * b:S * (b + 1), j0:j1, t, :], pv4[rr, j0:j1, t, :],
                                            rsum[rr, r].unsqueeze(2).to_broadcast([S, j1 - j0, XD]),
                                            ALU.mult).then_inc(o_done, 1)

            lo(5)
            vq = list(vs[8:])
            v_evac(vq.pop(0))
            for u in range(NPAIR):
                reduce_pair(u)
                if u >= 2:
                    pt_evac(u - 2)
                if vq:
                    v_evac(vq.pop(0))
            pt_evac(NPAIR - 2)
            reduce_pair(NPAIR)
            pt_evac(NPAIR - 1)
            reduce_pair(NPAIR + 1)
            attend_out(0, 0, NPAIR)
            pt_evac(NPAIR)
            scale_row(1)
            v.wait_ge(bo_in, 16)
            nc.vector.tensor_tensor(x[:, :], x[:, :], bias_a[:, :], ALU.add).then_inc(x_bias, 1)
            for u in range(2, NPAIR):
                reduce_pair(NPAIR + u)
                pt_evac(NPAIR + u - 1)
                if u in (2, 4, 6, 7):
                    lo(6 + (2, 4, 6, 7).index(u))
            attend_out(1, 0, NPAIR - 1)
            pt_evac(2 * NPAIR - 1)
            cut = 2 * XD * (NPAIR - 1)
            v.wait_ge(o_done, 4)
            link(nc.vector.tensor_reduce(small[:, 54:55], ob[:, 0:cut], AX.X, ALU.max, apply_absolute_value=True))
            take_row(1)
            attend_out(1, NPAIR - 1, NPAIR)
            v.wait_ge(o_done, 6)
            link(nc.vector.tensor_reduce(small[:, 55:56], ob[:, cut:D], AX.X, ALU.max, apply_absolute_value=True))
            link(nc.vector.tensor_reduce(small[:, 32:33], small[:, 54:56], AX.X, ALU.max))
            quantise_rows(ob[:, :], 1)
            xqT_copy(1)
            dequantise(1)
            v.wait_ge(x_bias, 1)
            nc.vector.tensor_tensor(x[:, :], x[:, :], tmp[:, :], ALU.add).then_inc(x_second, 1)
            v.wait_ge(x_second, 1)
            layer_norm(1)

            def yT_lo(n):
                v.wait_ge(yTh_r, n)
                nc.vector.tensor_tensor(yT[1][:, :, :].rearrange("p k t -> p (k t)"), misc[:, :],
                                        yT[0][:, :, :].rearrange("p k t -> p (k t)"), ALU.subtract).then_inc(yTl_r, 1)

            yT_lo(1)
            v.wait_ge(down_mm, 1)
            v.wait_ge(bd_in, 16)
            nc.vector.tensor_tensor(tmp[:, :], proj[0][:, :], bias_b[:, :], ALU.add).then_inc(down_r, 1)
            lo(10)
            v.wait_ge(cTh_r, 1)
            nc.vector.tensor_tensor(cT[1][:, :, :].rearrange("p k t -> p (k t)"), misc[:, :],
                                    cT[0][:, :, :].rearrange("p k t -> p (k t)"), ALU.subtract).then_inc(cTl_r, 1)
            v.wait_ge(brope_in, 32)
            for j in range(2):
                v.wait_ge(kr_mm, j + 1)
                nc.vector.tensor_tensor(krn[:, 512 * j:512 * (j + 1)], sps[:, 512 * j:512 * (j + 1)],
                                        brope[:, 512 * j:512 * (j + 1)], ALU.add).then_inc(krn_r, 1)
            lo(11)
            for j in range(2):
                v.wait_ge(qr_mm, j + 1)
                nc.vector.tensor_tensor(qrn[:, 512 * j:512 * (j + 1)], sps[:, 512 * j:512 * (j + 1)],
                                        brope[:, 1024 + 512 * j:1024 + 512 * (j + 1)], ALU.add).then_inc(qrn_r, 1)
                if j == 0:
                    lo(12)

            def up_evac(n, dst, which):
                v.wait_ge(up_t, n + 1)
                j = n % 4
                nc.vector.tensor_tensor(dst[:, 4 * j:4 * j + 4, :], tps[n % 2][:, :].rearrange("p (h t) -> p h t", h=4),
                                        hbias[:, which, 4 * j:4 * j + 4].unsqueeze(2).to_broadcast([P, 4, P]),
                                        ALU.add).then_inc(up_out, 1)

            v.wait_ge(small_in, 64)
            up_evac(0, kT, 0)
            up_evac(1, kT, 0)
            lo(13)
            up_evac(2, kT, 0)
            up_evac(3, kT, 0)
            lo(14)
            lo(15)
            v.wait_ge(bom_in, 16)
            nc.vector.tensor_tensor(x[:, :], x[:, :], bias_a[:, :], ALU.add).then_inc(x_bias, 1)
            up_evac(4, qT, 1)
            lo(16)
            up_evac(5, qT, 1)
            v.wait_ge(consts, 10)

            def latent_mask(g):
                v.wait_ge(ms_mm, g + 1)
                for i in range(HG):
                    c = slice(P * i, P * (i + 1))
                    nc.vector.tensor_tensor_reduce(pg[g][:, c], sgp[g][:, c], cmask[:, :], 1.0, -3e38, ALU.add, ALU.max,
                                                   accum_out=mst[:, HG * g + i:HG * g + i + 1]).then_inc(mmax, 1)
                v.wait_ge(mmax, HG * (g + 1))
                nc.vector.tensor_scalar(mst[:, 16 + HG * g:16 + HG * (g + 1)], mst[:, HG * g:HG * (g + 1)], -M_SCALE, None,
                                        ALU.mult).then_inc(mneg, 1)

            def latent_norm(g):
                v.wait_ge(me_done, HG * (g + 1))
                r = mst[:, 32 + HG * g:32 + HG * (g + 1)]
                link(nc.vector.reciprocal(r, r))
                pgv = pg[g].rearrange("p (h k) -> p h k", h=HG)
                nc.vector.tensor_tensor(pgv, pgv, r.unsqueeze(2).to_broadcast([P, HG, P]), ALU.mult).then_inc(mp_r, 1)

            def attn_hi(g):
                v.wait_ge(ma_mm, g + 1)
                nc.vector.tensor_tensor(attnT[0][:, HG * g:HG * (g + 1), :], proj[g % 2][:, :].rearrange("p (h t) -> p h t", h=HG),
                                        hbias[:, 2, HG * g:HG * (g + 1)].unsqueeze(2).to_broadcast([P, HG, P]),
                                        ALU.add).then_inc(ma_hi_dve, 1)

            def attn_lo(g):
                v.wait_ge(*((ma_hi_dve, g // 2 + 1) if g % 2 else (ma_hi, HG * (g // 2 + 1))))
                for i in range(HG):
                    h = HG * g + i
                    nc.vector.scalar_tensor_tensor(attnT[1][:, h, :], proj[g % 2][:, P * i:P * (i + 1)], hbias[:, 2, h:h + 1],
                                                   attnT[0][:, h, :], ALU.add, ALU.subtract).then_inc(ma_lo, 1)

            def lo13(n, g, s, half):
                v.wait_ge(f_hi13, 2 * n + 1 + half)
                c = slice(half * KT * FH, (half + 1) * KT * FH)
                nc.vector.tensor_tensor(e13[g][1][:, c], eraw13[s][:, c], e13[g][0][:, c], ALU.subtract)\
                    .then_inc(f_lo13h if half == 0 else f_lo13, 1)

            latent_mask(0)
            lo(17)
            latent_norm(0)
            up_evac(6, qT, 1)
            latent_mask(1)
            up_evac(7, qT, 1)
            v.wait_ge(raw_in[HI_DVE % RAW], 16 * (HI_DVE // RAW + 1))
            v.wait_ge(*freed[max(p for p in range(HI_DVE) if order[p] == order[HI_DVE])])
            nc.vector.tensor_copy(where[HI_DVE][0][:, :], raw[:, HI_DVE % RAW, :]).then_inc(hi_dve, 1)
            latent_mask(2)
            latent_norm(1)
            attn_lo(0)
            latent_mask(3)
            latent_norm(2)
            latent_norm(3)
            attn_hi(1)
            attn_lo(1)
            attn_lo(2)
            attn_hi(3)
            attn_lo(3)
            lo13(0, 0, 0, 0)
            v.wait_ge(wo_mm, 4)
            v.wait_ge(x_bias, 2)
            link(nc.vector.tensor_tensor(x[:, :], wop[:, :], x[:, :], ALU.add))
            link(nc.vector.bn_stats(st[:, 0:6], x[:, :]))
            nc.vector.bn_aggr(mv[:, :], st[:, 0:6]).then_inc(stats, 1)

            normalise(2)
            lo13(0, 0, 0, 1)
            yT_lo(2)
            nc.vector.tensor_copy(tmp[:, :], misc[:, :]).then_inc(yT32, 1)
            lo13(1, 1, 1, 0)

            def compare():
                v.wait_ge(gate_e, 1)
                link(nc.vector.tensor_scalar(lg[:, 1, :], lg[:, 0, :], 1.0, None, ALU.add))
                link(nc.vector.reciprocal(lg[:, 2, :], lg[:, 1, :]))
                link(nc.vector.tensor_tensor(lg[:, 3, :], lg[:, 2, :], gb[:, :], ALU.add))
                other = lg[:, 3, :].unsqueeze(1).to_broadcast([P, NE, NE])
                own = lg[:, 3, :].unsqueeze(2).to_broadcast([P, NE, NE])
                link(nc.vector.tensor_tensor(rk[:, 0, :, :], other, own, ALU.is_gt))
                link(nc.vector.tensor_tensor(rk[:, 1, :, :], other, own, ALU.is_equal))
                v.wait_ge(tri_ready, 2)
                link(nc.vector.tensor_tensor(rk[:, 1, :, :], rk[:, 1, :, :], tri, ALU.mult))

            def choose():
                link(nc.vector.tensor_tensor(rk[:, 0, :, :], rk[:, 0, :, :], rk[:, 1, :, :], ALU.add))
                link(nc.vector.tensor_reduce(lg[:, 4, :], rk[:, 0, :, :], AX.X, ALU.add))
                link(nc.vector.tensor_scalar(lg[:, 5, :], lg[:, 4, :], float(TOPK), None, ALU.is_lt))
                link(nc.vector.tensor_tensor(lg[:, 4, :], lg[:, 5, :], lg[:, 3, :], ALU.mult))
                link(nc.vector.tensor_reduce(small[:, 52:53], lg[:, 4, :], AX.X, ALU.add))
                link(nc.vector.reciprocal(small[:, 53:54], small[:, 52:53]))
                link(nc.vector.tensor_scalar(probs[:, :], lg[:, 4, :], small[:, 53:54], None, ALU.mult))

            for g in range(2):
                nc.vector.memset(h3[g][:, FH:FP], 0.0).then_inc(padded, 1)

            def product(m, g, out_t, done):
                v.wait_ge(f_h1c, m + 1)
                v.wait_ge(f_h2, m + 1)
                nc.vector.tensor_tensor(out_t, h1c[g], h2p[g], ALU.mult).then_inc(done, 1)

            def weigh(m, g):
                v.wait_ge(f_silu, m)
                if not isinstance(m, int) or m >= 2:
                    v.wait_ge(f_t, m - 1)
                col = probs[:, m - 1:m] if isinstance(m, int) else probs[:, bass.ds(m - 1, 1)]
                nc.vector.tensor_scalar(h3[g][:, 0:FH], vv[g], col, None, ALU.mult).then_inc(f_h3, 1)

            def t_lo(m):
                v.wait_ge(f_thi, m + 1)
                nc.vector.tensor_tensor(hT[1].rearrange("p k t -> p (k t)"), tps[0][:, 0:FP],
                                        hT[0].rearrange("p k t -> p (k t)"), ALU.subtract).then_inc(f_tlo, 1)

            def step(n, g, s):
                lo13(n + 1, 1 - g, (s + 1) % ERAW, 0)
                t_lo(n - 1)
                product(n, g, vv[g], f_v)
                lo13(n + 1, 1 - g, (s + 1) % ERAW, 1)
                weigh(n, g)

            compare()
            v.wait_ge(padded, 2)
            product(0, 0, h3[0][:, 0:FH], f_h3)
            choose()
            t_lo(0)
            lo13(2, 0, 2, 0)
            product(1, 1, vv[1], f_v)
            v.wait_ge(f_lo13, 2)
            lo13(2, 0, 2, 1)
            weigh(1, 1)
            step(2, 0, 2)
            with v.Fori(0, (NE - 4) // 4) as i:
                for j in range(4):
                    step(4 * i + 3 + j, (3 + j) % 2, (3 + j) % ERAW)
            step(NE - 1, 1, 3)
            t_lo(NE - 1)
            product(NE, 0, vv[0], f_v)
            weigh(NE, 0)
            t_lo(NE)
            v.wait_ge(f_out, NE + 1)
            nc.vector.tensor_tensor(x[:, :], pvp[:, :], x[:, :], ALU.add).then_inc(res_ready, 1)

        @block.tensor
        def _(pe):
            def mm3(o, w, m, start, stop):
                nc.tensor.matmul(o, w[0], m[0], start=start, stop=False)
                nc.tensor.matmul(o, w[1], m[0], start=False, stop=False)
                return nc.tensor.matmul(o, w[0], m[1], start=False, stop=stop)

            def mm3_late_lo(o, ws, ms, turn):
                for k, (w, m) in enumerate(zip(ws, ms)):
                    nc.tensor.matmul(o, w[0], m[0], start=k == 0, stop=False)
                    nc.tensor.matmul(o, w[0], m[1], start=False, stop=False)
                pe.wait_ge(yTl_r, turn)
                for k, (w, m) in enumerate(zip(ws, ms)):
                    last = nc.tensor.matmul(o, w[1], m[0], start=False, stop=k == len(ws) - 1)
                return last

            def split(hl2, f):
                return [f(t) for t in hl2]

            def wait_item(q):
                pe.wait_ge(*split_at(q))

            def ktile(t, k, lo_, hi_, n):
                return t[:, k * n + lo_:k * n + hi_]

            def evacuated(n):
                if n >= 2:
                    m = n - 2
                    if parts[m][0] == "K":
                        pe.wait_ge(k_out, k_before[m])
                    else:
                        pe.wait_ge(v_out, v_before[m])

            def part(n):
                kind, c, j = parts[n]
                slot = where[CTX_Q[c]]
                evacuated(n)
                if n:
                    wait_item(CTX_Q[c])
                if kind == "V":
                    wait_item(WV_Q)
                elif n and c == 0:
                    pe.wait_ge(*piece_at(KT + j, lo_first, lo_done))
                for k in range(KT):
                    if n == 0:
                        pe.wait_ge(*piece_at(1 + k, lo_first, lo_done))
                    if kind == "K":
                        w = split(wk_hl, lambda t: t[:, j * D + k * P:j * D + (k + 1) * P])
                        m = split(slot, lambda t: ktile(t, k, 0, CH, CH))
                    else:
                        w = split(slot, lambda t: ktile(t, k, P * j, P * (j + 1), CH))
                        m = split(wv_hl, lambda t: ktile(t, k, 0, D, D))
                    last = mm3(proj[n % 2][:, :], w, m, k == 0, k == KT - 1)
                last.then_inc(proj_mm, 1)

            def keep_warm(bank, n):
                for _ in range(n):
                    nc.tensor.matmul(bank[:, 0:P], ones[:, :], ones[:, :], start=True, stop=True)

            def x_transposes(n):
                pe.wait_ge(xq_ready, n + 1)
                o = misc[:, 0:256].bitcast(BF16)
                for k in range(KT):
                    last = nc.tensor.transpose(o[:, P * k:P * (k + 1)], xq[:, P * k:P * (k + 1)], identb[:, :])
                last.then_inc(xqT_mm, 1)

            def w_transposes(src, n, ready):
                pe.wait_ge(ready, 1)
                if n:
                    pe.wait_ge(wT_ready, 2 * n)
                for k2 in range(2):
                    o = tps[k2][:, :].bitcast(BF16)
                    for k in range(2):
                        for t in range(4):
                            last = nc.tensor.transpose(o[:, D * k + P * t:D * k + P * (t + 1)],
                                                       src[:, t, P * (2 * k2 + k):P * (2 * k2 + k + 1)], identb[:, :])
                    last.then_inc(wT_mm, 1)

            def row_of_scales(n):
                pe.wait_ge(diag, 4 * (n + 1))
                nc.tensor.matmul(misc[:, :], ones[:, :], dg[:, :, :].rearrange("p t n -> p (t n)"), start=True, stop=True).then_inc(sw_mm, 1)

            def integer_product(w, n):
                pe.wait_ge(sw_row, n + 1)
                pe.wait_ge(xqT_ready, n + 1)
                pe.wait_ge(wT_ready, 2 * (n + 1))
                for k in range(KT):
                    last = nc.tensor.matmul(misc[:, :], xqT[:, P * k:P * (k + 1)], w[:, k, :], start=(k == 0), stop=(k == KT - 1))
                last.then_inc(q_mm, 1)

            pe.wait_ge(consts, 4)
            keep_warm(pvp, 10)
            for n in range(0, 8):
                part(n)
            pe.wait_ge(consts, 6)
            x_transposes(0)
            for n in range(8, 12):
                part(n)
            pe.wait_ge(xqT_ready, 1)
            row_of_scales(0)
            w_transposes(wq_int, 0, wq_q)
            for n in range(12, 14):
                part(n)
            integer_product(wqT, 0)
            for n in range(14, 16):
                part(n)
            pe.wait_ge(q_ready, 1)
            for k in range(4):
                last = nc.tensor.transpose(misc[:, P * k:P * (k + 1)], tmp[:, P * k:P * (k + 1)], ident[:, :])
            last.then_inc(qT_mm, 1)
            w_transposes(wo_int, 1, wo_q)

            def scores(w):
                b, u = w // NPAIR, w % NPAIR
                if w:
                    pe.wait_ge(s_red, w)
                for c in range(2):
                    last = nc.tensor.matmul(sps[:, CH * c:CH * (c + 1)], qdv[:, b, u, :], kbuf[:, u // 2, CH * c:CH * (c + 1)],
                                            start=True, stop=True)
                last.then_inc(s_mm, 1)

            def p_transposes(w):
                pe.wait_ge(e_done, w + 1)
                for c in range(2):
                    if w:
                        pe.wait_ge((pt_a, pt_d)[c], w)
                    for t in range(4):
                        last = nc.tensor.transpose(tps[c][:, P * t:P * (t + 1)],
                                                   sbuf[:, w % 3, CH * c + P * t:CH * c + P * (t + 1)], ident[:, :])
                    last.then_inc(t_mm, 1)

            def values(w):
                b, u = w // NPAIR, w % NPAIR
                if w == NPAIR:
                    pe.wait_ge(o_done, 2)
                pe.wait_ge(pt_a, w + 1)
                for t in range(8):
                    if t == 4:
                        pe.wait_ge(pt_d, w + 1)
                    last = nc.tensor.matmul(pvp[:, 64 * u:64 * (u + 1)], ptbuf[:, w % 2, P * t:P * (t + 1)],
                                            vbuf[b][:, t, 64 * u:64 * (u + 1)], start=(t == 0), stop=(t == 7))
                last.then_inc(pv_mm, 1)

            part(16)
            pe.wait_ge(k_out, 8)
            pe.wait_ge(qd_ready, 8)
            pe.wait_ge(v_out, 8)
            pe.wait_ge(wT_ready, 4)
            nxt = 17
            for u in range(NPAIR):
                scores(u)
                part(nxt)
                nxt += 1
                if u >= 2:
                    p_transposes(u - 2)
                if u:
                    part(nxt)
                    nxt += 1
                if u >= 2:
                    values(u - 2)
            p_transposes(NPAIR - 2)
            pe.wait_ge(k_out, 10)
            scores(NPAIR)
            p_transposes(NPAIR - 1)
            values(NPAIR - 2)
            pe.wait_ge(k_out, 16)
            pe.wait_ge(v_out, 16)
            scores(NPAIR + 1)
            values(NPAIR - 1)
            p_transposes(NPAIR)
            for w in range(NPAIR + 2, 2 * NPAIR):
                scores(w)
                p_transposes(w - 1)
                values(w - 2)
            row_of_scales(1)
            values(2 * NPAIR - 2)
            p_transposes(2 * NPAIR - 1)
            pe.wait_ge(o_done, 4)
            values(2 * NPAIR - 1)
            pe.wait_ge(sw_row, 2)
            keep_warm(proj[1], 12)
            x_transposes(1)
            keep_warm(proj[1], 3)
            integer_product(woT, 1)
            keep_warm(proj[1], 18)

            def y_transposes(n):
                pe.wait_ge(y_ready, n + 1)
                yv = y[:, :].rearrange("t (p k) -> t k p", k=KT)
                for k in range(KT):
                    last = nc.tensor.transpose(misc[:, P * k:P * (k + 1)], yv[:, k, :], ident[:, :])
                last.then_inc(yT_mm, 1)

            y_transposes(1)
            keep_warm(proj[1], 4)
            pe.wait_ge(yTh_r, 1)
            wait_item(WD_Q)
            mm3_late_lo(proj[0][:, :], [split(yT, lambda t: t[:, k, :]) for k in range(KT)],
                        [split(where[WD_Q], lambda t: ktile(t, k, 0, D, D)) for k in range(KT)], 1).then_inc(down_mm, 1)
            for j in range(2):
                q = WKR_Q + j
                wait_item(q)
                for k in range(KT):
                    last = mm3(sps[:, 512 * j:512 * (j + 1)], split(yT, lambda t: t[:, k, :]),
                               split(where[q], lambda t: ktile(t, k, 0, D, D)), k == 0, k == KT - 1)
                last.then_inc(kr_mm, 1)
                if j == 0:
                    pe.wait_ge(down_r, 1)
                    for k in range(4):
                        last = nc.tensor.transpose(misc[:, P * k:P * (k + 1)], tmp[:, P * k:P * (k + 1)], ident[:, :])
                    last.then_inc(cT_mm, 1)
            pe.wait_ge(cTl_r, 1)
            for j in range(2):
                q = WQR_Q + j
                wait_item(q)
                pe.wait_ge(krn_r, j + 1)
                for k in range(QT):
                    last = mm3(sps[:, 512 * j:512 * (j + 1)], split(cT, lambda t: t[:, 1 + k, :]),
                               split(where[q], lambda t: ktile(t, k, 0, 512, 512)), k == 0, k == QT - 1)
                last.then_inc(qr_mm, 1)

            def up_transposes(n):
                pe.wait_ge(up_nat, n + 1)
                if n >= 2:
                    pe.wait_ge(up_out, n - 1)
                for t in range(4):
                    last = nc.tensor.transpose(tps[n % 2][:, P * t:P * (t + 1)], stage[n % 2][:, P * t:P * (t + 1)], ident[:, :])
                last.then_inc(up_t, 1)

            wait_item(WKU_Q)
            for j in range(4):
                if j >= 2:
                    pe.wait_ge(up_nat, j - 1)
                last = mm3(up_ps[j % 2], split(cT, lambda t: t[:, 0, :]),
                           split(where[WKU_Q], lambda t: t[:, 512 * j:512 * (j + 1)]), True, True)
                last.then_inc(up_mm, 1)
                if j:
                    up_transposes(j - 1)
            wait_item(WVU_Q)
            for j in range(4):
                if j >= 2:
                    pe.wait_ge(vu_out, j - 1)
                last = mm3(proj[j % 2][:, :], split(cT, lambda t: t[:, 0, :]),
                           split(where[WVU_Q], lambda t: t[:, 512 * j:512 * (j + 1)]), True, True)
                last.then_inc(vu_mm, 1)
                if j == 0:
                    up_transposes(3)
            def query_up(j):
                q = WQU_Q + j
                wait_item(q)
                pe.wait_ge(up_nat, j + 3)
                for k in range(QT):
                    last = mm3(up_ps[j % 2], split(cT, lambda t: t[:, 1 + k, :]),
                               split(where[q], lambda t: ktile(t, k, 0, 512, 512)), k == 0, k == QT - 1)
                last.then_inc(up_mm, 1)

            def rope_transposes(t4, done):
                for i in range(2):
                    for t in range(4):
                        last = nc.tensor.transpose(proj[i][:, P * t:P * (t + 1)], t4[:, 512 * i + P * t:512 * i + P * (t + 1)], ident[:, :])
                    last.then_inc(done, 1)

            query_up(0)
            pe.wait_ge(kr_roped, 1)
            pe.wait_ge(vu_out, 4)
            rope_transposes(krn, krT_mm)
            query_up(1)
            up_transposes(4)
            pe.wait_ge(qr_roped, 1)
            pe.wait_ge(krT_r, 2)
            rope_transposes(qrn, qrT_mm)
            query_up(2)
            up_transposes(5)

            def latent_scores(g):
                pe.wait_ge(up_out, 5 + g)
                for i in range(HG):
                    h = HG * g + i
                    o = sgp[g][:, P * i:P * (i + 1)]
                    nc.tensor.matmul(o, qT[:, h, :], kT[:, h, :], start=True, stop=False)
                    last = nc.tensor.matmul(o, qrT[h % 2][:, h // 2, :], krT[:, h // 2, :], start=False, stop=True)
                last.then_inc(ms_mm, 1)

            def latent_transposes(g):
                pe.wait_ge(mp_r, g + 1)
                if g >= 2:
                    pe.wait_ge(mt_r, g - 1)
                for i in range(HG):
                    last = nc.tensor.transpose(ptp[g % 2][:, P * i:P * (i + 1)], pg[g][:, P * i:P * (i + 1)], ident[:, :])
                last.then_inc(mt_mm, 1)

            def latent_values(g):
                pe.wait_ge(mt_r, g + 1)
                if g >= 2:
                    pe.wait_ge(ma_lo, HG * (g - 1))
                for i in range(HG):
                    last = nc.tensor.matmul(proj[g % 2][:, P * i:P * (i + 1)], vm[:, HG * g + i, :], ptg[g % 2][:, P * i:P * (i + 1)],
                                            start=True, stop=True)
                last.then_inc(ma_mm, 1)

            def latent_out(g):
                q = WOM_Q + g
                wait_item(q)
                pe.wait_ge(ma_lo, HG * (g + 1))
                for i in range(HG):
                    h = HG * g + i
                    last = mm3(wop[:, :], split(attnT, lambda t: t[:, h, :]), split(where[q], lambda t: ktile(t, i, 0, D, D)),
                               h == 0, h == H - 1)
                last.then_inc(wo_mm, 1)

            pe.wait_ge(qrT_r, 4)
            pe.wait_ge(qr_zero2, 1)
            pe.wait_ge(qrn_r, 2)
            latent_scores(0)
            query_up(3)
            up_transposes(6)
            latent_scores(1)
            up_transposes(7)
            latent_transposes(0)
            latent_scores(2)
            latent_values(0)
            latent_scores(3)
            latent_transposes(1)
            pe.wait_ge(mmax, HG * 3)
            latent_out(0)
            latent_values(1)
            latent_transposes(2)
            latent_transposes(3)
            latent_values(2)
            latent_out(1)
            latent_values(3)
            latent_out(2)
            latent_out(3)

            keep_warm(pvp, 14)
            y_transposes(2)
            keep_warm(pvp, 4)

            def up(n, g, half):
                if half == 0:
                    pe.wait_ge(f_lo13h, n + 1)
                else:
                    pe.wait_ge(f_lo13, n + 1)
                if not isinstance(n, int) or n >= 2:
                    pe.wait_ge(f_h1c if half == 0 else f_h3, n - 1)
                o = proj[g][:, 0:FH] if half == 0 else h2p[g]
                base = half * KT * FH
                for k in range(KT):
                    last = mm3(o, split(yT, lambda t: t[:, k, :]),
                               split(e13[g], lambda t: t[:, base + k * FH:base + (k + 1) * FH]), k == 0, k == KT - 1)
                last.then_inc(f_h1 if half == 0 else f_h2, 1)

            def h_transposes(m, g):
                pe.wait_ge(f_h3, m + 1)
                if not isinstance(m, int) or m >= 1:
                    pe.wait_ge(f_tlo, m)
                for t in range(FT):
                    last = nc.tensor.transpose(tps[0][:, P * t:P * (t + 1)], h3[g][:, P * t:P * (t + 1)], ident[:, :])
                last.then_inc(f_t, 1)

            def down(m, g, start=False, stop=False):
                pe.wait_ge(f_thi, m + 1)
                pe.wait_ge(f_lo2, m + 1)
                for i in range(2):
                    for t in range(FT):
                        nc.tensor.matmul(pvp[:, :], hT[0][:, t, :], e2[g][i][:, D * t:D * (t + 1)],
                                         start=start and i == 0 and t == 0, stop=False)
                pe.wait_ge(f_tlo, m + 1)
                for t in range(FT):
                    last = nc.tensor.matmul(pvp[:, :], hT[1][:, t, :], e2[g][0][:, D * t:D * (t + 1)],
                                            start=False, stop=stop and t == FT - 1)
                last.then_inc(f_out, 1)

            def step(n, g, start=False):
                up(n, g, 0)
                h_transposes(n - 1, 1 - g)
                up(n, g, 1)
                down(n - 1, 1 - g, start=start)

            pe.wait_ge(yTh_r, 2)
            pe.wait_ge(f_lo13h, 1)
            mm3_late_lo(proj[0][:, 0:FH], [split(yT, lambda t: t[:, k, :]) for k in range(KT)],
                        [split(e13[0], lambda t: t[:, k * FH:(k + 1) * FH]) for k in range(KT)], 2).then_inc(f_h1, 1)
            pe.wait_ge(yT32, 1)
            for k in range(KT):
                last = nc.tensor.matmul(misc[:, 0:NE], tmp[:, P * k:P * (k + 1)], gw[:, k, :], start=(k == 0), stop=(k == KT - 1))
            last.then_inc(gate_mm, 1)
            up(0, 0, 1)
            step(1, 1, start=True)
            step(2, 0)
            with pe.Fori(0, (NE - 4) // 4) as i:
                for j in range(4):
                    step(4 * i + 3 + j, (3 + j) % 2)
            step(NE - 1, 1)
            step(NE, 0)
            h_transposes(NE, 0)
            down(NE, 0, stop=True)


def perceiver_block(nc, inputs, out):
    build(nc, inputs, out)


def kernel(**inputs):
    import numpy as _np
    import concourse.bacc as _bacc
    from concourse import mybir as _mybir
    from concourse.bass_utils import run_bass_kernel_spmd as _run

    g = {k: _np.asarray(v) for k, v in inputs.items()}
    f = _np.ascontiguousarray

    def tiles(w, k, j):
        n = w.shape[1] // j
        return f(w.reshape(k, 128, j, n).transpose(2, 1, 0, 3)).reshape(j, 128, k * n)

    def halves(w):
        return f(w.reshape(128, 4, 2, 512).transpose(2, 0, 1, 3)).reshape(2, 128, 2048)

    freq = (1.0 / 10000.0 ** (_np.arange(0, 64, 2, dtype=_np.float32) / _np.float32(64))).astype(_np.float32)
    ang = (_np.arange(128) % 64).astype(_np.float32)[:, None] * freq
    cos, sin = _np.cos(ang), _np.sin(ang)
    tables = f(_np.stack([_np.concatenate([cos, cos], 1), _np.concatenate([-sin, sin], 1)], 1).astype(_np.float32))

    arrays = {
        "x": f(g["x"].reshape(128, 512)),
        "mask": f(g["mask_BxSxS2_ff0"].reshape(128, 1024)),
        "ctx": f(g["ctx_2048"].reshape(4, 512, 512).transpose(0, 2, 1)).reshape(4, 128, 2048),
        "wk": f(g["L0_xattn_wk"].T.reshape(128, 4, 4, 128).transpose(0, 2, 1, 3)).reshape(128, 2048),
        "wv": f(g["L0_xattn_wv"].T).reshape(128, 2048),
        "wq": f(g["L0_xattn_wq"].reshape(4, 128, 512).transpose(1, 0, 2)),
        "wo": f(g["L0_xattn_wo"].reshape(4, 128, 512).transpose(1, 0, 2)),
        "bq": g["L0_xattn_bq"], "bv": g["L0_xattn_bv"], "bo": g["L0_xattn_bo"],
        "bkT": f(g["L0_xattn_bk"].reshape(4, 128).T),
        "wd": f(_np.concatenate([g["L0_attn_Wkd"], g["L0_attn_Wqd"]], 0).T).reshape(128, 2048),
        "bd": f(_np.concatenate([g["L0_attn_bkd"], g["L0_attn_bqd"]], 0)),
        "wkr": halves(g["L0_attn_Wkr"].T),
        "wku": f(g["L0_attn_Wku"].T), "wvu": f(g["L0_attn_Wvu"].T),
        "wqr": tiles(g["L0_attn_Wqr"].T, 3, 2),
        "wqu": tiles(g["L0_attn_Wqu"].T, 3, 4),
        "wom": f(g["L0_attn_Wo"].T.reshape(4, 4, 128, 512).transpose(0, 2, 1, 3)).reshape(4, 128, 2048),
        "bkr": g["L0_attn_bkr"], "bqr": g["L0_attn_bqr"], "bom": g["L0_attn_bo"],
        "hbias": f(_np.stack([g["L0_attn_" + n].reshape(16, 128).T for n in ("bku", "bqu", "bvu")], 1)),
        "rope": tables,
        "gw": f(g["L0_ffn_gate_w"].T).reshape(128, 4, 16),
        "gb": g["L0_ffn_gate_b"],
        "w1s": g["L0_ffn_w1_shared"], "w2s": g["L0_ffn_w2_shared"], "w3s": g["L0_ffn_w3_shared"],
        "w1r": g["L0_ffn_w1_routed"], "w2r": g["L0_ffn_w2_routed"], "w3r": g["L0_ffn_w3_routed"],
    }
    nc = _bacc.Bacc("TRN2", target_bir_lowering=False, num_devices=1)
    feeds, aps = {}, {}
    for name, v in arrays.items():
        v = f(v)
        feeds[f"in_{name}"] = v
        aps[name] = nc.dram_tensor(f"in_{name}", v.shape, _mybir.dt.from_np(v.dtype), kind="ExternalInput").ap()
    out = nc.dram_tensor("out", (128, 512), _mybir.dt.float32, kind="ExternalOutput").ap()
    perceiver_block(nc, aps, out)
    r = _run(nc, [feeds], core_ids=[0])
    return r.results[0]["out"].reshape(2, 64, 512)
```
